# Optimizing a Trainium2 kernel written in Bass

```python
import numpy as np
import jax
import jax.numpy as jnp

def _softmax(x, axis=-1):
    return jax.nn.softmax(x, axis=axis)

def _gelu(x):
    return jax.nn.gelu(x, approximate=True)

def _silu(x):
    return jax.nn.silu(x)

def _sigmoid(x):
    return jax.nn.sigmoid(x)

def _layernorm(x, axis=-1, eps=1e-05):
    m = jnp.mean(x, axis=axis, keepdims=True)
    v = jnp.var(x, axis=axis, keepdims=True)
    return (x - m) / jnp.sqrt(v + eps)

def _scatter_add(tgt, idx, src, axis=0):
    return tgt.at[idx].add(src)

def _segment_sum(src, seg, n):
    return jax.ops.segment_sum(src, seg, n)
kernel_name = 'mk_gnn_ffn_d1_gnn_r8_0f7210'

def setup_inputs(seed: int=0):
    np.random.seed(seed)
    _w = jnp.asarray

    def _rec_inputs():
        import jax
        import jax.numpy as jnp
        _gk = jax.random.key(seed)
        x = -0.0002117 + 1 * jax.random.normal(jax.random.fold_in(_gk, 1), (6250, 256), jnp.float32)
        _s = jax.random.randint(jax.random.fold_in(_gk, 2), (50000,), 0, 6250, jnp.int32)
        _d = jax.random.randint(jax.random.fold_in(_gk, 3), (50000,), 0, 6250, jnp.int32)
        _loop = jnp.arange(6250, dtype=jnp.int32)
        src = jnp.concatenate([_s, _d, _loop])
        dst = jnp.concatenate([_d, _s, _loop])
        _o = jnp.argsort(dst, stable=True)
        src = src[_o]
        dst = dst[_o]
        edge_weight = jax.random.uniform(jax.random.fold_in(_gk, 12), (106250,), jnp.float32, 0.0, 1)
        return (x, src, dst, edge_weight)
    x, src, dst, edge_weight = _rec_inputs()

    def _L0_gnn_setup():
        import jax, jax.numpy as jnp
        import numpy as np
        MU = 2.0
        key = jax.random.key(seed)
        ks = jax.random.split(key, 8)
        N, E, IN, P, OUT = (12500, 200000, 256, 128, 256)
        x = jax.random.normal(ks[0], (N, IN), dtype=jnp.float32)
        edge_vals = jnp.ones((E,), dtype=jnp.float32)
        Wp = jax.random.normal(ks[1], (P, IN), dtype=jnp.float32) * (1.0 / np.sqrt(IN))
        bp = jnp.zeros((P,), dtype=jnp.float32)
        W1 = jax.random.normal(ks[2], (OUT, P), dtype=jnp.float32) * (1.0 / np.sqrt(P))
        b1 = jnp.zeros((OUT,), dtype=jnp.float32)
        W2 = jax.random.normal(ks[3], (OUT, P), dtype=jnp.float32) * (1.0 / np.sqrt(P))
        b2 = jnp.zeros((OUT,), dtype=jnp.float32)
        src = jax.random.randint(ks[4], (E,), 0, N, dtype=jnp.int32)
        dst = jax.random.randint(ks[5], (E,), 0, N, dtype=jnp.int32)
        return {'x': x, 'edge_vals': edge_vals, 'Wp': Wp, 'bp': bp, 'W1': W1, 'b1': b1, 'W2': W2, 'b2': b2, 'src': src, 'dst': dst}
    _L0_gnn_all = _L0_gnn_setup()
    _L0_gnn_in = {k: v for k, v in _L0_gnn_all.items() if k in ('Wp', 'bp', 'W1', 'b1', 'W2', 'b2')}
    del _L0_gnn_all

    def _L0_ffn_setup():
        import jax, jax.numpy as jnp
        import numpy as np
        B, N, D = (16, 512, 256)
        NUM_EXPERTS, TOP_K, HEADS = (4, 2, 4)
        N_EDGES = 131072
        LN_EPS = 1e-05

        def _layernorm(x, g, b):
            mu = x.mean(-1, keepdims=True)
            var = ((x - mu) ** 2).mean(-1, keepdims=True)
            return (x - mu) * jax.lax.rsqrt(var + LN_EPS) * g + b

        def _forward(x, edge_index, W_gat, att_src, att_dst, b_gat, ln_gamma, ln_beta, W1, b1, W2, b2):
            Bc, Nc, Dc = x.shape
            M = Bc * Nc
            x_flat = x.reshape(M, Dc)
            h = (x_flat @ W_gat).reshape(M, HEADS, NUM_EXPERTS)
            loops = jnp.arange(M, dtype=edge_index.dtype)
            src = jnp.concatenate([edge_index[0], loops])
            dst = jnp.concatenate([edge_index[1], loops])
            a_src = (h * att_src).sum(-1)
            a_dst = (h * att_dst).sum(-1)
            e = jax.nn.leaky_relu(a_src[src] + a_dst[dst], negative_slope=0.2)
            e_max = jax.ops.segment_max(e, dst, num_segments=M)
            ee = jnp.exp(e - e_max[dst])
            denom = jax.ops.segment_sum(ee, dst, num_segments=M)
            alpha = ee / (denom[dst] + 1e-16)
            msg = h[src] * alpha[:, :, None]
            agg = jax.ops.segment_sum(msg, dst, num_segments=M).reshape(M, HEADS * NUM_EXPERTS) + b_gat
            scores = _layernorm(agg, ln_gamma, ln_beta).reshape(M, HEADS, NUM_EXPERTS).mean(1)
            scores = scores.reshape(Bc, Nc, NUM_EXPERTS)
            topk_s, topk_i = jax.lax.top_k(scores, TOP_K)
            w = jax.nn.softmax(topk_s, axis=-1)
            out = jnp.zeros_like(x)
            for ei in range(NUM_EXPERTS):
                g = jnp.where(topk_i == ei, w, 0.0).sum(-1)
                hh = jax.nn.gelu(x @ W1[ei] + b1[ei], approximate=False)
                out = out + g[..., None] * (hh @ W2[ei] + b2[ei])
            return out
        key = jax.random.key(seed)
        ks = jax.random.split(key, 8)
        s = 0.05
        return {'x': jax.random.normal(ks[0], (B, N, D), jnp.float32), 'W_gat': jax.random.normal(ks[1], (D, HEADS * NUM_EXPERTS), jnp.float32) * s, 'att_src': jax.random.normal(ks[2], (HEADS, NUM_EXPERTS), jnp.float32) * s, 'att_dst': jax.random.normal(ks[3], (HEADS, NUM_EXPERTS), jnp.float32) * s, 'b_gat': jnp.zeros((HEADS * NUM_EXPERTS,), jnp.float32), 'ln_gamma': jnp.ones((HEADS * NUM_EXPERTS,), jnp.float32), 'ln_beta': jnp.zeros((HEADS * NUM_EXPERTS,), jnp.float32), 'W1': jax.random.normal(ks[4], (NUM_EXPERTS, D, 2 * D), jnp.float32) * s, 'b1': jnp.zeros((NUM_EXPERTS, 2 * D), jnp.float32), 'W2': jax.random.normal(ks[5], (NUM_EXPERTS, 2 * D, D), jnp.float32) * s, 'b2': jnp.zeros((NUM_EXPERTS, D), jnp.float32), 'edge_index': jax.random.randint(ks[6], (2, N_EDGES), 0, B * N, jnp.int32)}
    _L0_ffn_all = _L0_ffn_setup()
    _L0_ffn_in = {k: v for k, v in _L0_ffn_all.items() if k in ('W_gat', 'att_src', 'att_dst', 'b_gat', 'ln_gamma', 'ln_beta', 'W1', 'b1', 'W2', 'b2', 'edge_index')}
    del _L0_ffn_all
    return {'x': x, 'src': src, 'dst': dst, 'edge_weight': edge_weight, 'L0_gnn_Wp': _L0_gnn_in['Wp'], 'L0_gnn_bp': _L0_gnn_in['bp'], 'L0_gnn_W1': _L0_gnn_in['W1'], 'L0_gnn_b1': _L0_gnn_in['b1'], 'L0_gnn_W2': _L0_gnn_in['W2'], 'L0_gnn_b2': _L0_gnn_in['b2'], 'L0_ffn_W_gat': _L0_ffn_in['W_gat'], 'L0_ffn_att_src': _L0_ffn_in['att_src'], 'L0_ffn_att_dst': _L0_ffn_in['att_dst'], 'L0_ffn_b_gat': _L0_ffn_in['b_gat'], 'L0_ffn_ln_gamma': _L0_ffn_in['ln_gamma'], 'L0_ffn_ln_beta': _L0_ffn_in['ln_beta'], 'L0_ffn_W1': _L0_ffn_in['W1'], 'L0_ffn_b1': _L0_ffn_in['b1'], 'L0_ffn_W2': _L0_ffn_in['W2'], 'L0_ffn_b2': _L0_ffn_in['b2'], 'L0_ffn_edge_index': _L0_ffn_in['edge_index']}

def reference(x, src, dst, edge_weight, L0_gnn_Wp, L0_gnn_bp, L0_gnn_W1, L0_gnn_b1, L0_gnn_W2, L0_gnn_b2, L0_ffn_W_gat, L0_ffn_att_src, L0_ffn_att_dst, L0_ffn_b_gat, L0_ffn_ln_gamma, L0_ffn_ln_beta, L0_ffn_W1, L0_ffn_b1, L0_ffn_W2, L0_ffn_b2, L0_ffn_edge_index):
    import jax
    import jax.numpy as jnp

    def _L0_gnn_ref(x, edge_vals, Wp, bp, W1, b1, W2, b2, src, dst):
        import jax, jax.numpy as jnp
        import numpy as np
        MU = 2.0
        N = x.shape[0]
        h = jax.nn.relu(x @ Wp.T + bp)
        hp = h ** MU
        msgs = edge_vals[:, None] * hp[src]
        agg = jax.ops.segment_sum(msgs, dst, num_segments=N)
        agg = agg ** (1.0 / MU)
        return h @ W1.T + b1 + agg @ W2.T + b2

    def _L0_ffn_ref(x, W_gat, att_src, att_dst, b_gat, ln_gamma, ln_beta, W1, b1, W2, b2, edge_index):
        import jax, jax.numpy as jnp
        import numpy as np
        B, N, D = (16, 512, 256)
        NUM_EXPERTS, TOP_K, HEADS = (4, 2, 4)
        N_EDGES = 131072
        LN_EPS = 1e-05

        def _layernorm(x, g, b):
            mu = x.mean(-1, keepdims=True)
            var = ((x - mu) ** 2).mean(-1, keepdims=True)
            return (x - mu) * jax.lax.rsqrt(var + LN_EPS) * g + b

        def _forward(x, edge_index, W_gat, att_src, att_dst, b_gat, ln_gamma, ln_beta, W1, b1, W2, b2):
            Bc, Nc, Dc = x.shape
            M = Bc * Nc
            x_flat = x.reshape(M, Dc)
            h = (x_flat @ W_gat).reshape(M, HEADS, NUM_EXPERTS)
            loops = jnp.arange(M, dtype=edge_index.dtype)
            src = jnp.concatenate([edge_index[0], loops])
            dst = jnp.concatenate([edge_index[1], loops])
            a_src = (h * att_src).sum(-1)
            a_dst = (h * att_dst).sum(-1)
            e = jax.nn.leaky_relu(a_src[src] + a_dst[dst], negative_slope=0.2)
            e_max = jax.ops.segment_max(e, dst, num_segments=M)
            ee = jnp.exp(e - e_max[dst])
            denom = jax.ops.segment_sum(ee, dst, num_segments=M)
            alpha = ee / (denom[dst] + 1e-16)
            msg = h[src] * alpha[:, :, None]
            agg = jax.ops.segment_sum(msg, dst, num_segments=M).reshape(M, HEADS * NUM_EXPERTS) + b_gat
            scores = _layernorm(agg, ln_gamma, ln_beta).reshape(M, HEADS, NUM_EXPERTS).mean(1)
            scores = scores.reshape(Bc, Nc, NUM_EXPERTS)
            topk_s, topk_i = jax.lax.top_k(scores, TOP_K)
            w = jax.nn.softmax(topk_s, axis=-1)
            out = jnp.zeros_like(x)
            for ei in range(NUM_EXPERTS):
                g = jnp.where(topk_i == ei, w, 0.0).sum(-1)
                hh = jax.nn.gelu(x @ W1[ei] + b1[ei], approximate=False)
                out = out + g[..., None] * (hh @ W2[ei] + b2[ei])
            return out
        return _forward(x, edge_index, W_gat, att_src, att_dst, b_gat, ln_gamma, ln_beta, W1, b1, W2, b2)
    x = x + _L0_gnn_ref(_layernorm(x, axis=-1), edge_weight, L0_gnn_Wp, L0_gnn_bp, L0_gnn_W1, L0_gnn_b1, L0_gnn_W2, L0_gnn_b2, src, dst)
    x = x + _L0_ffn_ref(_layernorm(x, axis=-1)[None], L0_ffn_W_gat, L0_ffn_att_src, L0_ffn_att_dst, L0_ffn_b_gat, L0_ffn_ln_gamma, L0_ffn_ln_beta, L0_ffn_W1, L0_ffn_b1, L0_ffn_W2, L0_ffn_b2, L0_ffn_edge_index)[0]
    return x

_drawn_inputs = setup_inputs


def setup_inputs(seed=0):
    import zlib

    import numpy as np

    out = dict(_drawn_inputs(seed))
    spreads = {'L0_gnn_bp': (0.0, 0.1),
     'L0_gnn_b1': (0.0, 0.1),
     'L0_gnn_b2': (0.0, 0.1),
     'L0_ffn_b_gat': (0.0, 0.8),
     'L0_ffn_ln_gamma': (1.0, 0.6),
     'L0_ffn_ln_beta': (0.0, 0.8),
     'L0_ffn_b1': (0.0, 0.351),
     'L0_ffn_b2': (0.0, 0.283)}
    factors = {'L0_ffn_att_src': 64.0, 'L0_ffn_att_dst': 64.0}
    for name, (base, spread) in spreads.items():
        noise = np.random.default_rng([zlib.crc32(name.encode()), seed]).standard_normal(out[name].shape)
        drawn = base * np.exp(spread * noise) if base else spread * noise
        out[name] = jnp.asarray(drawn.astype(out[name].dtype))
    for name, factor in factors.items():
        out[name] = (out[name] * factor).astype(out[name].dtype)
    return out
```

```python
from contextlib import ExitStack

import concourse.bass as bass
from concourse import mybir

F32 = mybir.dt.float32
I32 = mybir.dt.int32
BF16 = mybir.dt.bfloat16
ALU = mybir.AluOpType
ACT = mybir.ActivationFunctionType
AX = mybir.AxisListType

P = 128
N = 6250
NT = 49
NP = NT * P
D = 256
KD = D // P
GT = 7
NG = NT // GT
GN = GT * P
HN = GN // 2
EG = 106250
ET = 8
EGN = ET * P
GG = 104
EF = 131072
FC = EF // P
FLOG = 10
ELOG = 17
DST_BITS = 13
CH = 32
NCH = FC // CH
HEADS = 4
NE = 4
HK = HEADS * NE
RW = 24
HID = 512
FB = HID // P
MB = 448
NMB = NP // MB
MQ = 112
QB = MB // MQ
CR = 40
TRASH = 8192
LN_EPS = 1e-5
BIG = 1e30
KEY_TOP = 0x40000000

STAGES = [(k, j) for k in range(1, ELOG + 1) for j in range(k - 1, -1, -1)]
BUDGET = 7.0
HIST_CH = 16


def gnn_ffn(nc, x, gsrc, gdst, gw, WpT, bp, W1T, b1, W2T, b2, Wgat, att_src, att_dst, b_gat,
            ln_gamma, ln_beta, mW1, mb1, mW2, mb2, fsrc, fdst, out, debug):
    ctx = ExitStack()
    with ctx:
        def sb(name, shape, dt=F32):
            return ctx.enter_context(nc.sbuf_tensor(name, shape, dt))

        def sem(name):
            return ctx.enter_context(nc.semaphore(name))

        def dram(name, shape, dt=F32):
            kind = "ExternalOutput" if debug and name in debug else "Internal"
            return nc.dram_tensor(name, shape, dt, kind=kind).ap()

        hp_tab = dram("hp_tab", (NP, P))
        x2_tab = dram("x2_tab", (NP, D))
        src_tab = dram("src_tab", (NP, RW))
        adst_tab = dram("adst_tab", (TRASH, HEADS))
        adst_edge = dram("adst_edge", (EF + NP, HEADS))
        rec_tab = dram("rec_tab", (EF, RW))
        carry_tab = dram("carry_tab", (TRASH + P, CR))
        y_tab = dram("y_tab", (NP, NE * D))


        big_x = sb("big_x", [P, NT * D])
        big_t = sb("big_t", [P, KD * NP])
        big_h = sb("big_h", [P, 2 * NP + P])
        ring = sb("ring", [P, 4 * EGN])

        def carve(whole, at, n):
            return whole[:, at:at + n]

        x_all = big_x[:, :].rearrange("p (t d) -> p t d", d=D)
        hT = big_h[:, 0:NP]
        aggT = big_h[:, NP:2 * NP + P]
        xn2T = big_t[:, :].rearrange("p (k n) -> p k n", k=KD)
        xn = ring[:, 0:GT * D].rearrange("p (t d) -> p t d", d=D)
        xnT = ring[:, GT * D:2 * GT * D].rearrange("p (k n) -> p k n", k=KD)
        g_ring = ring[:, 0:2 * EGN].rearrange("p (h j f) -> p h j f", h=2, j=ET)
        oh_ring = ring[:, 2 * EGN:4 * EGN].rearrange("p (h j f) -> p h j f", h=2, j=ET)
        keys = [carve(big_t, i * FC, FC) for i in range(2)]
        e_src = carve(big_t, 2 * FC, FC).bitcast(I32)
        e_dst = carve(big_t, 3 * FC, FC).bitcast(I32)
        g_src = carve(big_t, 4 * FC, EGN).bitcast(I32)
        g_dst = carve(big_t, 5 * FC, EGN).bitcast(I32)
        g_w = carve(big_t, 6 * FC, EGN)
        g_srcf = carve(big_t, 7 * FC, EGN)
        g_dstf = carve(big_t, 8 * FC, EGN)
        half_i = carve(big_t, 10 * FC, FC).bitcast(I32)
        lo_bf = carve(big_t, 11 * FC, FC // 2).bitcast(BF16)
        hi_bf = carve(big_t, 11 * FC + FC // 2, FC // 2).bitcast(BF16)
        oh_lo = carve(big_t, 4 * FC, HIST_CH * P).bitcast(BF16).rearrange("p (s t c) -> p s t c", s=2, c=P)
        oh_hi = carve(big_t, 8 * FC, HIST_CH * 64).bitcast(BF16).rearrange("p (s t c) -> p s t c", s=2, c=64)
        b12 = carve(big_t, 6 * FC, 2 * D).rearrange("p (s d) -> p s d", s=2)
        s_dst = carve(big_t, 4 * FC, FC)
        was_equal = carve(big_t, 5 * FC, FC)
        w1m = carve(big_x, 0, 4096).rearrange("p (e k f) -> p e k f", e=NE, k=KD)
        w2m = carve(big_x, 4096, 4096).rearrange("p (e f d) -> p e f d", e=NE, f=FB)
        hid = carve(big_x, 8192, 2 * FB * MB).rearrange("p (s f n) -> p s f n", s=2, f=FB)
        a_edge = carve(big_h, 0, HEADS * FC).rearrange("p (t h) -> p t h", h=HEADS)
        at = HEADS * FC
        rec_in = carve(big_h, at, 2 * CH * RW).rearrange("p (s t c) -> p s t c", s=2, c=RW)
        at += 2 * CH * RW
        rec_out = carve(big_h, at, 2 * CH * RW).rearrange("p (s t c) -> p s t c", s=2, c=RW)
        at += 2 * CH * RW
        z1 = carve(big_h, at, CH * 4).rearrange("p (t h) -> p t h", h=HEADS)
        at += CH * 4
        z2 = carve(big_h, at, CH * 4).rearrange("p (t h) -> p t h", h=HEADS)
        at += CH * 4
        dq = carve(big_h, at, CH * 8).rearrange("p (q t h) -> p q t h", q=2, h=HEADS)
        at += CH * 8
        vals = carve(big_h, at, CH * 20).rearrange("p (t h k) -> p t h k", h=HEADS, k=5)
        at += CH * 20
        not_start = carve(big_h, at, FC)
        y_sb = ring[0:MQ, 0:4 * NE * D].rearrange("p (q e d) -> p q e d", q=QB, e=NE)
        at = 0
        node_r = carve(big_t, at, NT * RW).rearrange("p (t c) -> p t c", c=RW)
        at += NT * RW
        node_c = carve(big_t, at, NT * CR).rearrange("p (t c) -> p t c", c=CR)
        at += NT * CR
        y_in = carve(big_t, at, 2 * NE * D).rearrange("p (s e d) -> p s e d", s=2, e=NE)
        at += 2 * NE * D
        x_in = carve(big_t, at, 2 * D).rearrange("p (s d) -> p s d", s=2)
        at += 2 * D
        x_out = carve(big_t, at, 2 * D).rearrange("p (s d) -> p s d", s=2)
        at += 2 * D
        rowt = carve(big_t, at, 12 * P).rearrange("p (s c) -> p s c", c=P)
        at += 12 * P
        s_tmp = carve(big_t, at, NT * 20).rearrange("p (t h k) -> p t h k", h=HEADS, k=5)
        at += NT * 20
        n_tmp = carve(big_t, at, 8 * NT * 4).rearrange("p (s t h) -> p s t h", s=8, h=4)
        at += 8 * NT * 4
        n16 = carve(big_t, at, 2 * NT * HK).rearrange("p (s t c) -> p s t c", s=2, c=HK)
        at += 2 * NT * HK
        last = carve(big_t, at, 4 * 20).rearrange("p (s c) -> p s c", c=20)
        at += 80
        carried = carve(big_t, at, 60)
        at += 60
        gates = carve(big_t, at, NT * NE).rearrange("p (t e) -> p t e", e=NE)

        ident = sb("ident", [P, P])
        lower = sb("lower", [P, P])
        ones = sb("ones", [P, P])
        iota_row = sb("iota_row", [P, P])
        iota_bf = sb("iota_bf", [P, P], BF16)
        part_i = sb("part_i", [P, 1], I32)
        sgn_i = sb("sgn_i", [P, 8], I32)
        sgn = sb("sgn", [P, 8])
        eps = sb("eps", [P, 1])
        zeros = sb("zeros", [P, 256])
        no_edge = sb("no_edge", [P, CR])
        wp_sb = sb("wp_sb", [P, KD, P])
        bp_sb = sb("bp_sb", [P, 1])
        w1_sb = sb("w1_sb", [P, D])
        w2_sb = sb("w2_sb", [P, D])
        wg_sb = sb("wg_sb", [P, KD, HK])
        att = sb("att", [P, 2, HK])
        gat_par = sb("gat_par", [P, 3, HK])
        b1m = sb("b1m", [P, NE * FB])
        b2m = sb("b2m", [1, NE, D])

        g_cols = sb("g_cols", [P, 3, GG * ET])
        srcT = g_cols[:, 0, :].bitcast(I32).rearrange("p (g j) -> p g j", j=ET)
        relT = g_cols[:, 1, :].rearrange("p (g j) -> p g j", j=ET)
        wT = g_cols[:, 2, :].rearrange("p (g j) -> p g j", j=ET)
        h_now = carve(big_t, 9 * FC, GN)
        h_now2 = g_cols[:, :, :].rearrange("p a n -> p (a n)")[:, 0:GN]
        att_tmp = g_cols[:, :, :].rearrange("p a n -> p (a n)")[:, GN:GN + GT * HK].rearrange("p (t c) -> p t c", c=HK)
        spread = sb("spread", [P, 4])
        base_row = sb("base_row", [1, 2, GG], I32)
        base_f = sb("base_f", [1, GG])
        base_all = sb("base_all", [P, GG])
        far = sb("far", [1, 1], I32)
        far_cols = sb("far_cols", [P, 2, ET])
        g_idx = sb("g_idx", [P, 2, ET], I32)

        s_src = sb("s_src", [P, FC], I32)
        ends = sb("ends", [P, 2])
        pen = sb("pen", [P, FC])
        f_idx = sb("f_idx", [P, 2, CH], I32)
        first_idx = sb("first_idx", [P, 1], I32)
        cum = sb("cum", [P, 5, 64])
        has = sb("has", [P, NT])
        e_idx = sb("e_idx", [P, NT], I32)
        st_idx = sb("st_idx", [P, NT], I32)
        carry_idx = sb("carry_idx", [P, 1], I32)
        a_first = sb("a_first", [P, HEADS])

        st6 = sb("st6", [P, GT, 6])
        mv = sb("mv", [P, GT, 2])
        sd = sb("sd", [P, GT])
        rs = sb("rs", [P, GT])
        nm = sb("nm", [P, GT])
        hp_sb = sb("hp_sb", [P, GT, P])
        iota_i = hp_sb[:, 0, :].bitcast(I32)
        tab = sb("tab", [P, NT, RW])
        adst = sb("adst", [P, NT, HEADS])

        ps = ctx.enter_context(nc.psum_tensor("ps", [P, 8, 512], F32))
        flat = ps[:, :, :].rearrange("p b n -> p (b n)")

        x_ld, par_in, ge_in, fe_in = sem("x_ld"), sem("par_in"), sem("ge_in"), sem("fe_in")
        pool_c, dv, consts = sem("pool_c"), sem("dv"), sem("consts")
        ln_mv, ln_sd, ln_xn = sem("ln_mv"), sem("ln_sd"), sem("ln_xn")
        tp_done, tp_ev = sem("tp_done"), sem("tp_ev")
        h_mm, h_ev, hb_mm, hb_ev, hp_out = sem("h_mm"), sem("h_ev"), sem("hb_mm"), sem("hb_ev"), sem("hp_out")
        rel_rdy, ge_tp, ge_ev = sem("rel_rdy"), sem("ge_tp"), sem("ge_ev")
        far_idx, far_gath, far_oh, far_mm, far_add, agg_done = (sem("far_idx"), sem("far_gath"), sem("far_oh"),
                                                                sem("far_mm"), sem("far_add"), sem("agg_done"))
        idx_cp, oh_rdy, mm_done, add_done = sem("idx_cp"), sem("oh_rdy"), sem("mm_done"), sem("add_done")
        gath = [sem(f"gath{i}") for i in range(2)]
        key_rdy, key_tp, key_back = sem("key_rdy"), sem("key_tp"), sem("key_back")
        hist_rdy, hist_mm, cum_rdy, cum_mm = sem("hist_rdy"), sem("hist_mm"), sem("cum_rdy"), sem("cum_mm")
        ends_rdy, sorted_s = sem("ends_rdy"), sem("sorted_s")
        sq_done, o_mm, x2_rdy, x2_out = sem("sq_done"), sem("o_mm"), sem("x2_rdy"), sem("x2_out")
        t2_done, t2_ev, g_mm, tab_rdy, tab_out = sem("t2_done"), sem("t2_ev"), sem("g_mm"), sem("tab_rdy"), sem("tab_out")
        zero_rdy, zero_out, a_scat, a_in, af_in = sem("zero_rdy"), sem("zero_out"), sem("a_scat"), sem("a_in"), sem("af_in")
        fidx_cp = sem("fidx_cp")
        bias_in, ln_rs, h_cp, x_cp = sem("bias_in"), sem("ln_rs"), sem("h_cp"), sem("x_cp")
        fgath = [sem(f"fgath{i}") for i in range(2)]
        q_rdy, ex_done, sc_done, in_free = sem("q_rdy"), sem("ex_done"), sem("sc_done"), sem("in_free")
        rec_st = [sem(f"rec_st{i}") for i in range(2)]
        mw_in, up_mm, gelu_done, dn_mm, y_ev, y_st = (sem("mw_in"), sem("up_mm"), sem("gelu_done"), sem("dn_mm"),
                                                      sem("y_ev"), sem("y_st"))
        r_in, last_rdy, last_tp, row_q, row_ex, back_rdy, back_tp = (
            sem("r_in"), sem("last_rdy"), sem("last_tp"), sem("row_q"), sem("row_ex"), sem("back_rdy"), sem("back_tp"))
        c_rdy, c_scat, c_in, nd_q, nd_act = sem("c_rdy"), sem("c_scat"), sem("c_in"), sem("nd_q"), sem("nd_act")
        fy_in = [sem(f"fy_in{i}") for i in range(2)]
        fo_rdy = sem("fo_rdy")
        fo_out = [sem(f"fo_out{i}") for i in range(2)]

        scrap = sb("scrap", [P, 4])

        def apart(eng):
            if eng.engine == nc.gpsimd.engine:
                eng.tensor_tensor(scrap[:, 0:1], ones[:, 0:1], ones[:, 0:1], ALU.mult)
            else:
                eng.memset(scrap[:, 1:2], 0.0)

        block = ctx.enter_context(nc.Block())

        def row_of(ap):
            return ap.rearrange("(a n) -> a n", a=1)

        N_PAR = 12

        @block.sync
        def _(sp):
            sp.dma_start(g_src[0:GG, :], gsrc).then_inc(ge_in, 16)
            sp.dma_start(g_dst[0:GG, :], gdst).then_inc(ge_in, 16)
            sp.dma_start(g_w[0:GG, :], gw).then_inc(ge_in, 16)
            for g in range(NG):
                sp.dma_start(x_all[:, g * GT:(g + 1) * GT, :],
                             x[g * GN:(g + 1) * GN, :].rearrange("(t p) d -> p t d", p=P)).then_inc(x_ld, 16)
            sp.dma_start(wp_sb[:, :, :], WpT.rearrange("(k p) f -> p k f", p=P)).then_inc(par_in, 16)
            sp.dma_start(bp_sb[:, :], bp.rearrange("(p a) -> p a", a=1)).then_inc(par_in, 16)
            sp.dma_start(w1_sb[:, :], W1T).then_inc(par_in, 16)
            sp.dma_start(w2_sb[:, :], W2T).then_inc(par_in, 16)
            sp.dma_start(wg_sb[:, :, :], Wgat.rearrange("(k p) f -> p k f", p=P)).then_inc(par_in, 16)
            sp.dma_start(att[:, 0, :], att_src.rearrange("h e -> (h e)").partition_broadcast(P)).then_inc(par_in, 16)
            sp.dma_start(att[:, 1, :], att_dst.rearrange("h e -> (h e)").partition_broadcast(P)).then_inc(par_in, 16)
            sp.dma_start(gat_par[:, 0, :], b_gat.partition_broadcast(P)).then_inc(par_in, 16)
            sp.dma_start(gat_par[:, 1, :], ln_gamma.partition_broadcast(P)).then_inc(par_in, 16)
            sp.dma_start(gat_par[:, 2, :], ln_beta.partition_broadcast(P)).then_inc(par_in, 16)
            sp.dma_start(b1m[:, :], mb1).then_inc(par_in, 16)
            sp.dma_start(b2m[:, :, :].rearrange("p e d -> p (e d)"), mb2).then_inc(par_in, 16)
            sp.dma_start(e_src, fsrc).then_inc(fe_in, 16)
            sp.dma_start(e_dst, fdst).then_inc(fe_in, 16)
            sp.wait_ge(zero_rdy, 1)
            zero_reps = EF * HEADS // P // 256
            sp.dma_start(adst_edge[0:EF, :].rearrange("(p r t) h -> p r (t h)", p=P, r=zero_reps),
                         zeros[:, :].unsqueeze(1).broadcast_to([P, zero_reps, 256])).then_inc(zero_out, 16)
            sp.dma_start(adst_tab[NP:TRASH, :].rearrange("(p t) h -> p (t h)", p=P),
                         zeros[:, 0:(TRASH - NP) * HEADS // P]).then_inc(zero_out, 16)
            sp.dma_start(carry_tab[0:NP, :].rearrange("(p t) c -> p t c", p=P),
                         no_edge[:, :].unsqueeze(1).broadcast_to([P, NT, CR])).then_inc(zero_out, 16)
            sp.wait_ge(ge_ev, 3)
            sp.dma_start(b12[:, 0, :], b1.partition_broadcast(P)).then_inc(bias_in, 16)
            sp.dma_start(b12[:, 1, :], b2.partition_broadcast(P)).then_inc(bias_in, 16)
            with sp.Fori(0, NG) as g:
                sp.wait_ge(hb_ev, g + 1)
                sp.dma_start(hp_tab[bass.ds(g * GN, GN), :].rearrange("(t p) f -> p t f", p=P),
                             hp_sb[:, :, :]).then_inc(hp_out, 16)
            with sp.Fori(0, NG) as g:
                rows = bass.ds(g * GN, GN)
                tiles = bass.ds(g * GT, GT)
                sp.wait_ge(x2_rdy, g + 1)
                sp.dma_start(x2_tab[rows, :].rearrange("(t p) d -> p t d", p=P), x_all[:, tiles, :]).then_inc(x2_out, 16)
                sp.wait_ge(tab_rdy, g + 1)
                sp.dma_start(src_tab[rows, :].rearrange("(t p) c -> p t c", p=P), tab[:, tiles, :]).then_inc(tab_out, 16)
                sp.dma_start(adst_tab[rows, :].rearrange("(t p) c -> p t c", p=P), adst[:, tiles, :]).then_inc(tab_out, 16)
            sp.wait_ge(x2_out, 16 * NG)
            sp.dma_start(w1m, mW1.rearrange("e (k p) f -> p e k f", p=P)).then_inc(mw_in, 16)
            sp.dma_start(w2m, mW2.rearrange("e (f p) d -> p e f d", p=P)).then_inc(mw_in, 16)
            sp.wait_ge(a_scat, 16 * NT)
            sp.dma_start(a_edge, adst_edge[0:EF, :].rearrange("(p t) h -> p t h", p=P)).then_inc(a_in, 16)
            rec_v = rec_tab.rearrange("(p t) c -> p (t c)", p=P)
            y_v = y_tab.rearrange("(b q p) n -> b p q n", q=QB, p=MQ)

            def store_records(i, s):
                sp.wait_ge(sc_done, 2 * i + s + 1)
                sp.dma_start(rec_v[:, bass.ds((2 * i + s) * CH * RW, CH * RW)],
                             rec_out[:, s, :, :].rearrange("p t c -> p (t c)")).then_inc(rec_st[s], 16)

            with sp.Fori(0, NCH // 2) as i:
                for s in range(2):
                    store_records(i, s)
            sp.wait_ge(c_scat, 16)
            sp.dma_start(node_c, carry_tab[0:NP, :].rearrange("(t p) c -> p t c", p=P)).then_inc(c_in, 16)

            def load(t, s):
                sp.dma_start(y_in[:, s, :, :].rearrange("p e d -> p (e d)"),
                             y_tab[bass.ds(t * P, P), :]).then_inc(fy_in[s], 16)
                sp.dma_start(x_in[:, s, :], x2_tab[bass.ds(t * P, P), :]).then_inc(fy_in[s], 16)

            def store(t, s, rows):
                sp.wait_ge(fo_rdy, t + 1)
                sp.dma_start(out[bass.ds(t * P, rows), :], x_out[0:rows, s, :]).then_inc(fo_out[s], 16)

            sp.wait_ge(y_st, 16 * NMB)
            load(0, 0)
            load(1, 1)
            with sp.Fori(1, NT // 2) as i:
                for s in range(2):
                    store(2 * i + s - 2, s, P)
                    load(2 * i + s, s)
            store(NT - 3, 0, P)
            load(NT - 1, 0)
            store(NT - 2, 1, P)
            store(NT - 1, 0, N - (NT - 1) * P)
            sp.wait_ge(fo_out[0], 16 * (NT // 2 + 1))
            sp.wait_ge(fo_out[1], 16 * (NT // 2))

        @block.gpsimd
        def _(pool):
            pool.memset(ident[:, :], 0.0).then_inc(pool_c, 1)
            pool.memset(lower[:, :], 1.0).then_inc(pool_c, 1)
            pool.iota(iota_i, [[1, P]], base=0, channel_multiplier=0).then_inc(pool_c, 1)
            pool.iota(part_i[:, :], [[0, 1]], base=0, channel_multiplier=1).then_inc(pool_c, 1)
            pool.wait_ge(pool_c, 4)
            pool.affine_select(out=ident[:, :], in_=ident[:, :], compare_op=ALU.not_equal, fill=1.0,
                               base=0, pattern=[[-1, P]], channel_multiplier=1).then_inc(pool_c, 1)
            pool.affine_select(out=lower[:, :], in_=lower[:, :], compare_op=ALU.is_gt, fill=0.0,
                               base=0, pattern=[[1, P]], channel_multiplier=-1).then_inc(pool_c, 1)

            def gather_group(g, s, n):
                pool.tensor_copy(g_idx[:, s, :], srcT[:, bass.ds(g, 1), :].rearrange("p a j -> p (a j)")).then_inc(idx_cp, 1)
                pool.wait_ge(idx_cp, g + 1)
                apart(pool)
                for j in range(ET):
                    pool.indirect_dma_start(out=g_ring[:, s, j, :], out_offset=None, in_=hp_tab,
                                            in_offset=bass.IndirectOffsetOnAxis(ap=g_idx[:, s, j:j + 1], axis=0)
                                            ).then_inc(gath[s], 16)

            pool.wait_ge(consts, 1)
            pool.wait_ge(ge_ev, 3)
            pool.wait_ge(hp_out, 16 * NG)
            for g in range(2):
                gather_group(g, g, 0)
            with pool.Fori(1, GG // 2) as i:
                for s in range(2):
                    pool.wait_ge(mm_done, 2 * i + s - 1)
                    gather_group(2 * i + s, s, i)

            with pool.If(pool.value_load(far[0:1, 0:1], min_val=0, max_val=1) > 0):
                pool.wait_ge(mm_done, GG)
                with pool.Fori(0, GG) as g:
                    pool.wait_ge(far_mm, g * NT)
                    pool.tensor_copy(g_idx[:, 0, :], srcT[:, bass.ds(g, 1), :].rearrange("p a j -> p (a j)")).then_inc(far_idx, 1)
                    pool.wait_ge(far_idx, g + 1)
                    apart(pool)
                    for j in range(ET):
                        pool.indirect_dma_start(out=g_ring[:, 0, j, :], out_offset=None, in_=hp_tab,
                                                in_offset=bass.IndirectOffsetOnAxis(ap=g_idx[:, 0, j:j + 1], axis=0)
                                                ).then_inc(far_gath, 16)

            def copy_h(g):
                pool.wait_ge(o_mm, g)
                pool.tensor_copy(h_now2, hT[:, bass.ds(g * GN, GN)]).then_inc(h_cp, 1)

            def copy_x(g):
                pool.wait_ge(t2_ev, 2 * g + 2)
                pool.tensor_copy(xn2T[:, :, bass.ds(g * GN, GN)], xnT).then_inc(x_cp, 1)

            pool.wait_ge(agg_done, 1)
            copy_h(0)
            with pool.Fori(1, NG) as g:
                copy_h(g)
                copy_x(g - 1)
            copy_x(NG - 1)

            def gather_chunk(c, s):
                pool.tensor_copy(f_idx[:, s, :], s_src[:, bass.ds(c * CH, CH)]).then_inc(fidx_cp, 1)
                pool.wait_ge(fidx_cp, c + 1)
                apart(pool)
                for j in range(CH):
                    pool.indirect_dma_start(out=rec_in[:, s, j, :], out_offset=None, in_=src_tab,
                                            in_offset=bass.IndirectOffsetOnAxis(ap=f_idx[:, s, j:j + 1], axis=0)
                                            ).then_inc(fgath[s], 16)

            pool.wait_ge(sorted_s, 1)
            pool.wait_ge(tab_out, 32 * NG)
            for c in range(2):
                gather_chunk(c, c)
            pool.wait_ge(zero_out, 48)
            for t in range(NT):
                pool.indirect_dma_start(out=adst_edge, out_offset=bass.IndirectOffsetOnAxis(ap=st_idx[:, t:t + 1], axis=0),
                                        in_=adst[:, t, :], in_offset=None).then_inc(a_scat, 16)
            pool.indirect_dma_start(out=a_first[:, :], out_offset=None, in_=adst_tab,
                                    in_offset=bass.IndirectOffsetOnAxis(ap=first_idx[:, :], axis=0)).then_inc(af_in, 16)
            with pool.Fori(1, NCH // 2) as i:
                for s in range(2):
                    pool.wait_ge(in_free, 2 * i + s - 1)
                    gather_chunk(2 * i + s, s)

            pool.wait_ge(rec_st[0], 16 * NCH // 2)
            pool.wait_ge(rec_st[1], 16 * NCH // 2)
            pool.wait_ge(dn_mm, NMB * NE * QB)
            for t in range(NT):
                pool.indirect_dma_start(out=node_r[:, t, :], out_offset=None, in_=rec_tab,
                                        in_offset=bass.IndirectOffsetOnAxis(ap=e_idx[:, t:t + 1], axis=0)
                                        ).then_inc(r_in, 16)
            pool.wait_ge(c_rdy, 1)
            pool.indirect_dma_start(out=carry_tab, out_offset=bass.IndirectOffsetOnAxis(ap=carry_idx[:, :], axis=0),
                                    in_=carried[:, 0:CR], in_offset=None).then_inc(c_scat, 16)

        @block.scalar
        def _(act):
            act.wait_ge(consts, 1)
            act.wait_ge(par_in, 16 * N_PAR)
            with act.Fori(0, NG) as g:
                act.wait_ge(ln_mv, g + 1)
                nc.scalar.activation(sd[:, :], mv[:, :, 1], ACT.Sqrt, bias=eps[:, :]).then_inc(ln_sd, 1)
                act.wait_ge(tp_done, g + 1)
                nc.scalar.activation(xnT[:, 0, :].rearrange("p (t n) -> p t n", n=P),
                                     flat[:, 0:GN].rearrange("p (t n) -> p t n", n=P),
                                     ACT.Copy).then_inc(tp_ev, 1)
                act.wait_ge(h_mm, g + 1)
                nc.scalar.activation(h_now.rearrange("p (b n) -> p b n", b=2), ps[:, 4:6, 0:HN],
                                     ACT.Relu, bias=bp_sb[:, :]).then_inc(h_ev, 1)
                nc.scalar.activation(hT[:, bass.ds(g * GN, GN)].rearrange("p (b n) -> p b n", b=2), ps[:, 4:6, 0:HN],
                                     ACT.Relu, bias=bp_sb[:, :]).then_inc(h_ev, 1)
                act.wait_ge(hb_mm, g + 1)
                act.wait_ge(hp_out, 16 * g)
                nc.scalar.activation(hp_sb[:, :, :].rearrange("p t f -> p (t f)"), flat[:, 6 * 512:6 * 512 + GN],
                                     ACT.Square).then_inc(hb_ev, 1)
            def roots(g):
                act.wait_ge(o_mm, g)
                nc.scalar.activation(hp_sb[:, :, :].rearrange("p t f -> p (t f)"), aggT[:, bass.ds(g * GN, GN)],
                                     ACT.Sqrt).then_inc(sq_done, 1)

            def normalize(g):
                act.wait_ge(ln_mv, NG + 1 + g)
                nc.scalar.activation(sd[:, :], mv[:, :, 1], ACT.Sqrt, bias=eps[:, :]).then_inc(ln_sd, 1)
                act.wait_ge(ln_rs, g + 1)
                act.wait_ge(t2_done, g)
                for t in range(GT):
                    op = nc.scalar.activation(xn[:, t, :], x_all[:, bass.ds(g * GT + t, 1), :].rearrange("p a d -> p (a d)"),
                                              ACT.Identity, bias=nm[:, t:t + 1], scale=rs[:, t:t + 1])
                op.then_inc(ln_xn, 1)

            def turned_half(g):
                act.wait_ge(t2_done, g + 1)
                act.wait_ge(x_cp, g)
                act.wait_ge(g_mm, g)
                nc.scalar.activation(xnT[:, 0, :].rearrange("p (t n) -> p t n", n=P),
                                     flat[:, 2048:2048 + GN].rearrange("p (t n) -> p t n", n=P),
                                     ACT.Copy).then_inc(t2_ev, 1)

            act.wait_ge(agg_done, 1)
            roots(0)
            roots(1)
            normalize(0)
            with act.Fori(1, NG - 1) as g:
                roots(g + 1)
                turned_half(g - 1)
                normalize(g)
            turned_half(NG - 2)
            normalize(NG - 1)
            turned_half(NG - 1)

            def exps(c):
                act.wait_ge(q_rdy, c + 1)
                nc.scalar.activation(dq, dq, ACT.Exp).then_inc(ex_done, 1)

            def experts(b):
                for e in range(NE):
                    for f in range(FB):
                        n = (b * NE + e) * FB + f
                        act.wait_ge(up_mm, n + 1)
                        nc.scalar.activation(hid[:, e % 2, f, :], ps[:, f % 2, 0:MB], ACT.Gelu,
                                             bias=b1m[:, e * FB + f:e * FB + f + 1]).then_inc(gelu_done, 1)
                    if e == 0:
                        act.wait_ge(y_st, 16 * b)
                    act.wait_ge(dn_mm, ((b * NE) + e + 1) * QB)
                    for h in range(2):
                        nc.scalar.activation(y_sb[:, 2 * h:2 * h + 2, e, :],
                                             ps[0:MQ, 2 + h, :].rearrange("p (q d) -> p q d", q=2),
                                             ACT.Copy).then_inc(y_ev, 1)
                act.wait_ge(y_ev, (b + 1) * 2 * NE)
                act.dma_start(y_tab.rearrange("(b q p) n -> b p q n", q=QB, p=MQ)[bass.ds(b, 1)].rearrange("a p q n -> p (a q) n"),
                              y_sb.rearrange("p q e d -> p q (e d)")).then_inc(y_st, 16)

            with act.Fori(0, NMB) as b:
                exps(2 * b)
                exps(2 * b + 1)
                experts(b)
            for c in range(2 * NMB, NCH):
                exps(c)
            act.wait_ge(row_q, 1)
            nc.scalar.activation(rowt[0:20, 5:7, :], rowt[0:20, 5:7, :], ACT.Exp).then_inc(row_ex, 1)
            act.wait_ge(nd_q, 1)
            nc.scalar.activation(n_tmp[:, 4:7], n_tmp[:, 4:7], ACT.Exp).then_inc(nd_act, 1)
            act.wait_ge(nd_q, 2)
            nc.scalar.activation(n_tmp[:, 7, :, 3], n_tmp[:, 7, :, 1], ACT.Sqrt, bias=eps[:, :]).then_inc(nd_act, 1)
            act.wait_ge(nd_q, 3)
            nc.scalar.activation(n_tmp[:, 2], n_tmp[:, 2], ACT.Exp).then_inc(nd_act, 1)

        @block.tensor
        def _(pe):
            pe.wait_ge(pool_c, 6)
            pe.wait_ge(consts, 1)
            pe.wait_ge(ge_in, 48)
            pe.wait_ge(rel_rdy, 1)
            for n, rows in enumerate((g_srcf, g_dstf, g_w)):
                for j in range(ET):
                    at = ps[:, 2 * n + j // 4, (j % 4) * GG:(j % 4 + 1) * GG]
                    mm = nc.tensor.transpose(at, rows[0:GG, j * P:(j + 1) * P], ident[0:GG, 0:GG])
                mm.then_inc(ge_tp, 1)
            for i in range(2):
                mm = nc.tensor.transpose(ps[0:1, 6, i * GG:(i + 1) * GG], spread[0:GG, i:i + 1], ident[0:GG, 0:GG])
            mm.then_inc(ge_tp, 1)
            pe.wait_ge(ge_ev, 4)
            nc.tensor.matmul(ps[:, 7, 0:GG], ones[0:1, :], base_f[:, :], start=True, stop=True).then_inc(ge_tp, 1)
            pe.wait_ge(par_in, 16 * N_PAR)
            pe.wait_ge(ge_ev, 5)
            with pe.Fori(0, NG) as g:
                pe.wait_ge(ln_xn, g + 1)
                pe.wait_ge(tp_ev, 2 * g)
                for t in range(GT):
                    for k in range(KD):
                        mm = nc.tensor.transpose(ps[:, 2 * k + t // 4, (t % 4) * P:(t % 4 + 1) * P],
                                                 xn[:, t, k * P:(k + 1) * P], ident[:, :])
                mm.then_inc(tp_done, 1)
                pe.wait_ge(tp_ev, 2 * g + 2)
                pe.wait_ge(h_ev, 2 * g)
                for h in range(2):
                    for k in range(KD):
                        mm = nc.tensor.matmul(ps[:, 4 + h, 0:HN], wp_sb[:, k, :], xnT[:, k, h * HN:(h + 1) * HN],
                                              start=(k == 0), stop=(k == KD - 1))
                mm.then_inc(h_mm, 1)
                pe.wait_ge(h_ev, 2 * g + 1)
                pe.wait_ge(hb_ev, g)
                for t in range(GT):
                    mm = nc.tensor.transpose(ps[:, 6 + t // 4, (t % 4) * P:(t % 4 + 1) * P],
                                             h_now[:, t * P:(t + 1) * P], ident[:, :])
                mm.then_inc(hb_mm, 1)
            pe.wait_ge(hb_ev, NG)

            def aggregate(g, s, n):
                pe.wait_ge(gath[s], 16 * ET * (n + 1))
                pe.wait_ge(oh_rdy, g + 1)
                for j in range(ET):
                    mm = nc.tensor.matmul(ps[:, s, 0:P], g_ring[:, s, j, :], oh_ring[:, s, j, :],
                                          start=(j == 0), stop=(j == ET - 1))
                mm.then_inc(mm_done, 1)

            def turn_keys(n, src):
                pe.wait_ge(key_rdy, n + 1)
                for b in range(FC // P):
                    mm = nc.tensor.transpose(ps[:, 2 + b // 4, (b % 4) * P:(b % 4 + 1) * P],
                                             src[:, b * P:(b + 1) * P], ident[:, :])
                mm.then_inc(key_tp, 1)

            def histogram(c):
                pe.wait_ge(hist_rdy, c + 1)
                for t in range(HIST_CH):
                    mm = nc.tensor.matmul(ps[:, 4, 0:64], oh_lo[:, c % 2, t, :], oh_hi[:, c % 2, t, :],
                                          start=(c == 0 and t == 0), stop=(c == FC // HIST_CH - 1 and t == HIST_CH - 1))
                mm.then_inc(hist_mm, 1)

            turns = 0
            for g, step in enumerate(STEPS):
                for kind, a, b in step:
                    if kind == "turn":
                        turn_keys(turns, keys[b])
                        turns += 1
                    elif kind == "hist":
                        histogram(a)
                    elif kind == "cum":
                        pe.wait_ge(cum_rdy, 1)
                        nc.tensor.matmul(ps[:, 4, 64:128], lower[:, :], cum[:, 0, :], start=True, stop=True)
                        nc.tensor.matmul(ps[:, 4, 128:192], ones[:, :], cum[:, 0, :], start=True, stop=True).then_inc(cum_mm, 1)
                if g >= 2:
                    pe.wait_ge(add_done, g - 1)
                aggregate(g, g % 2, g // 2)
            with pe.Fori(len(STEPS) // 2, GG // 2) as i:
                for s in range(2):
                    pe.wait_ge(add_done, 2 * i + s - 1)
                    aggregate(2 * i + s, s, i)

            with pe.If(pe.value_load(far[0:1, 0:1], min_val=0, max_val=1) > 0):
                with pe.Fori(0, GG) as g:
                    with pe.Fori(0, NT) as c:
                        pe.wait_ge(far_gath, 16 * ET * (g + 1))
                        pe.wait_ge(far_oh, g * NT + c + 1)
                        for j in range(ET):
                            mm = nc.tensor.matmul(ps[:, 0, 0:P], g_ring[:, 0, j, :], oh_ring[:, 0, j, :],
                                                  start=(j == 0), stop=(j == ET - 1))
                        mm.then_inc(far_mm, 1)

            def outputs(g):
                pe.wait_ge(sq_done, g + 1)
                pe.wait_ge(h_cp, g + 1)
                pe.wait_ge(x2_rdy, g)
                for t in range(GT):
                    at = ps[:, t // 2, (t % 2) * D:(t % 2 + 1) * D]
                    nc.tensor.matmul(at, h_now2[:, t * P:(t + 1) * P], w1_sb[:, :], start=True, stop=False)
                    mm = nc.tensor.matmul(at, hp_sb[:, t, :], w2_sb[:, :], start=False, stop=True)
                mm.then_inc(o_mm, 1)

            def features(g):
                pe.wait_ge(ln_xn, NG + 1 + g)
                pe.wait_ge(t2_ev, 2 * g)
                pe.wait_ge(tab_rdy, g)
                for t in range(GT):
                    for k in range(KD):
                        mm = nc.tensor.transpose(ps[:, 4 + 2 * k + t // 4, (t % 4) * P:(t % 4 + 1) * P],
                                                 xn[:, t, k * P:(k + 1) * P], ident[:, :])
                mm.then_inc(t2_done, 1)
                pe.wait_ge(t2_ev, 2 * g + 2)
                for t in range(GT):
                    for k in range(KD):
                        mm = nc.tensor.matmul(ps[:, 7, 384 + t * HK:384 + (t + 1) * HK],
                                              xnT[:, k, t * P:(t + 1) * P], wg_sb[:, k, :],
                                              start=(k == 0), stop=(k == KD - 1))
                mm.then_inc(g_mm, 1)

            outputs(0)
            with pe.Fori(1, NG) as g:
                outputs(g)
                features(g - 1)
            features(NG - 1)

            pe.wait_ge(mw_in, 32)
            pe.wait_ge(tab_rdy, NG)
            pe.wait_ge(x_cp, NG)
            with pe.Fori(0, NMB) as b:
                for e in range(NE):
                    for f in range(FB):
                        n = (b * NE + e) * FB + f
                        if f >= 2 or e >= 1:
                            pe.wait_ge(gelu_done, n - 1)
                        else:
                            pe.wait_ge(gelu_done, b * NE * FB)
                        for k in range(KD):
                            mm = nc.tensor.matmul(ps[:, f % 2, 0:MB], w1m[:, e, k, f * P:(f + 1) * P],
                                                  xn2T[:, k, bass.ds(b * MB, MB)], start=(k == 0), stop=(k == KD - 1))
                        mm.then_inc(up_mm, 1)
                    pe.wait_ge(gelu_done, (b * NE + e + 1) * FB)
                    pe.wait_ge(y_ev, (b * NE + e) * 2)
                    for q in range(QB):
                        at = ps[0:MQ, 2 + q // 2, (q % 2) * D:(q % 2 + 1) * D]
                        for f in range(FB):
                            nc.tensor.matmul(at, hid[:, e % 2, f, q * MQ:(q + 1) * MQ], w2m[:, e, f, :],
                                             start=(f == 0), stop=False)
                        nc.tensor.matmul(at, ones[0:1, 0:MQ], b2m[:, e, :], start=False, stop=True).then_inc(dn_mm, 1)

            pe.wait_ge(last_rdy, 1)
            for n in range(4):
                mm = nc.tensor.transpose(ps[0:20, 4, n * P:(n + 1) * P], last[:, n, :], ident[:, :])
            mm.then_inc(last_tp, 1)
            pe.wait_ge(back_rdy, 1)
            for n in range(3):
                mm = nc.tensor.transpose(ps[:, 5, n * 20:(n + 1) * 20], rowt[0:20, 9 + n, :], ident[0:20, 0:20])
            mm.then_inc(back_tp, 1)

        @block.vector
        def _(dve):
            V = nc.vector
            chain = [0]

            def step(*ops):
                for ins in ops:
                    ins.then_inc(dv, 1)
                    chain[0] += 1
                dve.wait_ge(dv, chain[0])

            class Loop:

                def __init__(self, sem_, at, i):
                    self.sem, self.at, self.i, self.n = sem_, at, i, 0

                def step(self, per, *ops):
                    for ins in ops:
                        ins.then_inc(self.sem, 1)
                        self.n += 1
                    dve.wait_ge(self.sem, self.i * per + (self.at + self.n))

            def bc(ap, shape):
                return ap.broadcast_to(shape)

            ops = [V.memset(ones[:, :], 1.0), V.memset(eps[:, :], LN_EPS), V.memset(zeros[:, :], 0.0),
                   V.memset(no_edge[:, 0:20], -BIG), V.memset(no_edge[:, 20:40], 0.0),
                   V.memset(tab[:, :, :], 1.0), V.memset(cum[:, :, :], 0.0), V.memset(aggT, 0.0)]
            dve.wait_ge(pool_c, 6)
            ops += [V.tensor_copy(iota_row[:, :], iota_i), V.tensor_copy(iota_bf[:, :], iota_i)]
            step(*ops)
            for i in range(8):
                dve_op = V.tensor_scalar(sgn_i[:, i:i + 1], part_i[:, :], i, 1, ALU.logical_shift_right, ALU.bitwise_and)
                dve_op.then_inc(dv, 1)
                chain[0] += 1
            dve.wait_ge(dv, chain[0])
            step(V.tensor_copy(sgn[:, :], sgn_i[:, :]))
            step(V.tensor_scalar(sgn[:, :], sgn[:, :], -2.0, 1.0, ALU.mult, ALU.add))
            V.memset(spread[:, :], 0.0).then_inc(consts, 1)
            V.memset(zeros[:, 0:1], 0.0).then_inc(zero_rdy, 1)

            dve.wait_ge(ge_in, 48)
            step(V.tensor_copy(g_srcf[0:GG, :], g_src[0:GG, :]), V.tensor_copy(g_dstf[0:GG, :], g_dst[0:GG, :]))
            step(V.tensor_reduce(spread[0:GG, 0:1], g_dstf[0:GG, :], AX.X, ALU.min))
            step(V.tensor_scalar(g_dstf[0:GG, :], g_dstf[0:GG, :], spread[0:GG, 0:1], None, ALU.subtract))
            V.tensor_reduce(spread[0:GG, 1:2], g_dstf[0:GG, :], AX.X, ALU.max).then_inc(rel_rdy, 1)
            for n, cols in enumerate((srcT, relT, wT)):
                dve.wait_ge(ge_tp, n + 1)
                for h in range(2):
                    op = V.tensor_copy(cols[:, :, 4 * h:4 * h + 4].rearrange("p g j -> p j g"),
                                       ps[:, 2 * n + h, 0:4 * GG].rearrange("p (j g) -> p j g", g=GG))
                op.then_inc(ge_ev, 1)
            dve.wait_ge(ge_tp, 4)
            step(V.tensor_copy(base_row[:, :, :], ps[0:1, 6, 0:2 * GG].rearrange("p (a g) -> p a g", a=2)),
                 V.tensor_reduce(scrap[0:1, 2:3], ps[0:1, 6, GG:2 * GG], AX.X, ALU.max),
                 V.tensor_copy(base_f[:, :], ps[0:1, 6, 0:GG]))
            V.tensor_scalar(far[:, :], scrap[0:1, 2:3], float(P) - 0.5, None, ALU.is_ge).then_inc(ge_ev, 1)
            dve.wait_ge(ge_tp, 5)
            V.tensor_copy(base_all[:, :], ps[:, 7, 0:GG]).then_inc(ge_ev, 1)
            dve.wait_ge(ge_ev, 5)

            def layer_norm(g, loop, per, first):
                apart(dve)
                loop.step(per, *[V.bn_stats(st6[:, t, :], x_all[:, bass.ds(g * GT + t, 1), :].rearrange("p a d -> p (a d)"))
                                 for t in range(GT)])
                apart(dve)
                last_op = [V.bn_aggr(mv[:, t, :], st6[:, t, :]) for t in range(GT)]
                loop.step(per, *last_op[:-1])
                last_op[-1].then_inc(ln_mv, 1)
                dve.wait_ge(ln_sd, g + 1 + first)
                loop.step(per, V.reciprocal(rs[:, :], sd[:, :]))
                for t in range(GT):
                    op = V.tensor_scalar(xn[:, t, :], x_all[:, bass.ds(g * GT + t, 1), :].rearrange("p a d -> p (a d)"),
                                         mv[:, t, 0:1], rs[:, t:t + 1], ALU.subtract, ALU.mult)
                op.then_inc(ln_xn, 1)

            dve.wait_ge(x_ld, 16 * NG)
            per = 2 * GT
            with dve.Fori(0, NG) as g:
                loop = Loop(dv, chain[0], g)
                layer_norm(g, loop, per, 0)
                dve.wait_ge(tp_done, g + 1)
                V.tensor_copy(xnT[:, 1, :].rearrange("p (t n) -> p t n", n=P),
                              flat[:, 1024:1024 + GN].rearrange("p (t n) -> p t n", n=P)).then_inc(tp_ev, 1)
                assert loop.n == per, loop.n
            chain[0] += NG * per
            dve.wait_ge(h_mm, NG)

            def one_hots(g, s):
                for j in range(ET):
                    at = [cols.rearrange("p g j -> p (g j)")[:, bass.ds(g * ET + j, 1)] for cols in (relT, wT)]
                    op = V.tensor_scalar(oh_ring[:, s, j, :], iota_row[:, :], at[0], at[1], ALU.is_equal, ALU.mult)
                op.then_inc(oh_rdy, 1)

            def add_window(g, s):
                base = dve.value_load(base_row[0:1, 0, bass.ds(g, 1)], min_val=0, max_val=NP - 1)
                dve.wait_ge(mm_done, g + 1)
                dve.wait_ge(add_done, g)
                V.tensor_tensor(aggT[:, bass.ds(base, P)], aggT[:, bass.ds(base, P)], ps[:, s, 0:P],
                                ALU.add).then_inc(add_done, 1)

            cur = [0]

            def make_keys():
                dve.wait_ge(fe_in, 32)
                k_i = [k.bitcast(I32) for k in keys]
                step(V.tensor_scalar(k_i[0], e_src, float(N - 1), None, ALU.min),
                     V.tensor_scalar(k_i[1], e_dst, DST_BITS, KEY_TOP, ALU.logical_shift_left, ALU.bitwise_or))
                step(V.tensor_tensor(k_i[0], k_i[0], k_i[1], ALU.bitwise_or))

            def swap_stage(k, j):
                a, b = cur[0], 1 - cur[0]
                d = 1 << j
                if j == k - 1 and k > FLOG - 1 and k - FLOG < 8:
                    i = k - FLOG
                    if i >= 1:
                        step(V.tensor_scalar(keys[a], keys[a], sgn[:, i - 1:i], None, ALU.mult))
                    if k < ELOG:
                        step(V.tensor_scalar(keys[a], keys[a], sgn[:, i:i + 1], None, ALU.mult))
                if j >= FLOG:
                    if j == k - 1:
                        src = turned(a)
                    else:
                        src = keys[a]
                    m = P // (2 * (d >> FLOG))
                    v = src.rearrange("p (c m s i) -> p s c m i", c=FC // P, m=m, s=2)
                    w = keys[b].rearrange("p (c m s i) -> p s c m i", c=FC // P, m=m, s=2)
                    step(V.tensor_tensor(w[:, 0], v[:, 0], v[:, 1], ALU.min),
                         V.tensor_tensor(w[:, 1], v[:, 0], v[:, 1], ALU.max))
                else:
                    src = turned(a) if (j == FLOG - 1 and k > FLOG) else keys[a]
                    if k < FLOG:
                        r, m = FC >> (k + 1), 1 << (k - 1 - j)
                        v = src.rearrange("p (r z m s i) -> p z s r m i", r=r, z=2, m=m, s=2)
                        w = keys[b].rearrange("p (r z m s i) -> p z s r m i", r=r, z=2, m=m, s=2)
                        step(*[V.tensor_tensor(w[:, z, s], v[:, z, 0], v[:, z, 1], (ALU.min, ALU.max)[z ^ s])
                               for z in range(2) for s in range(2)])
                    else:
                        m = FC // (2 * d)
                        v = src.rearrange("p (m s i) -> p s m i", m=m, s=2)
                        w = keys[b].rearrange("p (m s i) -> p s m i", m=m, s=2)
                        step(V.tensor_tensor(w[:, 0], v[:, 0], v[:, 1], ALU.min),
                             V.tensor_tensor(w[:, 1], v[:, 0], v[:, 1], ALU.max))
                cur[0] = b

            n_turn = [0]

            def turned(a):
                V.tensor_copy(spread[0:1, 3:4], zeros[0:1, 1:2]).then_inc(key_rdy, 1)
                n_turn[0] += 1
                dve.wait_ge(key_tp, n_turn[0])
                step(V.tensor_copy(keys[a], flat[:, 2 * 512:2 * 512 + FC]))
                return keys[a]

            def halves():
                step(V.tensor_scalar(half_i, e_dst, P - 1, None, ALU.bitwise_and))
                step(V.tensor_copy(lo_bf, half_i))
                step(V.tensor_scalar(half_i, e_dst, 7, None, ALU.logical_shift_right))
                step(V.tensor_copy(hi_bf, half_i))

            def histogram(c):
                if c >= 2:
                    dve.wait_ge(hist_mm, c - 1)
                cols = slice(c * HIST_CH, (c + 1) * HIST_CH)
                V.tensor_tensor(oh_lo[:, c % 2], bc(iota_bf[:, :].unsqueeze(1), [P, HIST_CH, P]),
                                bc(lo_bf[:, cols].unsqueeze(2), [P, HIST_CH, P]), ALU.is_equal).then_inc(dv, 1)
                chain[0] += 1
                V.tensor_tensor(oh_hi[:, c % 2], bc(iota_bf[:, 0:64].unsqueeze(1), [P, HIST_CH, 64]),
                                bc(hi_bf[:, cols].unsqueeze(2), [P, HIST_CH, 64]), ALU.is_equal).then_inc(hist_rdy, 1)

            def positions():
                dve.wait_ge(hist_mm, FC // HIST_CH)
                V.tensor_copy(cum[:, 0, :], ps[:, 4, 0:64]).then_inc(cum_rdy, 1)
                dve.wait_ge(cum_rdy, 1)
                dve.wait_ge(cum_mm, 1)
                step(V.tensor_copy(cum[:, 2, :], ps[:, 4, 128:192]))
                step(V.tensor_tensor_scan(cum[:, 1, :], ones[:, 0:64], cum[:, 2, :], 0.0, ALU.mult, ALU.add))
                step(V.tensor_tensor(cum[:, 1, :], cum[:, 1, :], cum[:, 2, :], ALU.subtract))
                step(V.tensor_tensor(cum[:, 1, :], cum[:, 1, :], ps[:, 4, 64:128], ALU.add),
                     V.tensor_scalar(has[:, :], cum[:, 0, 0:NT], 0.0, None, ALU.is_gt))
                step(V.tensor_tensor(cum[:, 2, :], cum[:, 1, :], cum[:, 0, :], ALU.add))
                step(V.tensor_scalar(cum[:, 2, :], cum[:, 2, :], -1.0, 0.0, ALU.add, ALU.max))
                step(V.tensor_copy(e_idx[:, :], cum[:, 2, 0:NT]))
                step(V.tensor_copy(cum[:, 4, 0:1], part_i[:, :]))
                step(V.tensor_scalar(cum[:, 3, :], iota_row[:, 0:64], float(P), float(EF), ALU.mult, ALU.add))
                step(V.tensor_scalar(cum[:, 3, :], cum[:, 3, :], cum[:, 4, 0:1], None, ALU.add))
                step(V.tensor_tensor(cum[:, 1, :], cum[:, 1, :], cum[:, 3, :], ALU.subtract))
                step(V.tensor_tensor(cum[:, 1, 0:NT], cum[:, 1, 0:NT], has[:, :], ALU.mult))
                step(V.tensor_tensor(cum[:, 1, :], cum[:, 1, :], cum[:, 3, :], ALU.add))
                step(V.tensor_copy(st_idx[:, :], cum[:, 1, 0:NT]))

            def marks():
                k_i = keys[cur[0]].bitcast(I32)
                t_i = keys[1 - cur[0]].bitcast(I32)
                step(V.tensor_scalar(s_src[:, :], k_i, (1 << DST_BITS) - 1, None, ALU.bitwise_and),
                     V.tensor_scalar(t_i, k_i, DST_BITS, (1 << DST_BITS) - 1, ALU.logical_shift_right, ALU.bitwise_and))
                step(V.tensor_copy(s_dst, t_i))
                V.tensor_copy(ends[:, :], s_dst[:, 0:FC:FC - 1]).then_inc(ends_rdy, 1)
                dve.wait_ge(ends_rdy, 1)
                step(V.tensor_copy(first_idx[:, :], ends[:, 0:1]), V.memset(was_equal[:, 0:1], 0.0),
                     V.tensor_tensor(was_equal[:, 1:FC], s_dst[:, 1:FC], s_dst[:, 0:FC - 1], ALU.is_equal))
                V.tensor_scalar(pen[:, :], was_equal, -1.0, BIG, ALU.add, ALU.mult).then_inc(sorted_s, 1)

            def add_bias(g):
                if g == 0:
                    dve.wait_ge(bias_in, 32)
                    step(V.tensor_tensor(b12[:, 0, :], b12[:, 0, :], b12[:, 1, :], ALU.add))
                group = x_all[:, g * GT:(g + 1) * GT, :]
                step(V.tensor_tensor(group, group, bc(b12[:, 0:1, :], [P, GT, D]), ALU.add))

            def do(kind, a, b):
                if kind == "keys":
                    make_keys()
                    halves()
                elif kind == "bias":
                    add_bias(a)
                elif kind == "stage":
                    swap_stage(a, b)
                elif kind == "hist":
                    histogram(a)
                elif kind == "cum":
                    positions()
                elif kind == "marks":
                    marks()

            for g, todo in enumerate(STEPS):
                one_hots(g, g % 2)
                for kind, a, b in todo:
                    do(kind, a, b)
                if g >= 1:
                    add_window(g - 1, (g - 1) % 2)
            add_window(len(STEPS) - 1, 1)
            done = len(STEPS)
            with dve.Fori(done // 2, GG // 2) as i:
                for s in range(2):
                    one_hots(2 * i + s, s)
                    add_window(2 * i + s, s)

            dve.wait_ge(add_done, GG)
            with dve.If(dve.value_load(far[0:1, 0:1], min_val=0, max_val=1) > 0):
                with dve.Fori(0, GG) as g:
                    rel = relT[:, bass.ds(g, 1), :].rearrange("p a j -> p (a j)")
                    w = wT[:, bass.ds(g, 1), :].rearrange("p a j -> p (a j)")
                    dve.wait_ge(far_add, g * (NT * 3 + 1))
                    V.scalar_tensor_tensor(out=far_cols[:, 0, :], in0=rel, scalar=float(P) - 0.5, in1=w,
                                           op0=ALU.is_ge, op1=ALU.mult)
                    V.tensor_scalar(far_cols[:, 1, :], rel, base_all[:, bass.ds(g, 1)], None, ALU.add).then_inc(far_add, 1)
                    with dve.Fori(0, NT) as c:
                        at = g * (NT * 3 + 1) + c * 3
                        dve.wait_ge(far_add, at + 1)
                        V.tensor_tensor(oh_ring[:, 0], bc(iota_row[:, :].unsqueeze(1), [P, ET, P]),
                                        bc(far_cols[:, 1, :].unsqueeze(2), [P, ET, P]), ALU.is_equal).then_inc(far_add, 1)
                        dve.wait_ge(far_add, at + 2)
                        V.tensor_tensor(oh_ring[:, 0], oh_ring[:, 0], bc(far_cols[:, 0, :].unsqueeze(2), [P, ET, P]),
                                        ALU.mult).then_inc(far_oh, 1)
                        V.tensor_scalar(far_cols[:, 1, :], far_cols[:, 1, :], -float(P), None, ALU.add).then_inc(far_add, 1)
                        dve.wait_ge(far_mm, g * NT + c + 1)
                        block_c = aggT[:, bass.ds(c * P, P)]
                        V.tensor_tensor(block_c, block_c, ps[:, 0, 0:P], ALU.add).then_inc(far_add, 1)
                dve.wait_ge(far_add, GG * (NT * 3 + 1))
            V.memset(scrap[:, 3:4], 0.0).then_inc(agg_done, 1)

            def add_outputs(g, loop):
                dve.wait_ge(o_mm, g + 1)
                dve.wait_ge(ln_xn, NG + g)
                group = x_all[:, bass.ds(g * GT, GT), :].rearrange("p t d -> p (t d)")
                V.tensor_tensor(group, group, flat[:, 0:GT * D], ALU.add).then_inc(x2_rdy, 1)
                dve.wait_ge(x2_rdy, g + 1)
                apart(dve)
                loop.step(per, *[V.bn_stats(st6[:, t, :], x_all[:, bass.ds(g * GT + t, 1), :].rearrange("p a d -> p (a d)"))
                                 for t in range(GT)])
                apart(dve)
                for t in range(GT):
                    op = V.bn_aggr(mv[:, t, :], st6[:, t, :])
                op.then_inc(ln_mv, 1)

            def scales(g, loop):
                dve.wait_ge(ln_sd, NG + 1 + g)
                loop.step(per, V.reciprocal(rs[:, :], sd[:, :]))
                V.scalar_tensor_tensor(out=nm[:, :], in0=mv[:, :, 0], scalar=-1.0, in1=rs[:, :],
                                       op0=ALU.mult, op1=ALU.mult).then_inc(ln_rs, 1)

            def other_half(g):
                dve.wait_ge(t2_done, g + 1)
                dve.wait_ge(x_cp, g)
                dve.wait_ge(g_mm, g)
                V.tensor_copy(xnT[:, 1, :].rearrange("p (t n) -> p t n", n=P),
                              flat[:, 3072:3072 + GN].rearrange("p (t n) -> p t n", n=P)).then_inc(t2_ev, 1)

            def logits(g, loop):
                dve.wait_ge(g_mm, g + 1)
                h = ps[:, 7, 384:384 + GT * HK].rearrange("p (t c) -> p t c", c=HK)
                V.tensor_copy(tab[:, bass.ds(g * GT, GT), 4:RW].rearrange("p t (h k) -> p t h k", k=5)[:, :, :, 0:NE],
                              h.rearrange("p t (h k) -> p t h k", k=NE))
                loop.step(per, V.tensor_tensor(att_tmp[:, :, :], h, bc(att[:, 0:1, :], [P, GT, HK]), ALU.mult))
                loop.step(per, V.tensor_reduce(tab[:, bass.ds(g * GT, GT), 0:HEADS],
                                               att_tmp[:, :, :].rearrange("p t (h k) -> p t h k", k=NE), AX.X, ALU.add))
                loop.step(per, V.tensor_tensor(att_tmp[:, :, :], h, bc(att[:, 1:2, :], [P, GT, HK]), ALU.mult))
                V.tensor_reduce(adst[:, bass.ds(g * GT, GT), :],
                                att_tmp[:, :, :].rearrange("p t (h k) -> p t h k", k=NE), AX.X, ALU.add).then_inc(tab_rdy, 1)

            per = GT + 1
            loop = Loop(dv, chain[0], 0)
            add_outputs(0, loop)
            scales(0, loop)
            chain[0] += loop.n
            per = GT + 4
            with dve.Fori(1, NG) as g:
                loop = Loop(dv, chain[0] - per, g)
                add_outputs(g, loop)
                other_half(g - 1)
                scales(g, loop)
                logits(g - 1, loop)
                assert loop.n == per, loop.n
            chain[0] += (NG - 1) * per
            loop = Loop(dv, chain[0], 0)
            other_half(NG - 1)
            logits(NG - 1, loop)
            chain[0] += loop.n
            dve.wait_ge(tab_rdy, NG)

            dve.wait_ge(af_in, 16)
            dve.wait_ge(a_in, 16)
            step(V.tensor_copy(a_edge[:, 0, :], a_first[:, :]))
            step(V.tensor_scalar(not_start, pen[:, :], 0.0, None, ALU.is_equal))
            step(*[V.tensor_tensor_scan(a_edge[:, :, h], not_start, a_edge[:, :, h], 0.0, ALU.mult, ALU.add)
                   for h in range(HEADS)])
            step(V.memset(rec_out[:, 1, CH - 1, :], 0.0))

            def scan_chunk(c, s, i, steps, first):
                prev, cols = rec_out[:, 1 - s], bass.ds(c * CH, CH)
                dve.wait_ge(fgath[s], 16 * CH * (i + 1))
                steps(V.tensor_tensor(z1, rec_in[:, s, :, 0:HEADS], a_edge[:, cols, :], ALU.add))
                steps(V.scalar_tensor_tensor(out=z2, in0=z1, scalar=0.2, in1=z1, op0=ALU.mult, op1=ALU.max))
                if not first:
                    dve.wait_ge(rec_st[s], 16 * i)
                steps(*[V.tensor_tensor_scan(rec_out[:, s, :, h], pen[:, cols], z2[:, :, h], prev[:, CH - 1, h:h + 1],
                                             ALU.add, ALU.max) for h in range(HEADS)])
                m = rec_out[:, s, :, 0:HEADS]
                steps(V.tensor_tensor(dq[:, 0, 1:CH, :], m[:, 0:CH - 1, :], m[:, 1:CH, :], ALU.subtract),
                      V.tensor_tensor(dq[:, 0, 0, :], prev[:, CH - 1, 0:HEADS], m[:, 0, :], ALU.subtract),
                      V.tensor_tensor(dq[:, 1], z2, m, ALU.subtract))
                V.tensor_tensor(dq[:, 0], dq[:, 0], bc(pen[:, cols].unsqueeze(2), [P, CH, HEADS]), ALU.add).then_inc(q_rdy, 1)
                dve.wait_ge(ex_done, c + 1)
                V.tensor_tensor(vals, rec_in[:, s, :, HEADS:RW].rearrange("p t (h k) -> p t h k", k=5),
                                bc(dq[:, 1].unsqueeze(3), [P, CH, HEADS, 5]), ALU.mult).then_inc(in_free, 1)
                dve.wait_ge(in_free, c + 1)
                for h in range(HEADS):
                    for k in range(5):
                        n = HEADS + h * 5 + k
                        op = V.tensor_tensor_scan(rec_out[:, s, :, n], dq[:, 0, :, h], vals[:, :, h, k],
                                                  prev[:, CH - 1, n:n + 1], ALU.mult, ALU.add)
                op.then_inc(sc_done, 1)
                dve.wait_ge(sc_done, c + 1)

            per = 2 * 9
            with dve.Fori(0, NCH // 2) as i:
                loop = Loop(dv, chain[0], i)
                for s in range(2):
                    scan_chunk(2 * i + s, s, i, lambda *ops: loop.step(per, *ops), False)
                assert loop.n == per, loop.n
            chain[0] += NCH // 2 * per

            dve.wait_ge(dn_mm, NMB * NE * QB)
            tail = rec_out[:, 1, CH - 1, :]
            V.tensor_copy(last[:, 0, :].rearrange("p (h k) -> p h k", k=5), bc(tail[:, 0:HEADS].unsqueeze(2), [P, HEADS, 5]))
            V.tensor_copy(last[:, 1, :], tail[:, HEADS:RW])
            V.tensor_copy(last[:, 2, :], bc(ends[:, 0:1], [P, 20]))
            V.tensor_copy(last[:, 3, :], bc(ends[:, 1:2], [P, 20])).then_inc(last_rdy, 1)
            dve.wait_ge(last_tp, 1)
            step(V.tensor_copy(rowt[0:20, 0:4, :], ps[0:20, 4, :].rearrange("p (s c) -> p s c", c=P)))
            R = rowt[0:20]
            step(V.memset(R[:, 4, 0:1], 0.0),
                 V.tensor_tensor(R[:, 4, 1:P], R[:, 3, 0:P - 1], R[:, 2, 1:P], ALU.is_equal),
                 V.tensor_tensor(R[:, 7, :], R[:, 2, :], R[:, 3, :], ALU.is_equal))
            step(V.tensor_tensor(R[:, 7, :], R[:, 7, :], R[:, 4, :], ALU.mult))
            step(V.tensor_scalar(R[:, 8, :], R[:, 7, :], -1.0, BIG, ALU.add, ALU.mult))
            step(V.tensor_tensor_scan(R[:, 9, :], R[:, 8, :], R[:, 0, :], 0.0, ALU.add, ALU.max))
            step(V.memset(R[:, 5, 0:1], -BIG),
                 V.tensor_tensor(R[:, 5, 1:P], R[:, 9, 0:P - 1], R[:, 9, 1:P], ALU.subtract),
                 V.tensor_tensor(R[:, 6, :], R[:, 0, :], R[:, 9, :], ALU.subtract))
            V.tensor_tensor(R[:, 5, :], R[:, 5, :], R[:, 8, :], ALU.add).then_inc(row_q, 1)
            dve.wait_ge(row_ex, 1)
            step(V.tensor_tensor(R[:, 6, :], R[:, 6, :], R[:, 1, :], ALU.mult))
            step(V.tensor_tensor_scan(R[:, 1, :], R[:, 5, :], R[:, 6, :], 0.0, ALU.mult, ALU.add))
            step(V.memset(R[:, 0, 0:1], -BIG), V.memset(R[:, 10, 0:1], 0.0),
                 V.tensor_tensor(R[:, 0, 1:P], R[:, 9, 0:P - 1], R[:, 4, 1:P], ALU.mult),
                 V.tensor_tensor(R[:, 10, 1:P], R[:, 1, 0:P - 1], R[:, 4, 1:P], ALU.mult),
                 V.tensor_scalar(R[:, 8, :], R[:, 4, :], -1.0, BIG, ALU.add, ALU.mult))
            step(V.tensor_tensor(R[:, 9, :], R[:, 0, :], R[:, 8, :], ALU.add))
            step(V.memset(R[:, 5, :], 0.0), V.memset(R[:, 11, :], 0.0))
            step(V.tensor_copy(R[:, 5, 0:P - 1], R[:, 7, 1:P]),
                 V.tensor_scalar(R[:, 6, :], iota20(iota_row), float(TRASH), None, ALU.add))
            step(V.tensor_tensor(R[:, 5, 0:P - 1], R[:, 3, 0:P - 1], R[:, 2, 1:P], ALU.is_equal),
                 V.tensor_tensor(R[:, 11, :], R[:, 2, :], R[:, 3, :], ALU.is_equal))
            step(V.tensor_tensor(R[:, 5, :], R[:, 5, :], R[:, 11, :], ALU.mult))
            step(V.tensor_scalar(R[:, 5, :], R[:, 5, :], -1.0, 1.0, ALU.mult, ALU.add))
            step(V.tensor_tensor(R[:, 5, :], R[:, 5, :], R[:, 4, :], ALU.mult))
            step(V.tensor_tensor(R[:, 2, :], R[:, 2, :], R[:, 6, :], ALU.subtract))
            step(V.tensor_tensor(R[:, 2, :], R[:, 2, :], R[:, 5, :], ALU.mult))
            V.tensor_tensor(R[:, 11, :], R[:, 2, :], R[:, 6, :], ALU.add).then_inc(back_rdy, 1)
            dve.wait_ge(back_tp, 1)
            step(V.tensor_copy(carried, ps[:, 5, 0:60]))
            V.tensor_copy(carry_idx[:, :], carried[:, 40:41]).then_inc(c_rdy, 1)

            dve.wait_ge(r_in, 16 * NT)
            dve.wait_ge(c_in, 16)
            m_r, m_c, m_s = n_tmp[:, 0], n_tmp[:, 1], n_tmp[:, 2]
            hasb = bc(has[:, :].unsqueeze(2), [P, NT, HEADS])
            cm = node_c[:, :, 0:20].rearrange("p t (h k) -> p t h k", k=5)[:, :, :, 0]
            step(V.tensor_tensor(m_r, node_r[:, :, 0:HEADS], hasb, ALU.mult),
                 V.tensor_scalar(n_tmp[:, 3], hasb, -1.0, BIG, ALU.add, ALU.mult),
                 V.tensor_tensor(m_s, tab[:, :, 0:HEADS], adst[:, :, :], ALU.add),
                 V.tensor_copy(m_c, cm))
            step(V.tensor_tensor(m_r, m_r, n_tmp[:, 3], ALU.add),
                 V.scalar_tensor_tensor(out=n_tmp[:, 7], in0=m_s, scalar=0.2, in1=m_s, op0=ALU.mult, op1=ALU.max))
            step(V.tensor_tensor(n_tmp[:, 3], m_r, m_c, ALU.max))
            step(V.tensor_tensor(n_tmp[:, 3], n_tmp[:, 3], n_tmp[:, 7], ALU.max))
            step(V.tensor_tensor(n_tmp[:, 4], m_r, n_tmp[:, 3], ALU.subtract),
                 V.tensor_tensor(n_tmp[:, 5], m_c, n_tmp[:, 3], ALU.subtract))
            V.tensor_tensor(n_tmp[:, 6], n_tmp[:, 7], n_tmp[:, 3], ALU.subtract).then_inc(nd_q, 1)
            dve.wait_ge(nd_act, 1)

            def b5(ap):
                return bc(ap.unsqueeze(3), [P, NT, HEADS, 5])

            def hk(ap):
                return ap.rearrange("p t (h k) -> p t h k", k=5)

            r5, c5, t5 = hk(node_r[:, :, HEADS:RW]), hk(node_c[:, :, 20:40]), hk(tab[:, :, HEADS:RW])
            step(V.tensor_tensor(r5, r5, b5(n_tmp[:, 4]), ALU.mult), V.tensor_tensor(c5, c5, b5(n_tmp[:, 5]), ALU.mult),
                 V.tensor_tensor(s_tmp, t5, b5(n_tmp[:, 6]), ALU.mult))
            step(V.tensor_tensor(r5, r5, c5, ALU.add))
            step(V.tensor_tensor(s_tmp, s_tmp, r5, ALU.add))
            step(V.tensor_scalar(n_tmp[:, 0], s_tmp[:, :, :, 4], 1e-16, None, ALU.add))
            step(V.reciprocal(n_tmp[:, 1], n_tmp[:, 0]))
            agg, dev = n16[:, 0], n16[:, 1]
            agg4 = agg.rearrange("p t (h k) -> p t h k", k=NE)
            step(V.tensor_tensor(agg4, s_tmp[:, :, :, 0:NE], bc(n_tmp[:, 1].unsqueeze(3), [P, NT, HEADS, NE]), ALU.mult))
            step(V.tensor_tensor(agg, agg, bc(gat_par[:, 0:1, :], [P, NT, HK]), ALU.add))
            mean, var, sd2, rs2 = (n_tmp[:, 7, :, i] for i in (0, 1, 3, 2))
            step(V.tensor_reduce(mean, agg, AX.X, ALU.add))
            step(V.tensor_scalar(mean, mean, 1.0 / HK, None, ALU.mult))
            step(V.tensor_tensor(agg, agg, bc(mean.unsqueeze(2), [P, NT, HK]), ALU.subtract))
            step(V.tensor_tensor(dev, agg, agg, ALU.mult))
            step(V.tensor_reduce(var, dev, AX.X, ALU.add))
            V.tensor_scalar(var, var, 1.0 / HK, None, ALU.mult).then_inc(nd_q, 1)
            dve.wait_ge(nd_act, 2)
            step(V.reciprocal(rs2, sd2))
            step(V.tensor_tensor(agg, agg, bc(rs2.unsqueeze(2), [P, NT, HK]), ALU.mult))
            step(V.tensor_tensor(agg, agg, bc(gat_par[:, 1:2, :], [P, NT, HK]), ALU.mult))
            step(V.tensor_tensor(agg, agg, bc(gat_par[:, 2:3, :], [P, NT, HK]), ALU.add))
            score, rank, top = n_tmp[:, 0], n_tmp[:, 1], n_tmp[:, 7, :, 0]
            step(V.tensor_reduce(score, agg.rearrange("p t (h k) -> p t k h", k=NE), AX.X, ALU.add))
            step(V.tensor_scalar(score, score, 1.0 / HEADS, None, ALU.mult), V.memset(rank, 0.0))
            beats = n_tmp[:, 3, :, 0]
            for j in range(NE):
                for i in range(j + 1, NE):
                    step(V.tensor_tensor(beats, score[:, :, j], score[:, :, i], ALU.is_ge))
                    step(V.tensor_tensor(rank[:, :, i], rank[:, :, i], beats, ALU.add),
                         V.scalar_tensor_tensor(out=rank[:, :, j], in0=rank[:, :, j], scalar=1.0, in1=beats,
                                                op0=ALU.add, op1=ALU.subtract))
            step(V.tensor_reduce(top, score, AX.X, ALU.max))
            V.tensor_tensor(n_tmp[:, 2], score, bc(top.unsqueeze(2), [P, NT, NE]), ALU.subtract).then_inc(nd_q, 1)
            dve.wait_ge(nd_act, 3)
            step(V.tensor_scalar(rank, rank, 1.5, None, ALU.is_lt))
            step(V.tensor_tensor(n_tmp[:, 2], n_tmp[:, 2], rank, ALU.mult))
            step(V.tensor_reduce(top, n_tmp[:, 2], AX.X, ALU.add))
            step(V.reciprocal(mean_r(n_tmp), top))
            step(V.tensor_tensor(gates[:, :, :], n_tmp[:, 2], bc(mean_r(n_tmp).unsqueeze(2), [P, NT, NE]), ALU.mult))

            def combine(t, s, n, steps, first):
                dve.wait_ge(fy_in[s], 32 * (n + 1))
                if not first:
                    dve.wait_ge(fo_out[s], 16 * n)
                g4 = gates[:, bass.ds(t, 1), :].rearrange("p a e -> p (a e)")
                acc = x_in[:, s, :]
                for e in range(NE):
                    to = x_out[:, s, :] if e == NE - 1 else acc
                    op = V.scalar_tensor_tensor(out=to, in0=y_in[:, s, e, :], scalar=g4[:, e:e + 1], in1=acc,
                                                op0=ALU.mult, op1=ALU.add)
                    if e < NE - 1:
                        steps(op)
                op.then_inc(fo_rdy, 1)

            per = 2 * (NE - 1)
            with dve.Fori(0, NT // 2) as i:
                loop = Loop(dv, chain[0], i)
                for s in range(2):
                    combine(2 * i + s, s, i, lambda *ops: loop.step(per, *ops), False)
                assert loop.n == per
            chain[0] += NT // 2 * per
            combine(NT - 1, 0, NT // 2, step, False)


def iota20(iota_row):
    return iota_row[0:20, :]


def mean_r(n_tmp):
    return n_tmp[:, 7, :, 2]


def plan_steps():
    work = [("keys", 0, 0)]
    cur = 0
    for k, j in STAGES:
        if (j >= FLOG and j == k - 1) or (j == FLOG - 1 and k > FLOG):
            work.append(("turn", 0, cur))
        work.append(("stage", k, j))
        cur = 1 - cur
    work += [("hist", c, 0) for c in range(FC // HIST_CH)]
    work += [("bias", g, 0) for g in range(NG)]
    work += [("cum", 0, 0), ("marks", 0, 0)]
    steps, room = [[]], BUDGET
    for kind, a, b in work:
        took = {"keys": 8.0, "bias": 2.5, "turn": 4.0, "stage": 1.4, "hist": 3.4, "cum": 5.0, "marks": 8.0}[kind]
        if took > room and steps[-1]:
            steps.append([])
            room = BUDGET
        steps[-1].append((kind, a, b))
        room -= took
    if len(steps) % 2:
        steps.append([])
    assert len(steps) < GG
    return steps


STEPS = plan_steps()


DEBUG = ()


def kernel(x, src, dst, edge_weight, L0_gnn_Wp, L0_gnn_bp, L0_gnn_W1, L0_gnn_b1, L0_gnn_W2, L0_gnn_b2, L0_ffn_W_gat,
           L0_ffn_att_src, L0_ffn_att_dst, L0_ffn_b_gat, L0_ffn_ln_gamma, L0_ffn_ln_beta, L0_ffn_W1, L0_ffn_b1,
           L0_ffn_W2, L0_ffn_b2, L0_ffn_edge_index):
    import numpy as np
    import concourse.bacc as bacc
    from concourse.bass_utils import run_bass_kernel_spmd as run

    nc = bacc.Bacc("TRN2", target_bir_lowering=False, num_devices=1)
    tail = GG * EGN - EG
    pad_e = lambda a: np.pad(np.asarray(a), (0, tail), mode="edge").reshape(GG, EGN)
    edges = np.asarray(L0_ffn_edge_index)
    arrays = {
        "x": np.pad(np.asarray(x), ((0, NP - N), (0, 0))),
        "gsrc": pad_e(src), "gdst": pad_e(dst),
        "gw": np.pad(np.asarray(edge_weight), (0, tail)).reshape(GG, EGN),
        "WpT": np.asarray(L0_gnn_Wp).T, "bp": L0_gnn_bp, "W1T": np.asarray(L0_gnn_W1).T, "b1": L0_gnn_b1,
        "W2T": np.asarray(L0_gnn_W2).T, "b2": L0_gnn_b2, "Wgat": L0_ffn_W_gat, "att_src": L0_ffn_att_src,
        "att_dst": L0_ffn_att_dst, "b_gat": L0_ffn_b_gat, "ln_gamma": L0_ffn_ln_gamma, "ln_beta": L0_ffn_ln_beta,
        "mW1": L0_ffn_W1, "mb1": np.asarray(L0_ffn_b1).reshape(NE * FB, P).T, "mW2": L0_ffn_W2,
        "mb2": np.asarray(L0_ffn_b2).reshape(1, NE * D),
        "fsrc": edges[0].reshape(P, FC), "fdst": edges[1].reshape(P, FC),
    }
    arrays = {k: np.ascontiguousarray(v) for k, v in arrays.items()}
    args = [nc.dram_tensor(k, v.shape, mybir.dt.from_np(v.dtype), kind="ExternalInput").ap() for k, v in arrays.items()]
    out = nc.dram_tensor("out", (N, D), F32, kind="ExternalOutput").ap()
    gnn_ffn(nc, *args, out, DEBUG)
    r = run(nc, [arrays], core_ids=[0])
    return r.results[0]["out"]
```

```python
from contextlib import ExitStack

import concourse.bass as bass
from concourse import mybir

F32 = mybir.dt.float32
I32 = mybir.dt.int32
BF16 = mybir.dt.bfloat16
ALU = mybir.AluOpType
ACT = mybir.ActivationFunctionType
AX = mybir.AxisListType

P = 128
N = 6250
NT = 49
NP = NT * P
D = 256
KD = D // P
GT = 7
NG = NT // GT
X_FIRST = 3
GN = GT * P
HN = GN // 2
EG = 106250
ET = 8
EGN = ET * P
GG = 104
EF = 131072
FC = EF // P
FLOG = 10
ELOG = 17
DST_BITS = 13
CH = 32
NCH = FC // CH
HEADS = 4
NE = 4
HK = HEADS * NE
RW = 24
HID = 512
FB = HID // P
MB = 448
NMB = NP // MB
MQ = 112
QB = MB // MQ
YT = 4
YS = 4
YL = NT // (YT * YS)
CR = 40
TRASH = 8192
LN_EPS = 1e-5
BIG = 1e30
KEY_TOP = 0x40000000

STAGES = [(k, j) for k in range(1, ELOG + 1) for j in range(k - 1, -1, -1)]
BUDGET = 7.0
HIST_CH = 16


def gnn_ffn(nc, x, gsrc, gdst, gw, WpT, bp, W1T, b1, W2T, b2, Wgat, att_src, att_dst, b_gat,
            ln_gamma, ln_beta, mW1, mb1, mW2, mb2, fsrc, fdst, out, debug):
    ctx = ExitStack()
    with ctx:
        def sb(name, shape, dt=F32):
            return ctx.enter_context(nc.sbuf_tensor(name, shape, dt))

        def sem(name):
            return ctx.enter_context(nc.semaphore(name))

        def dram(name, shape, dt=F32):
            kind = "ExternalOutput" if debug and name in debug else "Internal"
            return nc.dram_tensor(name, shape, dt, kind=kind).ap()

        hp_tab = dram("hp_tab", (NP, P))
        x2_tab = dram("x2_tab", (NP, D))
        src_tab = dram("src_tab", (NP, RW))
        adst_tab = dram("adst_tab", (TRASH, HEADS))
        adst_edge = dram("adst_edge", (EF + NP, HEADS))
        rec_tab = dram("rec_tab", (EF, RW))
        carry_tab = dram("carry_tab", (TRASH + P, CR))
        y_tab = dram("y_tab", (NP, NE * D))
        key_tab = dram("key_tab", (EF // (2 * CH), 2 * CH))

        big_x = sb("big_x", [P, NT * D])
        big_t = sb("big_t", [P, KD * NP])
        big_h = sb("big_h", [P, 2 * NP + P])
        ring = sb("ring", [P, 4 * EGN])

        def carve(whole, at, n):
            return whole[:, at:at + n]

        x_all = big_x[:, :].rearrange("p (t d) -> p t d", d=D)
        hT = big_h[:, 0:NP]
        aggT = big_h[:, NP:2 * NP + P]
        xn2T = big_t[:, :].rearrange("p (k n) -> p k n", k=KD)
        xn = ring[:, 0:GT * D].rearrange("p (t d) -> p t d", d=D)
        xn_s = [ring[:, i * GT * D:(i + 1) * GT * D].rearrange("p (t d) -> p t d", d=D) for i in range(2)]
        featT = ring[0:HK, GT * D:GT * D + GN]
        g_ring = ring[:, 0:2 * EGN].rearrange("p (h j f) -> p h j f", h=2, j=ET)
        oh_ring = ring[:, 2 * EGN:4 * EGN].rearrange("p (h j f) -> p h j f", h=2, j=ET)
        xnT = carve(big_t, 0, GT * D).rearrange("p (k n) -> p k n", k=KD)
        mv_x = carve(big_t, 10 * FC, 2 * NT).rearrange("p (t s) -> p t s", s=2)
        sd_x, rs_x = (carve(big_t, 10 * FC + i * NT, NT) for i in (2, 3))
        keys = [carve(big_t, i * FC, FC) for i in range(2)]
        e_src = carve(big_t, 2 * FC, FC).bitcast(I32)
        e_dst = carve(big_t, 3 * FC, FC).bitcast(I32)
        g_src = carve(big_t, 4 * FC, EGN).bitcast(I32)
        g_dst = carve(big_t, 5 * FC, EGN).bitcast(I32)
        g_w = carve(big_t, 6 * FC, EGN)
        g_srcf = carve(big_t, 7 * FC, EGN)
        g_dstf = carve(big_t, 8 * FC, EGN)
        half_i = carve(big_t, 10 * FC, FC).bitcast(I32)
        lo_bf = carve(big_t, 11 * FC, FC // 2).bitcast(BF16)
        hi_bf = carve(big_t, 11 * FC + FC // 2, FC // 2).bitcast(BF16)
        oh_lo = carve(big_t, 4 * FC, HIST_CH * P).bitcast(BF16).rearrange("p (s t c) -> p s t c", s=2, c=P)
        oh_hi = carve(big_t, 8 * FC, HIST_CH * 64).bitcast(BF16).rearrange("p (s t c) -> p s t c", s=2, c=64)
        b12 = carve(big_t, 6 * FC, 2 * D).rearrange("p (s d) -> p s d", s=2)
        s_dst = carve(big_t, 4 * FC, FC)
        was_equal = carve(big_t, 5 * FC, FC)
        w1m = carve(big_x, 0, 4096).rearrange("p (e k f) -> p e k f", e=NE, k=KD)
        w2m = carve(big_x, 4096, 4096).rearrange("p (e f d) -> p e f d", e=NE, f=FB)
        hid = carve(big_x, 8192, 2 * FB * MB).rearrange("p (s f n) -> p s f n", s=2, f=FB)
        b2_parts = carve(big_x, 8192 + 2 * FB * MB, NE * D // 2).bitcast(BF16)[0:3].rearrange("p (e d) -> p e d", e=NE)
        a_edge = carve(big_h, 0, HEADS * FC).rearrange("p (t h) -> p t h", h=HEADS)
        at = HEADS * FC
        rec_in = carve(big_h, at, 2 * CH * RW).rearrange("p (s t c) -> p s t c", s=2, c=RW)
        at += 2 * CH * RW
        rec_out = carve(big_h, at, 2 * CH * RW).rearrange("p (s t c) -> p s t c", s=2, c=RW)
        at += 2 * CH * RW
        b2_rest = carve(big_h, at - 2 * CH * RW, NE * D)[0:3].rearrange("p (e d) -> p e d", e=NE)
        b2_part = carve(big_h, at - 2 * CH * RW + NE * D, NE * D // 2).bitcast(BF16)[0:3].rearrange("p (e d) -> p e d", e=NE)
        z1 = carve(big_h, at, CH * 4).rearrange("p (t h) -> p t h", h=HEADS)
        at += CH * 4
        z2 = carve(big_h, at, CH * 4).rearrange("p (t h) -> p t h", h=HEADS)
        at += CH * 4
        dq = carve(big_h, at, CH * 8).rearrange("p (q t h) -> p q t h", q=2, h=HEADS)
        at += CH * 8
        vals = carve(big_h, at, CH * 20).rearrange("p (t h k) -> p t h k", h=HEADS, k=5)
        at += CH * 20
        not_start = carve(big_h, at, FC)
        y_sb = ring[0:MQ, 0:4 * NE * D].rearrange("p (q e d) -> p q e d", q=QB, e=NE)
        at += FC
        node_r = carve(big_h, at, NT * RW).rearrange("p (t c) -> p t c", c=RW)
        at += NT * RW
        node_c = carve(big_h, at, NT * CR).rearrange("p (t c) -> p t c", c=CR)
        assert at + NT * CR <= 2 * NP + P
        y_in = [carve(big_t, i * YT * NE * D, YT * NE * D) for i in range(3)] + [ring[:, :]]
        y_in = [y.rearrange("p (t e d) -> p t e d", t=YT, e=NE) for y in y_in]
        at = 0
        last = carve(big_h, at, 4 * 20).rearrange("p (s c) -> p s c", c=20)
        at += 80
        carried = carve(big_h, at, 60)
        at += 60
        rowt = carve(big_h, at, 12 * P).rearrange("p (s c) -> p s c", c=P)
        at += 12 * P
        s_tmp = carve(big_h, at, NT * 20).rearrange("p (t h k) -> p t h k", h=HEADS, k=5)
        at += NT * 20
        n_tmp = carve(big_h, at, 8 * NT * 4).rearrange("p (s t h) -> p s t h", s=8, h=4)
        at += 8 * NT * 4
        n16 = carve(big_h, at, 2 * NT * HK).rearrange("p (s t c) -> p s t c", s=2, c=HK)
        at += 2 * NT * HK
        gates = carve(big_h, at, NT * NE).rearrange("p (t e) -> p t e", e=NE)

        ident = sb("ident", [P, P])
        lower = sb("lower", [P, P])
        ones = sb("ones", [P, P])
        iota_row = sb("iota_row", [P, P])
        iota_bf = sb("iota_bf", [P, P], BF16)
        part_i = sb("part_i", [P, 1], I32)
        sgn_i = sb("sgn_i", [P, 8], I32)
        sgn = sb("sgn", [P, 8])
        eps = sb("eps", [P, 1])
        zeros = sb("zeros", [P, 256])
        no_edge = sb("no_edge", [P, CR])
        wp_sb = sb("wp_sb", [P, KD, P])
        bp_sb = sb("bp_sb", [P, 1])
        w1_sb = sb("w1_sb", [P, D])
        w2_sb = sb("w2_sb", [P, D])
        wg_sb = sb("wg_sb", [P, KD, HK])
        att = sb("att", [P, 2, HK])
        gat_par = sb("gat_par", [P, 3, HK])
        b1m = sb("b1m", [P, NE * FB])
        b2m = sb("b2m", [3, NE, D])
        ones_bf = sb("ones_bf", [3, MQ], BF16)

        g_cols = sb("g_cols", [P, 3, GG * ET])
        srcT = g_cols[:, 0, :].bitcast(I32).rearrange("p (g j) -> p g j", j=ET)
        relT = g_cols[:, 1, :].rearrange("p (g j) -> p g j", j=ET)
        wT = g_cols[:, 2, :].rearrange("p (g j) -> p g j", j=ET)
        h_now = carve(big_t, 9 * FC, GN)
        h_now2 = g_cols[:, :, :].rearrange("p a n -> p (a n)")[:, 0:GN]
        att_tmp = g_cols[:, :, :].rearrange("p a n -> p (a n)")[:, GN:GN + GT * HK].rearrange("p (t c) -> p t c", c=HK)
        spread = sb("spread", [P, 4])
        base_row = sb("base_row", [1, 2, GG], I32)
        base_f = sb("base_f", [1, GG])
        base_all = sb("base_all", [P, GG])
        far = sb("far", [1, 1], I32)
        far_cols = sb("far_cols", [P, 2, ET])
        g_idx = sb("g_idx", [P, 2, ET], I32)

        s_src = sb("s_src", [P, FC], I32)
        ends = sb("ends", [P, 2])
        row_len = sb("row_len", [P, 4])
        fetch_idx = sb("fetch_idx", [P, NCH // 2], I32)
        row_i = sb("row_i", [P, 2], I32)
        pen = sb("pen", [P, FC])
        f_idx = sb("f_idx", [P, 2, CH], I32)
        first_idx = sb("first_idx", [P, 1], I32)
        cum = sb("cum", [P, 6, 64])
        has = sb("has", [P, NT])
        e_idx = sb("e_idx", [P, NT], I32)
        st_idx = sb("st_idx", [P, NT], I32)
        carry_idx = sb("carry_idx", [P, 1], I32)
        a_first = sb("a_first", [P, HEADS])

        st6 = sb("st6", [P, GT, 6])
        mv = sb("mv", [P, GT, 2])
        sd = sb("sd", [P, GT])
        rs = sb("rs", [P, GT])
        nm = sb("nm", [P, GT])
        hp_sb = sb("hp_sb", [P, GT, P])
        iota_i = hp_sb[:, 0, :].bitcast(I32)
        tab = sb("tab", [P, NT, RW])
        adst = sb("adst", [P, NT, HEADS])

        ps = ctx.enter_context(nc.psum_tensor("ps", [P, 8, 512], F32))
        flat = ps[:, :, :].rearrange("p b n -> p (b n)")

        x_ld = [sem(f"x_ld{i}") for i in range(2)]
        clear, hT_cp = sem("clear"), sem("hT_cp")
        par_in, ge_in, fe_in = sem("par_in"), sem("ge_in"), sem("fe_in")
        pool_c, dv, consts = sem("pool_c"), sem("dv"), sem("consts")
        ln_mv, ln_sd, ln_xn = sem("ln_mv"), sem("ln_sd"), sem("ln_xn")
        tp_done, tp_ev = sem("tp_done"), sem("tp_ev")
        h_mm, h_ev, hb_mm, hb_ev, hp_out = sem("h_mm"), sem("h_ev"), sem("hb_mm"), sem("hb_ev"), sem("hp_out")
        rel_rdy, ge_tp, ge_ev = sem("rel_rdy"), sem("ge_tp"), sem("ge_ev")
        far_idx, far_gath, far_oh, far_mm, far_add, agg_done = (sem("far_idx"), sem("far_gath"), sem("far_oh"),
                                                                sem("far_mm"), sem("far_add"), sem("agg_done"))
        idx_cp, oh_rdy, mm_done, add_done = sem("idx_cp"), sem("oh_rdy"), sem("mm_done"), sem("add_done")
        gath = [sem(f"gath{i}") for i in range(2)]
        key_rdy, key_tp = sem("key_rdy"), sem("key_tp")
        key_end, key_st, len_mm, len_rdy, fetched = (sem("key_end"), sem("key_st"), sem("len_mm"), sem("len_rdy"),
                                                     sem("fetched"))
        chunk_dv = sem("chunk_dv")
        hist_rdy, hist_mm, cum_rdy, cum_mm = sem("hist_rdy"), sem("hist_mm"), sem("cum_rdy"), sem("cum_mm")
        ends_rdy, sorted_s = sem("ends_rdy"), sem("sorted_s")
        sq_done, o_mm, x2_rdy, x2_out = sem("sq_done"), sem("o_mm"), sem("x2_rdy"), sem("x2_out")
        t2_done, t2_ev, g_mm, tab_rdy, tab_out = sem("t2_done"), sem("t2_ev"), sem("g_mm"), sem("tab_rdy"), sem("tab_out")
        zero_rdy, zero_out, a_scat, a_in, af_in = sem("zero_rdy"), sem("zero_out"), sem("a_scat"), sem("a_in"), sem("af_in")
        fidx_cp = sem("fidx_cp")
        feat_tp = sem("feat_tp")
        bias_in, ln_rs, h_cp, feat_ev = sem("bias_in"), sem("ln_rs"), sem("h_cp"), sem("feat_ev")
        fgath = [sem(f"fgath{i}") for i in range(2)]
        q_rdy, ex_done, sc_done, in_free = sem("q_rdy"), sem("ex_done"), sem("sc_done"), sem("in_free")
        rec_st = [sem(f"rec_st{i}") for i in range(2)]
        mw_in, up_mm, gelu_done, dn_mm, y_ev, y_st = (sem("mw_in"), sem("up_mm"), sem("gelu_done"), sem("dn_mm"),
                                                      sem("y_ev"), sem("y_st"))
        r_in, last_rdy, last_tp, row_q, row_ex, back_rdy, back_tp = (
            sem("r_in"), sem("last_rdy"), sem("last_tp"), sem("row_q"), sem("row_ex"), sem("back_rdy"), sem("back_tp"))
        b2_rdy = sem("b2_rdy")
        c_rdy, c_scat, c_in, nd_q, nd_act = sem("c_rdy"), sem("c_scat"), sem("c_in"), sem("nd_q"), sem("nd_act")
        fy_in = [sem(f"fy_in{i}") for i in range(YS)]
        fx_in, fo_rdy, fo_out = sem("fx_in"), sem("fo_rdy"), sem("fo_out")

        scrap = sb("scrap", [P, 4])

        def apart(eng):
            if eng.engine == nc.gpsimd.engine:
                eng.tensor_tensor(scrap[:, 0:1], ones[:, 0:1], ones[:, 0:1], ALU.mult)
            else:
                eng.memset(scrap[:, 1:2], 0.0)

        def after(eng, sem_, n):
            if not isinstance(n, int) or n > 0:
                eng.wait_ge(sem_, n)

        block = ctx.enter_context(nc.Block())

        def row_of(ap):
            return ap.rearrange("(a n) -> a n", a=1)

        N_PAR = 12

        @block.sync
        def _(sp):
            sp.dma_start(g_src[0:GG, :], gsrc).then_inc(ge_in, 16)
            sp.dma_start(g_dst[0:GG, :], gdst).then_inc(ge_in, 16)
            sp.dma_start(g_w[0:GG, :], gw).then_inc(ge_in, 16)
            for g in range(NG):
                sp.dma_start(x_all[:, g * GT:(g + 1) * GT, :],
                             x[g * GN:(g + 1) * GN, :].rearrange("(t p) d -> p t d", p=P)
                             ).then_inc(x_ld[0 if g < X_FIRST else 1], 16)
            sp.dma_start(wp_sb[:, :, :], WpT.rearrange("(k p) f -> p k f", p=P)).then_inc(par_in, 16)
            sp.dma_start(bp_sb[:, :], bp.rearrange("(p a) -> p a", a=1)).then_inc(par_in, 16)
            sp.dma_start(w1_sb[:, :], W1T).then_inc(par_in, 16)
            sp.dma_start(w2_sb[:, :], W2T).then_inc(par_in, 16)
            sp.dma_start(wg_sb[:, :, :], Wgat.rearrange("(k p) f -> p k f", p=P)).then_inc(par_in, 16)
            sp.dma_start(att[:, 0, :], att_src.rearrange("h e -> (h e)").partition_broadcast(P)).then_inc(par_in, 16)
            sp.dma_start(att[:, 1, :], att_dst.rearrange("h e -> (h e)").partition_broadcast(P)).then_inc(par_in, 16)
            sp.dma_start(gat_par[:, 0, :], b_gat.partition_broadcast(P)).then_inc(par_in, 16)
            sp.dma_start(gat_par[:, 1, :], ln_gamma.partition_broadcast(P)).then_inc(par_in, 16)
            sp.dma_start(gat_par[:, 2, :], ln_beta.partition_broadcast(P)).then_inc(par_in, 16)
            sp.dma_start(b1m[:, :], mb1).then_inc(par_in, 16)
            sp.dma_start(b2m[:, :, :].rearrange("p e d -> p (e d)"), mb2.partition_broadcast(3)).then_inc(par_in, 16)
            sp.dma_start(e_src, fsrc).then_inc(fe_in, 16)
            sp.dma_start(e_dst, fdst).then_inc(fe_in, 16)
            sp.wait_ge(zero_rdy, 1)
            zero_reps = EF * HEADS // P // 256
            sp.dma_start(adst_edge[0:EF, :].rearrange("(p r t) h -> p r (t h)", p=P, r=zero_reps),
                         zeros[:, :].unsqueeze(1).broadcast_to([P, zero_reps, 256])).then_inc(zero_out, 16)
            sp.dma_start(adst_tab[NP:TRASH, :].rearrange("(p t) h -> p (t h)", p=P),
                         zeros[:, 0:(TRASH - NP) * HEADS // P]).then_inc(zero_out, 16)
            sp.dma_start(carry_tab[0:NP, :].rearrange("(p t) c -> p t c", p=P),
                         no_edge[:, :].unsqueeze(1).broadcast_to([P, NT, CR])).then_inc(zero_out, 16)
            sp.wait_ge(ge_ev, 3)
            sp.dma_start(b12[:, 0, :], b1.partition_broadcast(P)).then_inc(bias_in, 16)
            sp.dma_start(b12[:, 1, :], b2.partition_broadcast(P)).then_inc(bias_in, 16)
            with sp.Fori(0, NG) as g:
                sp.wait_ge(hb_ev, g + 1)
                sp.dma_start(hp_tab[bass.ds(g * GN, GN), :].rearrange("(t p) f -> p t f", p=P),
                             hp_sb[:, :, :]).then_inc(hp_out, 16)
            sp.wait_ge(key_end, 1)
            sp.dma_start(key_tab.rearrange("(p t) c -> p (t c)", p=P), keys[len(STAGES) % 2]).then_inc(key_st, 16)
            with sp.Fori(0, NG) as g:
                rows = bass.ds(g * GN, GN)
                tiles = bass.ds(g * GT, GT)
                sp.wait_ge(x2_rdy, g + 1)
                sp.dma_start(x2_tab[rows, :].rearrange("(t p) d -> p t d", p=P), x_all[:, tiles, :]).then_inc(x2_out, 16)
                sp.wait_ge(tab_rdy, g + 1)
                sp.dma_start(src_tab[rows, :].rearrange("(t p) c -> p t c", p=P), tab[:, tiles, :]).then_inc(tab_out, 16)
                sp.dma_start(adst_tab[rows, :].rearrange("(t p) c -> p t c", p=P), adst[:, tiles, :]).then_inc(tab_out, 16)
            sp.wait_ge(x2_out, 16 * NG)
            sp.dma_start(w1m, mW1.rearrange("e (k p) f -> p e k f", p=P)).then_inc(mw_in, 16)
            sp.dma_start(w2m, mW2.rearrange("e (f p) d -> p e f d", p=P)).then_inc(mw_in, 16)
            sp.wait_ge(a_scat, 16 * NT)
            sp.dma_start(a_edge, adst_edge[0:EF, :].rearrange("(p t) h -> p t h", p=P)).then_inc(a_in, 16)
            rec_v = rec_tab.rearrange("(p t) c -> p (t c)", p=P)
            y_v = y_tab.rearrange("(b q p) n -> b p q n", q=QB, p=MQ)

            def store_records(i, s):
                sp.wait_ge(sc_done, 2 * i + s + 1)
                sp.dma_start(rec_v[:, bass.ds((2 * i + s) * CH * RW, CH * RW)],
                             rec_out[:, s, :, :].rearrange("p t c -> p (t c)")).then_inc(rec_st[s], 16)

            pairs = sp.value_load(row_i[0:1, 0:1], min_val=1, max_val=NCH // 2)
            with sp.Fori(0, NCH // 2) as i:
                with sp.If(pairs > i):
                    for s in range(2):
                        store_records(i, s)
                with sp.If(pairs <= i):
                    for s in range(2):
                        sp.dma_start(rec_v[:, bass.ds((2 * i + s) * CH * RW, CH * RW)].rearrange("p (r n) -> p r n", n=256),
                                     zeros[:, :].unsqueeze(1).broadcast_to([P, CH * RW // 256, 256])
                                     ).then_inc(rec_st[s], 16)
            sp.wait_ge(dn_mm, NMB * NE * QB)
            sp.dma_start(x_all, x2_tab.rearrange("(t p) d -> p t d", p=P)).then_inc(fx_in, 16)

            def load_y(t, n, s):
                sp.dma_start(y_in[s][:, 0:n].rearrange("p t e d -> p t (e d)"),
                             y_tab[bass.ds(t * P, n * P), :].rearrange("(t p) n -> p t n", p=P)).then_inc(fy_in[s], 16)

            sp.wait_ge(y_st, 16 * NMB)
            load_y(0, YT, 0)
            sp.wait_ge(c_scat, 16)
            sp.dma_start(node_c, carry_tab[0:NP, :].rearrange("(t p) c -> p t c", p=P)).then_inc(c_in, 16)

            for s in range(1, YS):
                load_y(s * YT, YT, s)
            with sp.Fori(1, YL) as i:
                for s in range(YS):
                    sp.wait_ge(fo_rdy, YS * i + s - YS + 1)
                    load_y((YS * i + s) * YT, YT, s)
            sp.wait_ge(fo_rdy, YS * (YL - 1) + 1)
            load_y(YL * YS * YT, 1, 0)
            sp.wait_ge(fo_out, 16 * (YL * YS + 1))

        @block.gpsimd
        def _(pool):
            pool.memset(ident[:, :], 0.0).then_inc(pool_c, 1)
            pool.memset(lower[:, :], 1.0).then_inc(pool_c, 1)
            pool.iota(iota_i, [[1, P]], base=0, channel_multiplier=0).then_inc(pool_c, 1)
            pool.iota(part_i[:, :], [[0, 1]], base=0, channel_multiplier=1).then_inc(pool_c, 1)
            pool.wait_ge(pool_c, 4)
            pool.affine_select(out=ident[:, :], in_=ident[:, :], compare_op=ALU.not_equal, fill=1.0,
                               base=0, pattern=[[-1, P]], channel_multiplier=1).then_inc(pool_c, 1)
            pool.affine_select(out=lower[:, :], in_=lower[:, :], compare_op=ALU.is_gt, fill=0.0,
                               base=0, pattern=[[1, P]], channel_multiplier=-1).then_inc(pool_c, 1)

            pool.memset(aggT, 0.0).then_inc(clear, 1)
            pool.memset(tab[:, :, :], 1.0).then_inc(clear, 1)
            with pool.Fori(0, NG) as g:
                pool.wait_ge(h_ev, g + 1)
                pool.tensor_copy(hT[:, bass.ds(g * GN, GN)], h_now).then_inc(hT_cp, 1)

            def gather_group(g, s, n):
                pool.tensor_copy(g_idx[:, s, :], srcT[:, bass.ds(g, 1), :].rearrange("p a j -> p (a j)")).then_inc(idx_cp, 1)
                pool.wait_ge(idx_cp, g + 1)
                apart(pool)
                for j in range(ET):
                    pool.indirect_dma_start(out=g_ring[:, s, j, :], out_offset=None, in_=hp_tab,
                                            in_offset=bass.IndirectOffsetOnAxis(ap=g_idx[:, s, j:j + 1], axis=0)
                                            ).then_inc(gath[s], 16)

            pool.wait_ge(consts, 1)
            pool.wait_ge(ge_ev, 3)
            pool.wait_ge(hp_out, 16 * NG)
            for g in range(2):
                gather_group(g, g, 0)
            with pool.Fori(1, FETCH) as i:
                for s in range(2):
                    pool.wait_ge(mm_done, 2 * i + s - 1)
                    gather_group(2 * i + s, s, i)
            pool.wait_ge(key_st, 16)
            pool.wait_ge(len_rdy, 1)
            for k in range(NCH // 2):
                pool.indirect_dma_start(out=keys[1 - len(STAGES) % 2][:, 2 * CH * k:2 * CH * (k + 1)], out_offset=None,
                                        in_=key_tab, in_offset=bass.IndirectOffsetOnAxis(ap=fetch_idx[:, k:k + 1], axis=0)
                                        ).then_inc(fetched, 16)
            with pool.Fori(FETCH, GG // 2) as i:
                for s in range(2):
                    pool.wait_ge(mm_done, 2 * i + s - 1)
                    gather_group(2 * i + s, s, i)

            with pool.If(pool.value_load(far[0:1, 0:1], min_val=0, max_val=1) > 0):
                pool.wait_ge(mm_done, GG)
                with pool.Fori(0, GG) as g:
                    pool.wait_ge(far_mm, g * NT)
                    pool.tensor_copy(g_idx[:, 0, :], srcT[:, bass.ds(g, 1), :].rearrange("p a j -> p (a j)")).then_inc(far_idx, 1)
                    pool.wait_ge(far_idx, g + 1)
                    apart(pool)
                    for j in range(ET):
                        pool.indirect_dma_start(out=g_ring[:, 0, j, :], out_offset=None, in_=hp_tab,
                                                in_offset=bass.IndirectOffsetOnAxis(ap=g_idx[:, 0, j:j + 1], axis=0)
                                                ).then_inc(far_gath, 16)

            def copy_h(g):
                after(pool, o_mm, g)
                pool.tensor_copy(h_now2, hT[:, bass.ds(g * GN, GN)]).then_inc(h_cp, 1)

            def scatter_logits(g):
                pool.wait_ge(tab_rdy, g + 1)
                for t in range(g * GT, (g + 1) * GT):
                    pool.indirect_dma_start(out=adst_edge, out_offset=bass.IndirectOffsetOnAxis(ap=st_idx[:, t:t + 1], axis=0),
                                            in_=adst[:, t, :], in_offset=None).then_inc(a_scat, 16)

            pool.wait_ge(agg_done, 1)
            pool.wait_ge(sorted_s, 1)
            pool.wait_ge(zero_out, 48)
            for g in range(NG):
                copy_h(g)
                if g >= 3:
                    scatter_logits(g - 3)
            for g in range(NG - 3, NG):
                scatter_logits(g)

            def gather_chunk(c, s):
                pool.tensor_copy(f_idx[:, s, :], s_src[:, bass.ds(c * CH, CH)]).then_inc(fidx_cp, 1)
                pool.wait_ge(fidx_cp, c + 1)
                apart(pool)
                for j in range(CH):
                    pool.indirect_dma_start(out=rec_in[:, s, j, :], out_offset=None, in_=src_tab,
                                            in_offset=bass.IndirectOffsetOnAxis(ap=f_idx[:, s, j:j + 1], axis=0)
                                            ).then_inc(fgath[s], 16)

            pool.wait_ge(tab_out, 32 * NG)
            pool.indirect_dma_start(out=a_first[:, :], out_offset=None, in_=adst_tab,
                                    in_offset=bass.IndirectOffsetOnAxis(ap=first_idx[:, :], axis=0)).then_inc(af_in, 16)
            for c in range(2):
                gather_chunk(c, c)
            pairs = pool.value_load(row_i[0:1, 0:1], min_val=1, max_val=NCH // 2)
            with pool.Fori(1, NCH // 2) as i:
                with pool.If(pairs > i):
                    for s in range(2):
                        pool.wait_ge(in_free, 2 * i + s - 1)
                        gather_chunk(2 * i + s, s)

            pool.wait_ge(rec_st[0], 16 * NCH // 2)
            pool.wait_ge(rec_st[1], 16 * NCH // 2)
            for t in range(NT):
                pool.indirect_dma_start(out=node_r[:, t, :], out_offset=None, in_=rec_tab,
                                        in_offset=bass.IndirectOffsetOnAxis(ap=e_idx[:, t:t + 1], axis=0)
                                        ).then_inc(r_in, 16)
                if t == NT // 3:
                    pool.wait_ge(c_rdy, 1)
                    pool.indirect_dma_start(out=carry_tab, out_offset=bass.IndirectOffsetOnAxis(ap=carry_idx[:, :], axis=0),
                                            in_=carried[:, 0:CR], in_offset=None).then_inc(c_scat, 16)

        @block.scalar
        def _(act):
            act.wait_ge(consts, 1)
            act.wait_ge(par_in, 16 * N_PAR)
            act.wait_ge(ln_mv, 1)
            nc.scalar.activation(sd_x, mv_x[:, :, 1], ACT.Sqrt, bias=eps[:, :]).then_inc(ln_sd, 1)

            def keep_rows(g):
                act.wait_ge(tp_done, g + 1)
                after(act, h_mm, g)
                nc.scalar.activation(xnT[:, 0, :].rearrange("p (t n) -> p t n", n=P),
                                     flat[:, 0:GN].rearrange("p (t n) -> p t n", n=P),
                                     ACT.Copy).then_inc(tp_ev, 1)

            def relu(g):
                act.wait_ge(h_mm, g + 1)
                after(act, hT_cp, g)
                after(act, hb_mm, g)
                nc.scalar.activation(h_now.rearrange("p (b n) -> p b n", b=2), ps[:, 4:6, 0:HN],
                                     ACT.Relu, bias=bp_sb[:, :]).then_inc(h_ev, 1)

            def squares(g):
                act.wait_ge(hb_mm, g + 1)
                after(act, hp_out, 16 * g)
                nc.scalar.activation(hp_sb[:, :, :].rearrange("p t f -> p (t f)"), flat[:, 6 * 512:6 * 512 + GN],
                                     ACT.Square).then_inc(hb_ev, 1)

            keep_rows(0)
            relu(0)
            keep_rows(1)
            squares(0)
            with act.Fori(1, NG - 1) as g:
                relu(g)
                keep_rows(g + 1)
                squares(g)
            relu(NG - 1)
            squares(NG - 1)

            def roots(g):
                after(act, o_mm, g)
                nc.scalar.activation(hp_sb[:, :, :].rearrange("p t f -> p (t f)"), aggT[:, bass.ds(g * GN, GN)],
                                     ACT.Sqrt).then_inc(sq_done, 1)

            def normalize(g):
                act.wait_ge(ln_mv, 2 + g)
                nc.scalar.activation(sd[:, :], mv[:, :, 1], ACT.Sqrt, bias=eps[:, :]).then_inc(ln_sd, 1)
                act.wait_ge(ln_rs, g + 1)
                after(act, t2_done, g)
                for t in range(GT):
                    op = nc.scalar.activation(xn[:, t, :], x_all[:, bass.ds(g * GT + t, 1), :].rearrange("p a d -> p (a d)"),
                                              ACT.Identity, bias=nm[:, t:t + 1], scale=rs[:, t:t + 1])
                op.then_inc(ln_xn, 1)

            def keep_turned(g):
                act.wait_ge(t2_done, g + 1)
                for k in range(KD):
                    op = nc.scalar.activation(xn2T[:, k, bass.ds(g * GN, GN)].rearrange("p (t n) -> p t n", n=P),
                                              flat[:, 2048 + 1024 * k:2048 + 1024 * k + GN].rearrange("p (t n) -> p t n", n=P),
                                              ACT.Copy)
                op.then_inc(t2_ev, 1)

            act.wait_ge(agg_done, 1)
            roots(0)
            roots(1)
            normalize(0)
            with act.Fori(1, NG - 1) as g:
                roots(g + 1)
                keep_turned(g - 1)
                normalize(g)
            keep_turned(NG - 2)
            normalize(NG - 1)
            keep_turned(NG - 1)

            def exps(c):
                act.wait_ge(q_rdy, c + 1)
                nc.scalar.activation(dq, dq, ACT.Exp).then_inc(ex_done, 1)

            def hidden(b, e):
                for f in range(FB):
                    act.wait_ge(up_mm, (b * NE + e) * FB + f + 1)
                    nc.scalar.activation(hid[:, e % 2, f, :], ps[:, f, 0:MB], ACT.Gelu,
                                         bias=b1m[:, e * FB + f:e * FB + f + 1]).then_inc(gelu_done, 1)

            def experts(b, pair, end):
                for e in range(NE):
                    if pair is not None and e % 2 == 0:
                        with act.If(pairs > pair):
                            exps(2 * pair + e // 2)
                    if e < NE - 1:
                        hidden(b, e + 1)
                    elif not end:
                        hidden(b + 1, 0)
                    if e == 0 and pair is not None:
                        act.wait_ge(y_st, 16 * b)
                    act.wait_ge(dn_mm, ((b * NE) + e + 1) * QB)
                    for h in range(2):
                        nc.scalar.activation(y_sb[:, 2 * h:2 * h + 2, e, :],
                                             ps[0:MQ, 4 + 2 * (e % 2) + h, :].rearrange("p (q d) -> p q d", q=2),
                                             ACT.Copy).then_inc(y_ev, 1)
                act.wait_ge(y_ev, (b + 1) * 2 * NE)
                act.dma_start(y_tab.rearrange("(b q p) n -> b p q n", q=QB, p=MQ)[bass.ds(b, 1)].rearrange("a p q n -> p (a q) n"),
                              y_sb.rearrange("p q e d -> p q (e d)")).then_inc(y_st, 16)

            pairs = act.value_load(row_i[0:1, 0:1], min_val=1, max_val=NCH // 2)
            hidden(0, 0)
            experts(0, None, False)
            with act.Fori(1, NMB - 1) as b:
                experts(b, b - 1, False)
            experts(NMB - 1, NMB - 2, True)
            with act.Fori(NMB - 1, NCH // 2) as i:
                with act.If(pairs > i):
                    exps(2 * i)
                    exps(2 * i + 1)
            act.wait_ge(row_q, 1)
            nc.scalar.activation(rowt[0:20, 5:7, :], rowt[0:20, 5:7, :], ACT.Exp).then_inc(row_ex, 1)
            act.wait_ge(nd_q, 1)
            nc.scalar.activation(n_tmp[:, 4:7], n_tmp[:, 4:7], ACT.Exp).then_inc(nd_act, 1)
            act.wait_ge(nd_q, 2)
            nc.scalar.activation(n_tmp[:, 7, :, 3], n_tmp[:, 7, :, 1], ACT.Sqrt, bias=eps[:, :]).then_inc(nd_act, 1)
            act.wait_ge(nd_q, 3)
            nc.scalar.activation(n_tmp[:, 2], n_tmp[:, 2], ACT.Exp).then_inc(nd_act, 1)

            def store_out(n, tiles, rows):
                act.wait_ge(fo_rdy, n + 1)
                act.dma_start(out[bass.ds(n * YT * P, tiles * rows), :].rearrange("(t p) d -> p t d", p=rows),
                              x_all[0:rows, bass.ds(n * YT, tiles), :]).then_inc(fo_out, 16)

            with act.Fori(0, YL * YS) as n:
                store_out(n, YT, P)
            store_out(YL * YS, 1, N - (NT - 1) * P)

        @block.tensor
        def _(pe):
            pe.wait_ge(pool_c, 6)
            pe.wait_ge(consts, 1)
            pe.wait_ge(ge_in, 48)
            pe.wait_ge(rel_rdy, 1)
            for n, rows in enumerate((g_srcf, g_dstf, g_w)):
                for j in range(ET):
                    at = ps[:, 2 * n + j // 4, (j % 4) * GG:(j % 4 + 1) * GG]
                    mm = nc.tensor.transpose(at, rows[0:GG, j * P:(j + 1) * P], ident[0:GG, 0:GG])
                mm.then_inc(ge_tp, 1)
            for i in range(2):
                mm = nc.tensor.transpose(ps[0:1, 6, i * GG:(i + 1) * GG], spread[0:GG, i:i + 1], ident[0:GG, 0:GG])
            mm.then_inc(ge_tp, 1)
            pe.wait_ge(ge_ev, 4)
            nc.tensor.matmul(ps[:, 7, 0:GG], ones[0:1, :], base_f[:, :], start=True, stop=True).then_inc(ge_tp, 1)
            pe.wait_ge(par_in, 16 * N_PAR)
            pe.wait_ge(ge_ev, 5)

            def turn_rows(g, s):
                pe.wait_ge(ln_xn, g + 1)
                after(pe, tp_ev, 2 * g)
                for t in range(GT):
                    for k in range(KD):
                        mm = nc.tensor.transpose(ps[:, 2 * k + t // 4, (t % 4) * P:(t % 4 + 1) * P],
                                                 xn_s[s][:, t, k * P:(k + 1) * P], ident[:, :])
                mm.then_inc(tp_done, 1)

            def project(g):
                pe.wait_ge(tp_ev, 2 * g + 2)
                after(pe, h_ev, g)
                for h in range(2):
                    for k in range(KD):
                        mm = nc.tensor.matmul(ps[:, 4 + h, 0:HN], wp_sb[:, k, :], xnT[:, k, h * HN:(h + 1) * HN],
                                              start=(k == 0), stop=(k == KD - 1))
                mm.then_inc(h_mm, 1)

            def turn_back(g):
                pe.wait_ge(h_ev, g + 1)
                after(pe, hb_ev, g)
                for t in range(GT):
                    mm = nc.tensor.transpose(ps[:, 6 + t // 4, (t % 4) * P:(t % 4 + 1) * P],
                                             h_now[:, t * P:(t + 1) * P], ident[:, :])
                mm.then_inc(hb_mm, 1)

            turn_rows(0, 0)
            project(0)
            turn_rows(1, 1)
            turn_back(0)
            with pe.Fori(0, NG // 2 - 1) as i:
                for s in range(2):
                    project(2 * i + 1 + s)
                    turn_rows(2 * i + 2 + s, s)
                    turn_back(2 * i + 1 + s)
            project(NG - 2)
            turn_rows(NG - 1, 0)
            turn_back(NG - 2)
            project(NG - 1)
            turn_back(NG - 1)
            pe.wait_ge(hb_ev, NG)

            def aggregate(g, s, n):
                pe.wait_ge(gath[s], 16 * ET * (n + 1))
                pe.wait_ge(oh_rdy, g + 1)
                for j in range(ET):
                    mm = nc.tensor.matmul(ps[:, s, 0:P], g_ring[:, s, j, :], oh_ring[:, s, j, :],
                                          start=(j == 0), stop=(j == ET - 1))
                mm.then_inc(mm_done, 1)

            def turn_keys(n, src):
                pe.wait_ge(key_rdy, n + 1)
                for b in range(FC // P):
                    mm = nc.tensor.transpose(ps[:, 2 + b // 4, (b % 4) * P:(b % 4 + 1) * P],
                                             src[:, b * P:(b + 1) * P], ident[:, :])
                mm.then_inc(key_tp, 1)

            def histogram(c):
                pe.wait_ge(hist_rdy, c + 1)
                for t in range(HIST_CH):
                    mm = nc.tensor.matmul(ps[:, 4, 0:64], oh_lo[:, c % 2, t, :], oh_hi[:, c % 2, t, :],
                                          start=(c == 0 and t == 0), stop=(c == FC // HIST_CH - 1 and t == HIST_CH - 1))
                mm.then_inc(hist_mm, 1)

            turns = 0
            for g, step in enumerate(STEPS):
                for kind, a, b in step:
                    if kind == "turn":
                        turn_keys(turns, keys[b])
                        turns += 1
                    elif kind == "hist":
                        histogram(a)
                    elif kind == "cum":
                        pe.wait_ge(cum_rdy, 1)
                        nc.tensor.matmul(ps[:, 4, 64:128], lower[:, :], cum[:, 0, :], start=True, stop=True)
                        nc.tensor.matmul(ps[:, 4, 128:192], ones[:, :], cum[:, 0, :], start=True, stop=True).then_inc(cum_mm, 1)
                        pe.wait_ge(len_mm, 1)
                        nc.tensor.matmul(ps[:, 4, 192:193], ones[:, :], row_len[:, 0:1], start=True, stop=True).then_inc(cum_mm, 1)
                if g >= 2:
                    pe.wait_ge(add_done, g - 1)
                aggregate(g, g % 2, g // 2)
            with pe.Fori(len(STEPS) // 2, GG // 2) as i:
                for s in range(2):
                    pe.wait_ge(add_done, 2 * i + s - 1)
                    aggregate(2 * i + s, s, i)

            with pe.If(pe.value_load(far[0:1, 0:1], min_val=0, max_val=1) > 0):
                with pe.Fori(0, GG) as g:
                    with pe.Fori(0, NT) as c:
                        pe.wait_ge(far_gath, 16 * ET * (g + 1))
                        pe.wait_ge(far_oh, g * NT + c + 1)
                        for j in range(ET):
                            mm = nc.tensor.matmul(ps[:, 0, 0:P], g_ring[:, 0, j, :], oh_ring[:, 0, j, :],
                                                  start=(j == 0), stop=(j == ET - 1))
                        mm.then_inc(far_mm, 1)

            def outputs(g, tiles):
                if tiles[0] == 0:
                    pe.wait_ge(sq_done, g + 1)
                    pe.wait_ge(h_cp, g + 1)
                    after(pe, x2_rdy, g)
                for t in tiles:
                    at = ps[:, t // 2, (t % 2) * D:(t % 2 + 1) * D]
                    nc.tensor.matmul(at, h_now2[:, t * P:(t + 1) * P], w1_sb[:, :], start=True, stop=False)
                    mm = nc.tensor.matmul(at, hp_sb[:, t, :], w2_sb[:, :], start=False, stop=True)
                if tiles[-1] == GT - 1:
                    mm.then_inc(o_mm, 1)

            def turn(g):
                pe.wait_ge(ln_xn, NG + 1 + g)
                after(pe, tab_rdy, g)
                for t in range(GT):
                    for k in range(KD):
                        mm = nc.tensor.transpose(ps[:, 4 + 2 * k + t // 4, (t % 4) * P:(t % 4 + 1) * P],
                                                 xn[:, t, k * P:(k + 1) * P], ident[:, :])
                mm.then_inc(t2_done, 1)
                pe.wait_ge(t2_ev, g + 1)
                for h in range(2):
                    for k in range(KD):
                        mm = nc.tensor.matmul(ps[0:HK, 4 + h, 0:HN], wg_sb[:, k, :],
                                              xn2T[:, k, bass.ds(g * GN + h * HN, HN)],
                                              start=(k == 0), stop=(k == KD - 1))
                mm.then_inc(g_mm, 1)

            def features(g):
                for t in range(GT):
                    mm = nc.tensor.transpose(ps[:, 7, 384 + t * HK:384 + (t + 1) * HK], featT[:, t * P:(t + 1) * P],
                                             ident[0:HK, 0:HK])
                mm.then_inc(feat_tp, 1)

            outputs(0, range(GT))
            outputs(1, range(GT))
            turn(0)
            with pe.Fori(2, NG) as g:
                outputs(g, range(3))
                pe.wait_ge(feat_ev, g - 1)
                outputs(g, range(3, 5))
                features(g - 2)
                outputs(g, range(5, GT))
                turn(g - 1)
            pe.wait_ge(feat_ev, NG - 1)
            features(NG - 2)
            turn(NG - 1)
            pe.wait_ge(feat_ev, NG)
            features(NG - 1)

            pe.wait_ge(mw_in, 32)
            pe.wait_ge(tab_rdy, NG)
            pe.wait_ge(b2_rdy, 1)

            def up(b, e, first):
                for f in range(FB):
                    if not first:
                        pe.wait_ge(gelu_done, (b * NE + e) * FB + f + 1 - FB)
                    for k in range(KD):
                        mm = nc.tensor.matmul(ps[:, f, 0:MB], w1m[:, e, k, f * P:(f + 1) * P],
                                              xn2T[:, k, bass.ds(b * MB, MB)], start=(k == 0), stop=(k == KD - 1))
                    mm.then_inc(up_mm, 1)

            def down(b, e, first):
                pe.wait_ge(gelu_done, (b * NE + e + 1) * FB)
                if not first:
                    pe.wait_ge(y_ev, (b * NE + e - 1) * 2)
                for q in range(QB):
                    at = ps[0:MQ, 4 + 2 * (e % 2) + q // 2, (q % 2) * D:(q % 2 + 1) * D]
                    for f in range(FB):
                        nc.tensor.matmul(at, hid[:, e % 2, f, q * MQ:(q + 1) * MQ], w2m[:, e, f, :],
                                         start=(f == 0), stop=False)
                    nc.tensor.matmul(at, ones_bf[:, :], b2_parts[:, e, :], start=False, stop=True).then_inc(dn_mm, 1)

            def experts(b, end):
                for e in range(NE):
                    if e < NE - 1:
                        up(b, e + 1, False)
                    elif not end:
                        up(b + 1, 0, False)
                    down(b, e, isinstance(b, int) and b == 0 and e < 2)

            up(0, 0, True)
            experts(0, False)
            with pe.Fori(1, NMB - 1) as b:
                experts(b, False)
            experts(NMB - 1, True)

            pe.wait_ge(y_ev, 2 * NMB * NE)
            pe.wait_ge(last_rdy, 1)
            for n in range(4):
                mm = nc.tensor.transpose(ps[0:20, 4, n * P:(n + 1) * P], last[:, n, :], ident[:, :])
            mm.then_inc(last_tp, 1)
            pe.wait_ge(back_rdy, 1)
            for n in range(3):
                mm = nc.tensor.transpose(ps[:, 5, n * 20:(n + 1) * 20], rowt[0:20, 9 + n, :], ident[0:20, 0:20])
            mm.then_inc(back_tp, 1)

        @block.vector
        def _(dve):
            V = nc.vector
            chain = [0]

            def step(*ops):
                for ins in ops:
                    ins.then_inc(dv, 1)
                    chain[0] += 1
                dve.wait_ge(dv, chain[0])

            class Loop:

                def __init__(self, sem_, at, i):
                    self.sem, self.at, self.i, self.n = sem_, at, i, 0

                def step(self, per, *ops):
                    for ins in ops:
                        ins.then_inc(self.sem, 1)
                        self.n += 1
                    dve.wait_ge(self.sem, self.i * per + (self.at + self.n))

            def bc(ap, shape):
                return ap.broadcast_to(shape)

            ops = [V.memset(ones[:, :], 1.0), V.memset(eps[:, :], LN_EPS), V.memset(ones_bf[:, :], 1.0), V.memset(zeros[:, :], 0.0),
                   V.memset(no_edge[:, 0:20], -BIG), V.memset(no_edge[:, 20:40], 0.0),
                   V.memset(cum[:, :, :], 0.0)]
            dve.wait_ge(pool_c, 6)
            ops += [V.tensor_copy(iota_row[:, :], iota_i), V.tensor_copy(iota_bf[:, :], iota_i)]
            step(*ops)
            for i in range(8):
                dve_op = V.tensor_scalar(sgn_i[:, i:i + 1], part_i[:, :], i, 1, ALU.logical_shift_right, ALU.bitwise_and)
                dve_op.then_inc(dv, 1)
                chain[0] += 1
            dve.wait_ge(dv, chain[0])
            step(V.tensor_copy(sgn[:, :], sgn_i[:, :]))
            step(V.tensor_scalar(sgn[:, :], sgn[:, :], -2.0, 1.0, ALU.mult, ALU.add))
            V.memset(spread[:, :], 0.0).then_inc(consts, 1)
            V.memset(zeros[:, 0:1], 0.0).then_inc(zero_rdy, 1)

            dve.wait_ge(ge_in, 48)
            step(V.tensor_copy(g_srcf[0:GG, :], g_src[0:GG, :]), V.tensor_copy(g_dstf[0:GG, :], g_dst[0:GG, :]))
            step(V.tensor_reduce(spread[0:GG, 0:1], g_dstf[0:GG, :], AX.X, ALU.min))
            step(V.tensor_scalar(g_dstf[0:GG, :], g_dstf[0:GG, :], spread[0:GG, 0:1], None, ALU.subtract))
            V.tensor_reduce(spread[0:GG, 1:2], g_dstf[0:GG, :], AX.X, ALU.max).then_inc(rel_rdy, 1)
            for n, cols in enumerate((srcT, relT, wT)):
                dve.wait_ge(ge_tp, n + 1)
                for h in range(2):
                    op = V.tensor_copy(cols[:, :, 4 * h:4 * h + 4].rearrange("p g j -> p j g"),
                                       ps[:, 2 * n + h, 0:4 * GG].rearrange("p (j g) -> p j g", g=GG))
                op.then_inc(ge_ev, 1)
            dve.wait_ge(ge_tp, 4)
            step(V.tensor_copy(base_row[:, :, :], ps[0:1, 6, 0:2 * GG].rearrange("p (a g) -> p a g", a=2)),
                 V.tensor_reduce(scrap[0:1, 2:3], ps[0:1, 6, GG:2 * GG], AX.X, ALU.max),
                 V.tensor_copy(base_f[:, :], ps[0:1, 6, 0:GG]))
            V.tensor_scalar(far[:, :], scrap[0:1, 2:3], float(P) - 0.5, None, ALU.is_ge).then_inc(ge_ev, 1)
            dve.wait_ge(ge_tp, 5)
            V.tensor_copy(base_all[:, :], ps[:, 7, 0:GG]).then_inc(ge_ev, 1)
            dve.wait_ge(ge_ev, 5)

            per = 2 * GT + 1
            for n, (g0, g1) in enumerate(((0, X_FIRST), (X_FIRST, NG))):
                dve.wait_ge(x_ld[n], 16 * (g1 - g0))
                with dve.Fori(g0, g1) as g:
                    loop = Loop(dv, chain[0] - g0 * per, g)
                    loop.step(per, *[V.bn_stats(st6[:, t, :], x_all[:, bass.ds(g * GT + t, 1), :].rearrange("p a d -> p (a d)"))
                                     for t in range(GT)])
                    apart(dve)
                    loop.step(per, *[V.bn_aggr(mv[:, t, :], st6[:, t, :]) for t in range(GT)])
                    loop.step(per, V.tensor_copy(mv_x[:, bass.ds(g * GT, GT), :], mv[:, :, :]))
                    apart(dve)
                    assert loop.n == per, loop.n
                chain[0] += (g1 - g0) * per
            V.memset(scrap[:, 3:4], 0.0).then_inc(ln_mv, 1)
            dve.wait_ge(ln_sd, 1)
            step(V.reciprocal(rs_x, sd_x))

            def normalize(g, s):
                after(dve, tp_done, g - 1)
                for t in range(GT):
                    op = V.tensor_scalar(xn_s[s][:, t, :], x_all[:, bass.ds(g * GT + t, 1), :].rearrange("p a d -> p (a d)"),
                                         mv_x[:, bass.ds(g * GT + t, 1), 0:1].rearrange("p a s -> p (a s)"),
                                         rs_x[:, bass.ds(g * GT + t, 1)], ALU.subtract, ALU.mult)
                op.then_inc(ln_xn, 1)

            def keep_rows(g):
                dve.wait_ge(tp_done, g + 1)
                after(dve, h_mm, g)
                V.tensor_copy(xnT[:, 1, :].rearrange("p (t n) -> p t n", n=P),
                              flat[:, 1024:1024 + GN].rearrange("p (t n) -> p t n", n=P)).then_inc(tp_ev, 1)

            normalize(0, 0)
            normalize(1, 1)
            keep_rows(0)
            with dve.Fori(1, NG // 2) as i:
                for s in range(2):
                    normalize(2 * i + s, s)
                    keep_rows(2 * i + s - 1)
            normalize(NG - 1, 0)
            keep_rows(NG - 2)
            keep_rows(NG - 1)
            dve.wait_ge(clear, 2)
            dve.wait_ge(h_mm, NG)

            def one_hots(g, s):
                for j in range(ET):
                    at = [cols.rearrange("p g j -> p (g j)")[:, bass.ds(g * ET + j, 1)] for cols in (relT, wT)]
                    op = V.tensor_scalar(oh_ring[:, s, j, :], iota_row[:, :], at[0], at[1], ALU.is_equal, ALU.mult)
                op.then_inc(oh_rdy, 1)

            def add_window(g, s):
                base = dve.value_load(base_row[0:1, 0, bass.ds(g, 1)], min_val=0, max_val=NP - 1)
                dve.wait_ge(mm_done, g + 1)
                dve.wait_ge(add_done, g)
                V.tensor_tensor(aggT[:, bass.ds(base, P)], aggT[:, bass.ds(base, P)], ps[:, s, 0:P],
                                ALU.add).then_inc(add_done, 1)

            cur = [0]

            def make_keys():
                dve.wait_ge(fe_in, 32)
                k_i = [k.bitcast(I32) for k in keys]
                step(V.tensor_scalar(k_i[0], e_src, float(N - 1), None, ALU.min),
                     V.tensor_scalar(k_i[1], e_dst, DST_BITS, KEY_TOP, ALU.logical_shift_left, ALU.bitwise_or))
                step(V.tensor_tensor(k_i[0], k_i[0], k_i[1], ALU.bitwise_or))

            def swap_stage(k, j):
                a, b = cur[0], 1 - cur[0]
                d = 1 << j
                if j == k - 1 and k > FLOG - 1 and k - FLOG < 8:
                    i = k - FLOG
                    if i >= 1:
                        step(V.tensor_scalar(keys[a], keys[a], sgn[:, i - 1:i], None, ALU.mult))
                    if k < ELOG:
                        step(V.tensor_scalar(keys[a], keys[a], sgn[:, i:i + 1], None, ALU.mult))
                if j >= FLOG:
                    if j == k - 1:
                        src = turned(a)
                    else:
                        src = keys[a]
                    m = P // (2 * (d >> FLOG))
                    v = src.rearrange("p (c m s i) -> p s c m i", c=FC // P, m=m, s=2)
                    w = keys[b].rearrange("p (c m s i) -> p s c m i", c=FC // P, m=m, s=2)
                    step(V.tensor_tensor(w[:, 0], v[:, 0], v[:, 1], ALU.min),
                         V.tensor_tensor(w[:, 1], v[:, 0], v[:, 1], ALU.max))
                else:
                    src = turned(a) if (j == FLOG - 1 and k > FLOG) else keys[a]
                    if k < FLOG:
                        r, m = FC >> (k + 1), 1 << (k - 1 - j)
                        v = src.rearrange("p (r z m s i) -> p z s r m i", r=r, z=2, m=m, s=2)
                        w = keys[b].rearrange("p (r z m s i) -> p z s r m i", r=r, z=2, m=m, s=2)
                        step(*[V.tensor_tensor(w[:, z, s], v[:, z, 0], v[:, z, 1], (ALU.min, ALU.max)[z ^ s])
                               for z in range(2) for s in range(2)])
                    else:
                        m = FC // (2 * d)
                        v = src.rearrange("p (m s i) -> p s m i", m=m, s=2)
                        w = keys[b].rearrange("p (m s i) -> p s m i", m=m, s=2)
                        step(V.tensor_tensor(w[:, 0], v[:, 0], v[:, 1], ALU.min),
                             V.tensor_tensor(w[:, 1], v[:, 0], v[:, 1], ALU.max))
                cur[0] = b
                if (k, j) == STAGES[-1]:
                    V.memset(scrap[:, 3:4], 0.0).then_inc(key_end, 1)

            n_turn = [0]

            def turned(a):
                V.tensor_copy(spread[0:1, 3:4], zeros[0:1, 1:2]).then_inc(key_rdy, 1)
                n_turn[0] += 1
                dve.wait_ge(key_tp, n_turn[0])
                step(V.tensor_copy(keys[a], flat[:, 2 * 512:2 * 512 + FC]))
                return keys[a]

            def halves():
                step(V.tensor_scalar(half_i, e_dst, P - 1, None, ALU.bitwise_and))
                step(V.tensor_copy(lo_bf, half_i))
                step(V.tensor_scalar(half_i, e_dst, 7, None, ALU.logical_shift_right))
                step(V.tensor_copy(hi_bf, half_i))

            def histogram(c):
                if c >= 2:
                    dve.wait_ge(hist_mm, c - 1)
                cols = slice(c * HIST_CH, (c + 1) * HIST_CH)
                V.tensor_tensor(oh_lo[:, c % 2], bc(iota_bf[:, :].unsqueeze(1), [P, HIST_CH, P]),
                                bc(lo_bf[:, cols].unsqueeze(2), [P, HIST_CH, P]), ALU.is_equal).then_inc(dv, 1)
                chain[0] += 1
                V.tensor_tensor(oh_hi[:, c % 2], bc(iota_bf[:, 0:64].unsqueeze(1), [P, HIST_CH, 64]),
                                bc(hi_bf[:, cols].unsqueeze(2), [P, HIST_CH, 64]), ALU.is_equal).then_inc(hist_rdy, 1)

            def into_rows(at):
                q, rest, off = cum[:, 2, :], cum[:, 3, :], cum[:, 5, :]
                step(V.tensor_scalar(q, at, row_len[:, 3:4], None, ALU.mult))
                step(V.tensor_copy(half_i[:, 0:64], q))
                step(V.tensor_copy(q, half_i[:, 0:64]))
                step(V.tensor_scalar(rest, q, row_len[:, 2:3], None, ALU.mult))
                step(V.tensor_tensor(rest, at, rest, ALU.subtract))
                step(V.tensor_scalar(off, rest, row_len[:, 2:3], None, ALU.is_ge),
                     V.tensor_scalar(rest, rest, 0.0, None, ALU.is_lt))
                step(V.tensor_tensor(q, q, off, ALU.add))
                step(V.tensor_tensor(q, q, rest, ALU.subtract))
                step(V.tensor_scalar(rest, q, row_len[:, 2:3], None, ALU.mult))
                step(V.tensor_tensor(at, at, rest, ALU.subtract), V.tensor_scalar(q, q, float(FC), None, ALU.mult))
                step(V.tensor_tensor(at, at, q, ALU.add))

            def positions():
                dve.wait_ge(hist_mm, FC // HIST_CH)
                V.tensor_copy(cum[:, 0, :], ps[:, 4, 0:64]).then_inc(cum_rdy, 1)
                dve.wait_ge(cum_rdy, 1)
                dve.wait_ge(cum_mm, 1)
                step(V.tensor_copy(cum[:, 2, :], ps[:, 4, 128:192]))
                step(V.tensor_tensor_scan(cum[:, 1, :], ones[:, 0:64], cum[:, 2, :], 0.0, ALU.mult, ALU.add))
                step(V.tensor_tensor(cum[:, 1, :], cum[:, 1, :], cum[:, 2, :], ALU.subtract))
                step(V.tensor_tensor(cum[:, 1, :], cum[:, 1, :], ps[:, 4, 64:128], ALU.add),
                     V.tensor_scalar(has[:, :], cum[:, 0, 0:NT], 0.0, None, ALU.is_gt))
                V.tensor_tensor(row_len[:, 0:1], cum[:, 1, N // P:N // P + 1], ident[:, N % P:N % P + 1],
                                ALU.mult).then_inc(len_mm, 1)
                dve.wait_ge(cum_mm, 2)
                step(V.tensor_copy(row_len[:, 1:2], ps[:, 4, 192:193]))
                step(V.tensor_scalar(cum[:, 2, 0:NCH // 2], iota_row[:, 0:NCH // 2], float(2 * CH * P), row_len[:, 1:2],
                                     ALU.mult, ALU.is_lt), V.memset(cum[:, 3, 0:1], 0.0))
                step(V.tensor_reduce(row_len[:, 1:2], cum[:, 2, 0:NCH // 2], AX.X, ALU.add),
                     V.tensor_copy(cum[:, 3, 0:1], part_i[:, :]))
                step(V.tensor_scalar(row_len[:, 1:2], row_len[:, 1:2], 1.0, None, ALU.max))
                step(V.tensor_scalar(row_len[:, 2:3], row_len[:, 1:2], float(2 * CH), None, ALU.mult),
                     V.tensor_tensor(cum[:, 3, 0:1], cum[:, 3, 0:1], row_len[:, 1:2], ALU.mult))
                step(V.reciprocal(row_len[:, 3:4], row_len[:, 2:3]),
                     V.tensor_scalar(cum[:, 3, 1:2], row_len[:, 2:3], -1.0, None, ALU.add),
                     V.tensor_copy(row_i[:, 0:1], row_len[:, 1:2]))
                step(V.tensor_copy(row_i[:, 1:2], cum[:, 3, 1:2]))
                step(V.tensor_scalar(cum[:, 2, 0:NCH // 2], iota_row[:, 0:NCH // 2], cum[:, 3, 0:1], None, ALU.add))
                V.tensor_copy(fetch_idx[:, :], cum[:, 2, 0:NCH // 2]).then_inc(len_rdy, 1)
                dve.wait_ge(len_rdy, 1)
                step(V.tensor_tensor(cum[:, 4, :], cum[:, 1, :], cum[:, 0, :], ALU.add))
                step(V.tensor_scalar(cum[:, 4, :], cum[:, 4, :], -1.0, 0.0, ALU.add, ALU.max))
                into_rows(cum[:, 4, :])
                into_rows(cum[:, 1, :])
                step(V.tensor_copy(e_idx[:, :], cum[:, 4, 0:NT]))
                step(V.tensor_copy(cum[:, 4, 0:1], part_i[:, :]))
                step(V.tensor_scalar(cum[:, 3, :], iota_row[:, 0:64], float(P), float(EF), ALU.mult, ALU.add))
                step(V.tensor_scalar(cum[:, 3, :], cum[:, 3, :], cum[:, 4, 0:1], None, ALU.add))
                step(V.tensor_tensor(cum[:, 1, :], cum[:, 1, :], cum[:, 3, :], ALU.subtract))
                step(V.tensor_tensor(cum[:, 1, 0:NT], cum[:, 1, 0:NT], has[:, :], ALU.mult))
                step(V.tensor_tensor(cum[:, 1, :], cum[:, 1, :], cum[:, 3, :], ALU.add))
                step(V.tensor_copy(st_idx[:, :], cum[:, 1, 0:NT]))

            def marks():
                dve.wait_ge(fetched, 16 * NCH // 2)
                k_i = keys[1 - cur[0]].bitcast(I32)
                t_i = keys[cur[0]].bitcast(I32)
                row_end = dve.value_load(row_i[0:1, 1:2], min_val=2 * CH - 1, max_val=FC - 1)
                step(V.tensor_scalar(s_src[:, :], k_i, (1 << DST_BITS) - 1, None, ALU.bitwise_and),
                     V.tensor_scalar(t_i, k_i, DST_BITS, (1 << DST_BITS) - 1, ALU.logical_shift_right, ALU.bitwise_and))
                step(V.tensor_copy(s_dst, t_i))
                step(V.tensor_copy(ends[:, 0:1], s_dst[:, 0:1]))
                V.tensor_copy(ends[:, 1:2], s_dst[:, bass.ds(row_end, 1)]).then_inc(ends_rdy, 1)
                dve.wait_ge(ends_rdy, 1)
                step(V.tensor_copy(first_idx[:, :], ends[:, 0:1]), V.memset(was_equal[:, 0:1], 0.0),
                     V.tensor_tensor(was_equal[:, 1:FC], s_dst[:, 1:FC], s_dst[:, 0:FC - 1], ALU.is_equal))
                V.tensor_scalar(pen[:, :], was_equal, -1.0, BIG, ALU.add, ALU.mult).then_inc(sorted_s, 1)

            def add_bias(g):
                if g == 0:
                    dve.wait_ge(bias_in, 32)
                    step(V.tensor_tensor(b12[:, 0, :], b12[:, 0, :], b12[:, 1, :], ALU.add))
                group = x_all[:, g * GT:(g + 1) * GT, :]
                step(V.tensor_tensor(group, group, bc(b12[:, 0:1, :], [P, GT, D]), ALU.add))

            def do(kind, a, b):
                if kind == "keys":
                    make_keys()
                    halves()
                elif kind == "bias":
                    add_bias(a)
                elif kind == "stage":
                    swap_stage(a, b)
                elif kind == "hist":
                    histogram(a)
                elif kind == "cum":
                    positions()
                elif kind == "marks":
                    marks()

            for g, todo in enumerate(STEPS):
                one_hots(g, g % 2)
                for kind, a, b in todo:
                    do(kind, a, b)
                if g >= 1:
                    add_window(g - 1, (g - 1) % 2)
            add_window(len(STEPS) - 1, 1)
            done = len(STEPS)
            with dve.Fori(done // 2, GG // 2) as i:
                for s in range(2):
                    one_hots(2 * i + s, s)
                    add_window(2 * i + s, s)

            dve.wait_ge(add_done, GG)
            with dve.If(dve.value_load(far[0:1, 0:1], min_val=0, max_val=1) > 0):
                with dve.Fori(0, GG) as g:
                    rel = relT[:, bass.ds(g, 1), :].rearrange("p a j -> p (a j)")
                    w = wT[:, bass.ds(g, 1), :].rearrange("p a j -> p (a j)")
                    dve.wait_ge(far_add, g * (NT * 3 + 1))
                    V.scalar_tensor_tensor(out=far_cols[:, 0, :], in0=rel, scalar=float(P) - 0.5, in1=w,
                                           op0=ALU.is_ge, op1=ALU.mult)
                    V.tensor_scalar(far_cols[:, 1, :], rel, base_all[:, bass.ds(g, 1)], None, ALU.add).then_inc(far_add, 1)
                    with dve.Fori(0, NT) as c:
                        at = g * (NT * 3 + 1) + c * 3
                        dve.wait_ge(far_add, at + 1)
                        V.tensor_tensor(oh_ring[:, 0], bc(iota_row[:, :].unsqueeze(1), [P, ET, P]),
                                        bc(far_cols[:, 1, :].unsqueeze(2), [P, ET, P]), ALU.is_equal).then_inc(far_add, 1)
                        dve.wait_ge(far_add, at + 2)
                        V.tensor_tensor(oh_ring[:, 0], oh_ring[:, 0], bc(far_cols[:, 0, :].unsqueeze(2), [P, ET, P]),
                                        ALU.mult).then_inc(far_oh, 1)
                        V.tensor_scalar(far_cols[:, 1, :], far_cols[:, 1, :], -float(P), None, ALU.add).then_inc(far_add, 1)
                        dve.wait_ge(far_mm, g * NT + c + 1)
                        block_c = aggT[:, bass.ds(c * P, P)]
                        V.tensor_tensor(block_c, block_c, ps[:, 0, 0:P], ALU.add).then_inc(far_add, 1)
                dve.wait_ge(far_add, GG * (NT * 3 + 1))
            V.memset(scrap[:, 3:4], 0.0).then_inc(agg_done, 1)

            def add_outputs(g, loop):
                dve.wait_ge(o_mm, g + 1)
                dve.wait_ge(ln_xn, NG + g)
                group = x_all[:, bass.ds(g * GT, GT), :].rearrange("p t d -> p (t d)")
                V.tensor_tensor(group, group, flat[:, 0:GT * D], ALU.add).then_inc(x2_rdy, 1)
                dve.wait_ge(x2_rdy, g + 1)
                apart(dve)
                loop.step(per, *[V.bn_stats(st6[:, t, :], x_all[:, bass.ds(g * GT + t, 1), :].rearrange("p a d -> p (a d)"))
                                 for t in range(GT)])
                apart(dve)
                for t in range(GT):
                    op = V.bn_aggr(mv[:, t, :], st6[:, t, :])
                op.then_inc(ln_mv, 1)

            def scales(g, loop):
                dve.wait_ge(ln_sd, 2 + g)
                loop.step(per, V.reciprocal(rs[:, :], sd[:, :]))
                V.scalar_tensor_tensor(out=nm[:, :], in0=mv[:, :, 0], scalar=-1.0, in1=rs[:, :],
                                       op0=ALU.mult, op1=ALU.mult).then_inc(ln_rs, 1)

            def keep_features(g):
                dve.wait_ge(g_mm, g + 1)
                V.tensor_copy(featT.rearrange("p (b n) -> p b n", b=2), ps[0:HK, 4:6, 0:HN]).then_inc(feat_ev, 1)

            def logits(g, loop):
                dve.wait_ge(feat_tp, g + 1)
                h = ps[:, 7, 384:384 + GT * HK].rearrange("p (t c) -> p t c", c=HK)
                V.tensor_copy(tab[:, bass.ds(g * GT, GT), 4:RW].rearrange("p t (h k) -> p t h k", k=5)[:, :, :, 0:NE],
                              h.rearrange("p t (h k) -> p t h k", k=NE))
                loop.step(per, V.tensor_tensor(att_tmp[:, :, :], h, bc(att[:, 0:1, :], [P, GT, HK]), ALU.mult))
                loop.step(per, V.tensor_reduce(tab[:, bass.ds(g * GT, GT), 0:HEADS],
                                               att_tmp[:, :, :].rearrange("p t (h k) -> p t h k", k=NE), AX.X, ALU.add))
                loop.step(per, V.tensor_tensor(att_tmp[:, :, :], h, bc(att[:, 1:2, :], [P, GT, HK]), ALU.mult))
                V.tensor_reduce(adst[:, bass.ds(g * GT, GT), :],
                                att_tmp[:, :, :].rearrange("p t (h k) -> p t h k", k=NE), AX.X, ALU.add).then_inc(tab_rdy, 1)

            loop = Loop(dv, chain[0], 0)
            per = 0
            for g in range(2):
                add_outputs(g, loop)
                scales(g, loop)
            keep_features(0)
            chain[0] += loop.n
            per = GT + 4
            with dve.Fori(2, NG) as g:
                loop = Loop(dv, chain[0] - 2 * per, g)
                logits(g - 2, loop)
                add_outputs(g, loop)
                scales(g, loop)
                keep_features(g - 1)
                assert loop.n == per, loop.n
            chain[0] += (NG - 2) * per
            loop = Loop(dv, chain[0], 0)
            logits(NG - 2, loop)
            keep_features(NG - 1)
            logits(NG - 1, loop)
            chain[0] += loop.n
            dve.wait_ge(tab_rdy, NG)

            dve.wait_ge(x2_out, 16 * NG)
            step(V.tensor_copy(b2_part, b2m[:, :, :]))
            step(V.tensor_scalar(b2_parts, b2_part, ident[0:3, 0:1], None, ALU.mult),
                 V.tensor_tensor(b2_rest, b2m[:, :, :], b2_part, ALU.subtract))
            step(V.tensor_copy(b2_part, b2_rest))
            step(V.scalar_tensor_tensor(out=b2_parts, in0=b2_part, scalar=ident[0:3, 1:2], in1=b2_parts,
                                        op0=ALU.mult, op1=ALU.add),
                 V.tensor_tensor(b2_rest, b2_rest, b2_part, ALU.subtract))
            step(V.tensor_copy(b2_part, b2_rest))
            V.scalar_tensor_tensor(out=b2_parts, in0=b2_part, scalar=ident[0:3, 2:3], in1=b2_parts,
                                   op0=ALU.mult, op1=ALU.add).then_inc(b2_rdy, 1)
            dve.wait_ge(b2_rdy, 1)

            dve.wait_ge(af_in, 16)
            dve.wait_ge(a_in, 16)
            step(V.tensor_copy(a_edge[:, 0, :], a_first[:, :]))
            step(V.tensor_scalar(not_start, pen[:, :], 0.0, None, ALU.is_equal))
            step(*[V.tensor_tensor_scan(a_edge[:, :, h], not_start, a_edge[:, :, h], 0.0, ALU.mult, ALU.add)
                   for h in range(HEADS)])
            step(V.memset(rec_out[:, 1, CH - 1, :], 0.0))

            def scan_chunk(c, s, i, steps, first):
                prev, cols = rec_out[:, 1 - s], bass.ds(c * CH, CH)
                dve.wait_ge(fgath[s], 16 * CH * (i + 1))
                steps(V.tensor_tensor(z1, rec_in[:, s, :, 0:HEADS], a_edge[:, cols, :], ALU.add))
                steps(V.scalar_tensor_tensor(out=z2, in0=z1, scalar=0.2, in1=z1, op0=ALU.mult, op1=ALU.max))
                if not first:
                    dve.wait_ge(rec_st[s], 16 * i)
                steps(*[V.tensor_tensor_scan(rec_out[:, s, :, h], pen[:, cols], z2[:, :, h], prev[:, CH - 1, h:h + 1],
                                             ALU.add, ALU.max) for h in range(HEADS)])
                m = rec_out[:, s, :, 0:HEADS]
                steps(V.tensor_tensor(dq[:, 0, 1:CH, :], m[:, 0:CH - 1, :], m[:, 1:CH, :], ALU.subtract),
                      V.tensor_tensor(dq[:, 0, 0, :], prev[:, CH - 1, 0:HEADS], m[:, 0, :], ALU.subtract),
                      V.tensor_tensor(dq[:, 1], z2, m, ALU.subtract))
                V.tensor_tensor(dq[:, 0], dq[:, 0], bc(pen[:, cols].unsqueeze(2), [P, CH, HEADS]), ALU.add).then_inc(q_rdy, 1)
                dve.wait_ge(ex_done, c + 1)
                V.tensor_tensor(vals, rec_in[:, s, :, HEADS:RW].rearrange("p t (h k) -> p t h k", k=5),
                                bc(dq[:, 1].unsqueeze(3), [P, CH, HEADS, 5]), ALU.mult).then_inc(in_free, 1)
                dve.wait_ge(in_free, c + 1)
                for h in range(HEADS):
                    for k in range(5):
                        n = HEADS + h * 5 + k
                        op = V.tensor_tensor_scan(rec_out[:, s, :, n], dq[:, 0, :, h], vals[:, :, h, k],
                                                  prev[:, CH - 1, n:n + 1], ALU.mult, ALU.add)
                op.then_inc(sc_done, 1)
                dve.wait_ge(sc_done, c + 1)

            per = 2 * 9
            pairs = dve.value_load(row_i[0:1, 0:1], min_val=1, max_val=NCH // 2)
            with dve.Fori(0, NCH // 2) as i:
                with dve.If(pairs > i):
                    loop = Loop(chunk_dv, 0, i)
                    for s in range(2):
                        scan_chunk(2 * i + s, s, i, lambda *ops: loop.step(per, *ops), False)
                    apart(dve)
                    assert loop.n == per, loop.n

            tail = rec_out[:, 1, CH - 1, :]
            V.tensor_copy(last[:, 0, :].rearrange("p (h k) -> p h k", k=5), bc(tail[:, 0:HEADS].unsqueeze(2), [P, HEADS, 5]))
            V.tensor_copy(last[:, 1, :], tail[:, HEADS:RW])
            V.tensor_copy(last[:, 2, :], bc(ends[:, 0:1], [P, 20]))
            V.tensor_copy(last[:, 3, :], bc(ends[:, 1:2], [P, 20])).then_inc(last_rdy, 1)
            dve.wait_ge(last_tp, 1)
            step(V.tensor_copy(rowt[0:20, 0:4, :], ps[0:20, 4, :].rearrange("p (s c) -> p s c", c=P)))
            R = rowt[0:20]
            step(V.memset(R[:, 4, 0:1], 0.0),
                 V.tensor_tensor(R[:, 4, 1:P], R[:, 3, 0:P - 1], R[:, 2, 1:P], ALU.is_equal),
                 V.tensor_tensor(R[:, 7, :], R[:, 2, :], R[:, 3, :], ALU.is_equal))
            step(V.tensor_tensor(R[:, 7, :], R[:, 7, :], R[:, 4, :], ALU.mult))
            step(V.tensor_scalar(R[:, 8, :], R[:, 7, :], -1.0, BIG, ALU.add, ALU.mult))
            step(V.tensor_tensor_scan(R[:, 9, :], R[:, 8, :], R[:, 0, :], 0.0, ALU.add, ALU.max))
            step(V.memset(R[:, 5, 0:1], -BIG),
                 V.tensor_tensor(R[:, 5, 1:P], R[:, 9, 0:P - 1], R[:, 9, 1:P], ALU.subtract),
                 V.tensor_tensor(R[:, 6, :], R[:, 0, :], R[:, 9, :], ALU.subtract))
            V.tensor_tensor(R[:, 5, :], R[:, 5, :], R[:, 8, :], ALU.add).then_inc(row_q, 1)
            dve.wait_ge(row_ex, 1)
            step(V.tensor_tensor(R[:, 6, :], R[:, 6, :], R[:, 1, :], ALU.mult))
            step(V.tensor_tensor_scan(R[:, 1, :], R[:, 5, :], R[:, 6, :], 0.0, ALU.mult, ALU.add))
            step(V.memset(R[:, 0, 0:1], -BIG), V.memset(R[:, 10, 0:1], 0.0),
                 V.tensor_tensor(R[:, 0, 1:P], R[:, 9, 0:P - 1], R[:, 4, 1:P], ALU.mult),
                 V.tensor_tensor(R[:, 10, 1:P], R[:, 1, 0:P - 1], R[:, 4, 1:P], ALU.mult),
                 V.tensor_scalar(R[:, 8, :], R[:, 4, :], -1.0, BIG, ALU.add, ALU.mult))
            step(V.tensor_tensor(R[:, 9, :], R[:, 0, :], R[:, 8, :], ALU.add))
            step(V.memset(R[:, 5, :], 0.0), V.memset(R[:, 11, :], 0.0))
            step(V.tensor_copy(R[:, 5, 0:P - 1], R[:, 7, 1:P]),
                 V.tensor_scalar(R[:, 6, :], iota20(iota_row), float(TRASH), None, ALU.add))
            step(V.tensor_tensor(R[:, 5, 0:P - 1], R[:, 3, 0:P - 1], R[:, 2, 1:P], ALU.is_equal),
                 V.tensor_tensor(R[:, 11, :], R[:, 2, :], R[:, 3, :], ALU.is_equal))
            step(V.tensor_tensor(R[:, 5, :], R[:, 5, :], R[:, 11, :], ALU.mult))
            step(V.tensor_scalar(R[:, 5, :], R[:, 5, :], -1.0, 1.0, ALU.mult, ALU.add))
            step(V.tensor_tensor(R[:, 5, :], R[:, 5, :], R[:, 4, :], ALU.mult))
            step(V.tensor_tensor(R[:, 2, :], R[:, 2, :], R[:, 6, :], ALU.subtract))
            step(V.tensor_tensor(R[:, 2, :], R[:, 2, :], R[:, 5, :], ALU.mult))
            V.tensor_tensor(R[:, 11, :], R[:, 2, :], R[:, 6, :], ALU.add).then_inc(back_rdy, 1)
            dve.wait_ge(back_tp, 1)
            step(V.tensor_copy(carried, ps[:, 5, 0:60]))
            V.tensor_copy(carry_idx[:, :], carried[:, 40:41]).then_inc(c_rdy, 1)

            dve.wait_ge(r_in, 16 * NT)
            dve.wait_ge(c_in, 16)
            m_r, m_c, m_s = n_tmp[:, 0], n_tmp[:, 1], n_tmp[:, 2]
            hasb = bc(has[:, :].unsqueeze(2), [P, NT, HEADS])
            cm = node_c[:, :, 0:20].rearrange("p t (h k) -> p t h k", k=5)[:, :, :, 0]
            step(V.tensor_tensor(m_r, node_r[:, :, 0:HEADS], hasb, ALU.mult),
                 V.tensor_scalar(n_tmp[:, 3], hasb, -1.0, BIG, ALU.add, ALU.mult),
                 V.tensor_tensor(m_s, tab[:, :, 0:HEADS], adst[:, :, :], ALU.add),
                 V.tensor_copy(m_c, cm))
            step(V.tensor_tensor(m_r, m_r, n_tmp[:, 3], ALU.add),
                 V.scalar_tensor_tensor(out=n_tmp[:, 7], in0=m_s, scalar=0.2, in1=m_s, op0=ALU.mult, op1=ALU.max))
            step(V.tensor_tensor(n_tmp[:, 3], m_r, m_c, ALU.max))
            step(V.tensor_tensor(n_tmp[:, 3], n_tmp[:, 3], n_tmp[:, 7], ALU.max))
            step(V.tensor_tensor(n_tmp[:, 4], m_r, n_tmp[:, 3], ALU.subtract),
                 V.tensor_tensor(n_tmp[:, 5], m_c, n_tmp[:, 3], ALU.subtract))
            V.tensor_tensor(n_tmp[:, 6], n_tmp[:, 7], n_tmp[:, 3], ALU.subtract).then_inc(nd_q, 1)
            dve.wait_ge(nd_act, 1)

            def b5(ap):
                return bc(ap.unsqueeze(3), [P, NT, HEADS, 5])

            def hk(ap):
                return ap.rearrange("p t (h k) -> p t h k", k=5)

            r5, c5, t5 = hk(node_r[:, :, HEADS:RW]), hk(node_c[:, :, 20:40]), hk(tab[:, :, HEADS:RW])
            step(V.tensor_tensor(r5, r5, b5(n_tmp[:, 4]), ALU.mult), V.tensor_tensor(c5, c5, b5(n_tmp[:, 5]), ALU.mult),
                 V.tensor_tensor(s_tmp, t5, b5(n_tmp[:, 6]), ALU.mult))
            step(V.tensor_tensor(r5, r5, c5, ALU.add))
            step(V.tensor_tensor(s_tmp, s_tmp, r5, ALU.add))
            step(V.tensor_scalar(n_tmp[:, 0], s_tmp[:, :, :, 4], 1e-16, None, ALU.add))
            step(V.reciprocal(n_tmp[:, 1], n_tmp[:, 0]))
            agg, dev = n16[:, 0], n16[:, 1]
            agg4 = agg.rearrange("p t (h k) -> p t h k", k=NE)
            step(V.tensor_tensor(agg4, s_tmp[:, :, :, 0:NE], bc(n_tmp[:, 1].unsqueeze(3), [P, NT, HEADS, NE]), ALU.mult))
            step(V.tensor_tensor(agg, agg, bc(gat_par[:, 0:1, :], [P, NT, HK]), ALU.add))
            mean, var, sd2, rs2 = (n_tmp[:, 7, :, i] for i in (0, 1, 3, 2))
            step(V.tensor_reduce(mean, agg, AX.X, ALU.add))
            step(V.tensor_scalar(mean, mean, 1.0 / HK, None, ALU.mult))
            step(V.tensor_tensor(agg, agg, bc(mean.unsqueeze(2), [P, NT, HK]), ALU.subtract))
            step(V.tensor_tensor(dev, agg, agg, ALU.mult))
            step(V.tensor_reduce(var, dev, AX.X, ALU.add))
            V.tensor_scalar(var, var, 1.0 / HK, None, ALU.mult).then_inc(nd_q, 1)
            dve.wait_ge(nd_act, 2)
            step(V.reciprocal(rs2, sd2))
            step(V.tensor_tensor(agg, agg, bc(rs2.unsqueeze(2), [P, NT, HK]), ALU.mult))
            step(V.tensor_tensor(agg, agg, bc(gat_par[:, 1:2, :], [P, NT, HK]), ALU.mult))
            step(V.tensor_tensor(agg, agg, bc(gat_par[:, 2:3, :], [P, NT, HK]), ALU.add))
            score, rank, top = n_tmp[:, 0], n_tmp[:, 1], n_tmp[:, 7, :, 0]
            step(V.tensor_reduce(score, agg.rearrange("p t (h k) -> p t k h", k=NE), AX.X, ALU.add))
            step(V.tensor_scalar(score, score, 1.0 / HEADS, None, ALU.mult), V.memset(rank, 0.0))
            beats = n_tmp[:, 3, :, 0]
            for j in range(NE):
                for i in range(j + 1, NE):
                    step(V.tensor_tensor(beats, score[:, :, j], score[:, :, i], ALU.is_ge))
                    step(V.tensor_tensor(rank[:, :, i], rank[:, :, i], beats, ALU.add),
                         V.scalar_tensor_tensor(out=rank[:, :, j], in0=rank[:, :, j], scalar=1.0, in1=beats,
                                                op0=ALU.add, op1=ALU.subtract))
            step(V.tensor_reduce(top, score, AX.X, ALU.max))
            V.tensor_tensor(n_tmp[:, 2], score, bc(top.unsqueeze(2), [P, NT, NE]), ALU.subtract).then_inc(nd_q, 1)
            dve.wait_ge(nd_act, 3)
            step(V.tensor_scalar(rank, rank, 1.5, None, ALU.is_lt))
            step(V.tensor_tensor(n_tmp[:, 2], n_tmp[:, 2], rank, ALU.mult))
            step(V.tensor_reduce(top, n_tmp[:, 2], AX.X, ALU.add))
            step(V.reciprocal(mean_r(n_tmp), top))
            step(V.tensor_tensor(gates[:, :, :], n_tmp[:, 2], bc(mean_r(n_tmp).unsqueeze(2), [P, NT, NE]), ALU.mult))

            def combine(t, n, s, i, steps):
                dve.wait_ge(fy_in[s], 16 * (i + 1))
                for e in range(NE):
                    ops = []
                    for k in range(n):
                        acc = x_all[:, bass.ds(t + k, 1), :].rearrange("p a d -> p (a d)")
                        gate = gates[:, bass.ds(t + k, 1), e:e + 1].rearrange("p a e -> p (a e)")
                        ops.append(V.scalar_tensor_tensor(out=acc, in0=y_in[s][:, k, e, :], scalar=gate, in1=acc,
                                                          op0=ALU.mult, op1=ALU.add))
                    if e < NE - 1:
                        steps(*ops)
                ops[-1].then_inc(fo_rdy, 1)

            dve.wait_ge(fx_in, 16)
            per = YS * (NE - 1) * YT
            with dve.Fori(0, YL) as i:
                loop = Loop(dv, chain[0], i)
                for s in range(YS):
                    combine((YS * i + s) * YT, YT, s, i, lambda *ops: loop.step(per, *ops))
                assert loop.n == per
            chain[0] += YL * per
            combine(YL * YS * YT, 1, 0, YL, step)


def iota20(iota_row):
    return iota_row[0:20, :]


def mean_r(n_tmp):
    return n_tmp[:, 7, :, 2]


def plan_steps():
    work = [("keys", 0, 0)]
    cur = 0
    for k, j in STAGES:
        if (j >= FLOG and j == k - 1) or (j == FLOG - 1 and k > FLOG):
            work.append(("turn", 0, cur))
        work.append(("stage", k, j))
        cur = 1 - cur
    work += [("hist", c, 0) for c in range(FC // HIST_CH)]
    work += [("bias", g, 0) for g in range(NG)]
    work += [("cum", 0, 0)]
    steps, room = [[]], BUDGET
    for kind, a, b in work:
        took = {"keys": 8.0, "bias": 2.5, "turn": 4.0, "stage": 1.4, "hist": 3.4, "cum": 5.0, "marks": 8.0}[kind]
        if took > room and steps[-1]:
            steps.append([])
            room = BUDGET
        steps[-1].append((kind, a, b))
        room -= took
    fetch = (len(steps) - 1) // 2 + 2
    while len(steps) < 2 * fetch + 1:
        steps.append([])
    steps.append([("marks", 0, 0)])
    if len(steps) % 2:
        steps.append([])
    assert len(steps) < GG
    return steps, fetch


STEPS, FETCH = plan_steps()


DEBUG = ()


def kernel(x, src, dst, edge_weight, L0_gnn_Wp, L0_gnn_bp, L0_gnn_W1, L0_gnn_b1, L0_gnn_W2, L0_gnn_b2, L0_ffn_W_gat,
           L0_ffn_att_src, L0_ffn_att_dst, L0_ffn_b_gat, L0_ffn_ln_gamma, L0_ffn_ln_beta, L0_ffn_W1, L0_ffn_b1,
           L0_ffn_W2, L0_ffn_b2, L0_ffn_edge_index):
    import numpy as np
    import concourse.bacc as bacc
    from concourse.bass_utils import run_bass_kernel_spmd as run

    nc = bacc.Bacc("TRN2", target_bir_lowering=False, num_devices=1)
    tail = GG * EGN - EG
    pad_e = lambda a: np.pad(np.asarray(a), (0, tail), mode="edge").reshape(GG, EGN)
    edges = np.asarray(L0_ffn_edge_index)
    arrays = {
        "x": np.pad(np.asarray(x), ((0, NP - N), (0, 0))),
        "gsrc": pad_e(src), "gdst": pad_e(dst),
        "gw": np.pad(np.asarray(edge_weight), (0, tail)).reshape(GG, EGN),
        "WpT": np.asarray(L0_gnn_Wp).T, "bp": L0_gnn_bp, "W1T": np.asarray(L0_gnn_W1).T, "b1": L0_gnn_b1,
        "W2T": np.asarray(L0_gnn_W2).T, "b2": L0_gnn_b2, "Wgat": L0_ffn_W_gat, "att_src": L0_ffn_att_src,
        "att_dst": L0_ffn_att_dst, "b_gat": L0_ffn_b_gat, "ln_gamma": L0_ffn_ln_gamma, "ln_beta": L0_ffn_ln_beta,
        "mW1": L0_ffn_W1, "mb1": np.asarray(L0_ffn_b1).reshape(NE * FB, P).T, "mW2": L0_ffn_W2,
        "mb2": np.asarray(L0_ffn_b2).reshape(NE * D),
        "fsrc": edges[0].reshape(P, FC), "fdst": edges[1].reshape(P, FC),
    }
    arrays = {k: np.ascontiguousarray(v) for k, v in arrays.items()}
    args = [nc.dram_tensor(k, v.shape, mybir.dt.from_np(v.dtype), kind="ExternalInput").ap() for k, v in arrays.items()]
    out = nc.dram_tensor("out", (N, D), F32, kind="ExternalOutput").ap()
    gnn_ffn(nc, *args, out, DEBUG)
    r = run(nc, [arrays], core_ids=[0])
    return r.results[0]["out"]
```

```python
from contextlib import ExitStack

import concourse.bass as bass
from concourse import mybir

F32 = mybir.dt.float32
I32 = mybir.dt.int32
BF16 = mybir.dt.bfloat16
ALU = mybir.AluOpType
ACT = mybir.ActivationFunctionType
AX = mybir.AxisListType

P = 128
N = 6250
NT = 49
NP = NT * P
D = 256
KD = D // P
GT = 7
NG = NT // GT
X_FIRST = 3
GN = GT * P
HN = GN // 2
EG = 106250
ET = 8
EGN = ET * P
GG = 104
EF = 131072
FC = EF // P
FLOG = 10
ELOG = 17
DST_BITS = 13
CH = 32
NCH = FC // CH
HEADS = 4
NE = 4
HK = HEADS * NE
RW = 24
HID = 512
FB = HID // P
MB = 448
NMB = NP // MB
MQ = 112
QB = MB // MQ
AHEAD = 4
YT = 4
YS = 4
YL = NT // (YT * YS)
NODE_PARTS = (slice(0, YT * YS), slice(YT * YS, NT))
CR = 40
TRASH = 8192
LN_EPS = 1e-5
BIG = 1e30
KEY_TOP = 0x40000000

STAGES = [(k, j) for k in range(1, ELOG + 1) for j in range(k - 1, -1, -1)]
BUDGET = 7.0
HIST_CH = 16


def gnn_ffn(nc, x, gsrc, gdst, gw, WpT, bp, W1T, b1, W2T, b2, Wgat, att_src, att_dst, b_gat,
            ln_gamma, ln_beta, mW1, mb1, mW2, mb2, fsrc, fdst, out, debug):
    ctx = ExitStack()
    with ctx:
        def sb(name, shape, dt=F32):
            return ctx.enter_context(nc.sbuf_tensor(name, shape, dt))

        def sem(name):
            return ctx.enter_context(nc.semaphore(name))

        def dram(name, shape, dt=F32):
            kind = "ExternalOutput" if debug and name in debug else "Internal"
            return nc.dram_tensor(name, shape, dt, kind=kind).ap()

        hp_tab = dram("hp_tab", (NP, P))
        x2_tab = dram("x2_tab", (NP, D))
        src_tab = dram("src_tab", (NP, RW))
        adst_tab = dram("adst_tab", (TRASH, HEADS))
        adst_edge = dram("adst_edge", (EF + NP, HEADS))
        rec_tab = dram("rec_tab", (EF, RW))
        carry_tab = dram("carry_tab", (TRASH + P, CR))
        y_tab = dram("y_tab", (NP, NE * D))
        key_tab = dram("key_tab", (EF,))
        key_rows = dram("key_rows", (P, FC))

        big_x = sb("big_x", [P, NT * D])
        big_t = sb("big_t", [P, KD * NP])
        big_h = sb("big_h", [P, 2 * NP + P])
        ring = sb("ring", [P, 4 * EGN])

        def carve(whole, at, n):
            return whole[:, at:at + n]

        x_all = big_x[:, :].rearrange("p (t d) -> p t d", d=D)
        hT = big_h[:, 0:NP]
        aggT = big_h[:, NP:2 * NP + P]
        xn2T = big_t[:, :].rearrange("p (k n) -> p k n", k=KD)
        xn = ring[:, 0:GT * D].rearrange("p (t d) -> p t d", d=D)
        xn_s = [ring[:, i * GT * D:(i + 1) * GT * D].rearrange("p (t d) -> p t d", d=D) for i in range(2)]
        featT = ring[0:HK, GT * D:GT * D + GN]
        g_ring = ring[:, 0:2 * EGN].rearrange("p (h j f) -> p h j f", h=2, j=ET)
        oh_ring = ring[:, 2 * EGN:4 * EGN].rearrange("p (h j f) -> p h j f", h=2, j=ET)
        xnT = carve(big_t, 0, GT * D).rearrange("p (k n) -> p k n", k=KD)
        mv_x = carve(big_t, 10 * FC, 2 * NT).rearrange("p (t s) -> p t s", s=2)
        sd_x, rs_x = (carve(big_t, 10 * FC + i * NT, NT) for i in (2, 3))
        keys = [carve(big_t, i * FC, FC) for i in range(2)]
        e_src = carve(big_t, 2 * FC, FC).bitcast(I32)
        e_dst = carve(big_t, 3 * FC, FC).bitcast(I32)
        g_src = carve(big_t, 4 * FC, EGN).bitcast(I32)
        g_dst = carve(big_t, 5 * FC, EGN).bitcast(I32)
        g_w = carve(big_t, 6 * FC, EGN)
        g_srcf = carve(big_t, 7 * FC, EGN)
        g_dstf = carve(big_t, 8 * FC, EGN)
        half_i = carve(big_t, 10 * FC, FC).bitcast(I32)
        rows_f = carve(big_t, 10 * FC + 256, P)[0:1]
        row_at = carve(big_t, 10 * FC - P, P).bitcast(I32)[0:1]
        lo_bf = carve(big_t, 11 * FC, FC // 2).bitcast(BF16)
        hi_bf = carve(big_t, 11 * FC + FC // 2, FC // 2).bitcast(BF16)
        oh_lo = carve(big_t, 4 * FC, HIST_CH * P).bitcast(BF16).rearrange("p (s t c) -> p s t c", s=2, c=P)
        oh_hi = carve(big_t, 8 * FC, HIST_CH * 64).bitcast(BF16).rearrange("p (s t c) -> p s t c", s=2, c=64)
        b12 = carve(big_t, 6 * FC, 2 * D).rearrange("p (s d) -> p s d", s=2)
        s_dst = carve(big_t, 4 * FC, FC)
        was_equal = carve(big_t, 5 * FC, FC)
        w1m = carve(big_x, 0, 4096).rearrange("p (e k f) -> p e k f", e=NE, k=KD)
        w2m = carve(big_x, 4096, 4096).rearrange("p (e f d) -> p e f d", e=NE, f=FB)
        hid = carve(big_x, 8192, 2 * FB * MB).rearrange("p (s f n) -> p s f n", s=2, f=FB)
        b2_parts = carve(big_x, 8192 + 2 * FB * MB, NE * D // 2).bitcast(BF16)[0:3].rearrange("p (e d) -> p e d", e=NE)
        a_edge = carve(big_h, 0, HEADS * FC).rearrange("p (t h) -> p t h", h=HEADS)
        at = HEADS * FC
        rec_in = carve(big_h, at, 2 * CH * RW).rearrange("p (s t c) -> p s t c", s=2, c=RW)
        at += 2 * CH * RW
        rec_out = carve(big_h, at, 2 * CH * RW).rearrange("p (s t c) -> p s t c", s=2, c=RW)
        at += 2 * CH * RW
        b2_rest = carve(big_h, at - 2 * CH * RW, NE * D)[0:3].rearrange("p (e d) -> p e d", e=NE)
        b2_part = carve(big_h, at - 2 * CH * RW + NE * D, NE * D // 2).bitcast(BF16)[0:3].rearrange("p (e d) -> p e d", e=NE)
        z1 = carve(big_h, at, CH * 4).rearrange("p (t h) -> p t h", h=HEADS)
        at += CH * 4
        z2 = carve(big_h, at, CH * 4).rearrange("p (t h) -> p t h", h=HEADS)
        at += CH * 4
        dq = carve(big_h, at, CH * 8).rearrange("p (q t h) -> p q t h", q=2, h=HEADS)
        at += CH * 8
        vals = carve(big_h, at, CH * 20).rearrange("p (t h k) -> p t h k", h=HEADS, k=5)
        at += CH * 20
        not_start = carve(big_h, at, FC)
        y_sb = ring[0:MQ, 0:4 * NE * D].rearrange("p (q e d) -> p q e d", q=QB, e=NE)
        at += FC
        node_r = carve(big_h, at, NT * RW).rearrange("p (t c) -> p t c", c=RW)
        at += NT * RW
        node_c = carve(big_h, at, NT * CR).rearrange("p (t c) -> p t c", c=CR)
        assert at + NT * CR <= 2 * NP + P
        y_in = [carve(big_t, i * YT * NE * D, YT * NE * D) for i in range(3)] + [ring[:, :]]
        y_in = [y.rearrange("p (t e d) -> p t e d", t=YT, e=NE) for y in y_in]
        at = 0
        last = carve(big_h, at, 4 * 20).rearrange("p (s c) -> p s c", c=20)
        at += 80
        carried = carve(big_h, at, 60)
        at += 60
        rowt = carve(big_h, at, 12 * P).rearrange("p (s c) -> p s c", c=P)
        at += 12 * P
        s_tmp = carve(big_h, at, NT * 20).rearrange("p (t h k) -> p t h k", h=HEADS, k=5)
        at += NT * 20
        n_tmp = carve(big_h, at, 8 * NT * 4).rearrange("p (s t h) -> p s t h", s=8, h=4)
        at += 8 * NT * 4
        n16 = carve(big_h, at, 2 * NT * HK).rearrange("p (s t c) -> p s t c", s=2, c=HK)
        at += 2 * NT * HK
        gates = carve(big_h, at, NT * NE).rearrange("p (t e) -> p t e", e=NE)

        ident = sb("ident", [P, P])
        lower = sb("lower", [P, P])
        ones = sb("ones", [P, P])
        iota_row = sb("iota_row", [P, P])
        iota_bf = sb("iota_bf", [P, P], BF16)
        part_i = sb("part_i", [P, 1], I32)
        sgn_i = sb("sgn_i", [P, 8], I32)
        sgn = sb("sgn", [P, 8])
        eps = sb("eps", [P, 1])
        zeros = sb("zeros", [P, 256])
        no_edge = sb("no_edge", [P, CR])
        wp_sb = sb("wp_sb", [P, KD, P])
        bp_sb = sb("bp_sb", [P, 1])
        w1_sb = sb("w1_sb", [P, D])
        w2_sb = sb("w2_sb", [P, D])
        wg_sb = sb("wg_sb", [P, KD, HK])
        att = sb("att", [P, 2, HK])
        gat_par = sb("gat_par", [P, 3, HK])
        b1m = sb("b1m", [P, NE * FB])
        b2m = sb("b2m", [3, NE, D])
        ones_bf = sb("ones_bf", [3, MQ], BF16)

        g_cols = sb("g_cols", [P, 3, GG * ET])
        srcT = g_cols[:, 0, :].bitcast(I32).rearrange("p (g j) -> p g j", j=ET)
        relT = g_cols[:, 1, :].rearrange("p (g j) -> p g j", j=ET)
        wT = g_cols[:, 2, :].rearrange("p (g j) -> p g j", j=ET)
        h_now = carve(big_t, 9 * FC, GN)
        h_now2 = g_cols[:, :, :].rearrange("p a n -> p (a n)")[:, 0:GN]
        att_tmp = g_cols[:, :, :].rearrange("p a n -> p (a n)")[:, GN:GN + GT * HK].rearrange("p (t c) -> p t c", c=HK)
        spread = sb("spread", [P, 4])
        base_row = sb("base_row", [1, 2, GG], I32)
        base_f = sb("base_f", [1, GG])
        base_all = sb("base_all", [P, GG])
        far = sb("far", [1, 1], I32)
        far_cols = sb("far_cols", [P, 2, ET])
        g_idx = sb("g_idx", [P, 2, 2 * ET], I32)

        s_src = sb("s_src", [P, FC], I32)
        ends = sb("ends", [P, 2])
        row_len = sb("row_len", [P, 4])
        row_i = sb("row_i", [P, 2], I32)
        run = sb("run", [P, RW])
        pen = sb("pen", [P, FC])
        f_idx = sb("f_idx", [P, 2, CH], I32)
        first_idx = sb("first_idx", [P, 1], I32)
        cum = sb("cum", [P, 6, 64])
        has = sb("has", [P, NT])
        e_idx = sb("e_idx", [P, NT], I32)
        st_idx = sb("st_idx", [P, NT], I32)
        carry_idx = sb("carry_idx", [P, 1], I32)
        a_first = sb("a_first", [P, HEADS])

        st6 = sb("st6", [P, GT, 6])
        mv = sb("mv", [P, GT, 2])
        sd = sb("sd", [P, GT])
        rs = sb("rs", [P, GT])
        nm = sb("nm", [P, GT])
        hp_sb = sb("hp_sb", [P, GT, P])
        iota_i = hp_sb[:, 0, :].bitcast(I32)
        tab = sb("tab", [P, NT, RW])
        adst = sb("adst", [P, NT, HEADS])

        ps = ctx.enter_context(nc.psum_tensor("ps", [P, 8, 512], F32))
        flat = ps[:, :, :].rearrange("p b n -> p (b n)")

        x_ld = [sem(f"x_ld{i}") for i in range(2)]
        clear, hT_cp = sem("clear"), sem("hT_cp")
        par_in, ge_in, fe_in = sem("par_in"), sem("ge_in"), sem("fe_in")
        pool_c, dv, consts = sem("pool_c"), sem("dv"), sem("consts")
        ln_mv, ln_sd, ln_xn = sem("ln_mv"), sem("ln_sd"), sem("ln_xn")
        tp_done, tp_ev = sem("tp_done"), sem("tp_ev")
        h_mm, h_ev, hb_mm, hb_ev, hp_out = sem("h_mm"), sem("h_ev"), sem("hb_mm"), sem("hb_ev"), sem("hp_out")
        cols_ev = sem("cols_ev")
        rel_rdy, ge_tp, ge_ev = sem("rel_rdy"), sem("ge_tp"), sem("ge_ev")
        far_idx, far_gath, far_oh, far_mm, far_add, agg_done = (sem("far_idx"), sem("far_gath"), sem("far_oh"),
                                                                sem("far_mm"), sem("far_add"), sem("agg_done"))
        idx_cp, oh_rdy, mm_done, add_done = sem("idx_cp"), sem("oh_rdy"), sem("mm_done"), sem("add_done")
        gath = [sem(f"gath{i}") for i in range(2)]
        key_rdy, key_tp = sem("key_rdy"), sem("key_tp")
        key_cp = sem("key_cp")
        counted, blank = sem("counted"), sem("blank")
        key_end, key_st, len_mm, len_rdy, fetched = (sem("key_end"), sem("key_st"), sem("len_mm"), sem("len_rdy"),
                                                     sem("fetched"))
        chunk_dv = sem("chunk_dv")
        hist_rdy, hist_mm, cum_rdy, cum_mm = sem("hist_rdy"), sem("hist_mm"), sem("cum_rdy"), sem("cum_mm")
        ends_rdy, sorted_s = sem("ends_rdy"), sem("sorted_s")
        sq_done, o_mm, x2_rdy, x2_out = sem("sq_done"), sem("o_mm"), sem("x2_rdy"), sem("x2_out")
        t2_done, t2_ev, g_mm, tab_rdy, tab_out = sem("t2_done"), sem("t2_ev"), sem("g_mm"), sem("tab_rdy"), sem("tab_out")
        zero_rdy, zero_out, a_scat, a_in, af_in = sem("zero_rdy"), sem("zero_out"), sem("a_scat"), sem("a_in"), sem("af_in")
        fidx_cp = sem("fidx_cp")
        feat_tp = sem("feat_tp")
        bias_in, ln_rs, h_cp, feat_ev = sem("bias_in"), sem("ln_rs"), sem("h_cp"), sem("feat_ev")
        fgath = [sem(f"fgath{i}") for i in range(2)]
        q_rdy, ex_done, sc_done, in_free = sem("q_rdy"), sem("ex_done"), sem("sc_done"), sem("in_free")
        rec_st = [sem(f"rec_st{i}") for i in range(2)]
        mw_in, up_mm, gelu_done, dn_mm, y_ev, y_st = (sem("mw_in"), sem("up_mm"), sem("gelu_done"), sem("dn_mm"),
                                                      sem("y_ev"), sem("y_st"))
        r_in = [sem(f"r_in{i}") for i in range(2)]
        last_rdy, last_tp, row_q, row_ex, back_rdy, back_tp = (
            sem("last_rdy"), sem("last_tp"), sem("row_q"), sem("row_ex"), sem("back_rdy"), sem("back_tp"))
        b2_rdy = sem("b2_rdy")
        c_rdy, c_scat, c_in, nd_q, nd_act = sem("c_rdy"), sem("c_scat"), sem("c_in"), sem("nd_q"), sem("nd_act")
        fy_in = [sem(f"fy_in{i}") for i in range(YS)]
        fx_in, fo_rdy, fo_out = sem("fx_in"), sem("fo_rdy"), sem("fo_out")

        scrap = sb("scrap", [P, 5])

        def apart(eng, to=0):
            if eng.engine == nc.gpsimd.engine:
                eng.tensor_tensor(scrap[:, to:to + 1], ones[:, 0:1], ones[:, 0:1], ALU.mult)
            else:
                eng.memset(scrap[:, 1:2], 0.0)

        def after(eng, sem_, n):
            if not isinstance(n, int) or n > 0:
                eng.wait_ge(sem_, n)

        block = ctx.enter_context(nc.Block())

        N_PAR = 12

        @block.sync
        def _(sp):
            sp.dma_start(g_src[0:GG, :], gsrc).then_inc(ge_in, 16)
            sp.dma_start(g_dst[0:GG, :], gdst).then_inc(ge_in, 16)
            sp.dma_start(g_w[0:GG, :], gw).then_inc(ge_in, 16)
            for g in range(NG):
                sp.dma_start(x_all[:, g * GT:(g + 1) * GT, :],
                             x[g * GN:(g + 1) * GN, :].rearrange("(t p) d -> p t d", p=P)
                             ).then_inc(x_ld[0 if g < X_FIRST else 1], 16)
            sp.dma_start(wp_sb[:, :, :], WpT.rearrange("(k p) f -> p k f", p=P)).then_inc(par_in, 16)
            sp.dma_start(bp_sb[:, :], bp.rearrange("(p a) -> p a", a=1)).then_inc(par_in, 16)
            sp.dma_start(w1_sb[:, :], W1T).then_inc(par_in, 16)
            sp.dma_start(w2_sb[:, :], W2T).then_inc(par_in, 16)
            sp.dma_start(wg_sb[:, :, :], Wgat.rearrange("(k p) f -> p k f", p=P)).then_inc(par_in, 16)
            sp.dma_start(att[:, 0, :], att_src.rearrange("h e -> (h e)").partition_broadcast(P)).then_inc(par_in, 16)
            sp.dma_start(att[:, 1, :], att_dst.rearrange("h e -> (h e)").partition_broadcast(P)).then_inc(par_in, 16)
            sp.dma_start(gat_par[:, 0, :], b_gat.partition_broadcast(P)).then_inc(par_in, 16)
            sp.dma_start(gat_par[:, 1, :], ln_gamma.partition_broadcast(P)).then_inc(par_in, 16)
            sp.dma_start(gat_par[:, 2, :], ln_beta.partition_broadcast(P)).then_inc(par_in, 16)
            sp.dma_start(b1m[:, :], mb1).then_inc(par_in, 16)
            sp.dma_start(b2m[:, :, :].rearrange("p e d -> p (e d)"), mb2.partition_broadcast(3)).then_inc(par_in, 16)
            sp.dma_start(e_src, fsrc).then_inc(fe_in, 16)
            sp.dma_start(e_dst, fdst).then_inc(fe_in, 16)
            sp.wait_ge(zero_rdy, 1)
            zero_reps = EF * HEADS // P // 256
            sp.dma_start(adst_edge[0:EF, :].rearrange("(p r t) h -> p r (t h)", p=P, r=zero_reps),
                         zeros[:, :].unsqueeze(1).broadcast_to([P, zero_reps, 256])).then_inc(zero_out, 16)
            sp.dma_start(adst_tab[NP:TRASH, :].rearrange("(p t) h -> p (t h)", p=P),
                         zeros[:, 0:(TRASH - NP) * HEADS // P]).then_inc(zero_out, 16)
            sp.dma_start(carry_tab[0:NP, :].rearrange("(p t) c -> p t c", p=P),
                         no_edge[:, :].unsqueeze(1).broadcast_to([P, NT, CR])).then_inc(zero_out, 16)
            sp.wait_ge(cols_ev, 3)
            sp.dma_start(b12[:, 0, :], b1.partition_broadcast(P)).then_inc(bias_in, 16)
            sp.dma_start(b12[:, 1, :], b2.partition_broadcast(P)).then_inc(bias_in, 16)
            with sp.Fori(0, NG) as g:
                sp.wait_ge(hb_ev, g + 1)
                sp.dma_start(hp_tab[bass.ds(g * GN, GN), :].rearrange("(t p) f -> p t f", p=P),
                             hp_sb[:, :, :]).then_inc(hp_out, 16)
            rec_v = rec_tab.rearrange("(p t) c -> p (t c)", p=P)
            sp.wait_ge(len_rdy, 1)
            chunks = sp.value_load(row_i[0:1, 0:1], min_val=2, max_val=NCH)
            with sp.Fori(2, NCH) as c:
                with sp.If(chunks <= c):
                    sp.dma_start(rec_v[:, bass.ds(c * CH * RW, CH * RW)].rearrange("p (r n) -> p r n", n=256),
                                 zeros[:, :].unsqueeze(1).broadcast_to([P, CH * RW // 256, 256])).then_inc(blank, 16)
                with sp.If(chunks > c):
                    sp.dma_start(rec_v[0:1, bass.ds(c * CH * RW, RW)], zeros[0:1, 0:RW]).then_inc(blank, 16)
            for s in range(2):
                sp.dma_start(rec_v[0:1, s * CH * RW:s * CH * RW + RW], zeros[0:1, 0:RW]).then_inc(rec_st[s], 16)
            sp.wait_ge(key_end, 1)
            sp.dma_start(key_tab.rearrange("(p t) -> p t", p=P), keys[len(STAGES) % 2]).then_inc(key_st, 16)
            sp.wait_ge(key_st, 16)
            with sp.Fori(0, P) as p:
                start = sp.value_load(row_at[:, bass.ds(p, 1)], min_val=0, max_val=EF - FC)
                sp.dma_start(key_rows[bass.ds(p, 1), :], key_tab[bass.ds(start, FC)].rearrange("(a n) -> a n", a=1)
                             ).then_inc(key_cp, 16)
            sp.wait_ge(key_cp, 16 * P)
            sp.dma_start(keys[1 - len(STAGES) % 2], key_rows).then_inc(fetched, 16)
            with sp.Fori(0, NG) as g:
                rows = bass.ds(g * GN, GN)
                tiles = bass.ds(g * GT, GT)
                sp.wait_ge(x2_rdy, g + 1)
                sp.dma_start(x2_tab[rows, :].rearrange("(t p) d -> p t d", p=P), x_all[:, tiles, :]).then_inc(x2_out, 16)
                sp.wait_ge(tab_rdy, g + 1)
                sp.dma_start(src_tab[rows, :].rearrange("(t p) c -> p t c", p=P), tab[:, tiles, :]).then_inc(tab_out, 16)
                sp.dma_start(adst_tab[rows, :].rearrange("(t p) c -> p t c", p=P), adst[:, tiles, :]).then_inc(tab_out, 16)
            sp.wait_ge(x2_out, 16 * NG)
            sp.dma_start(w1m, mW1.rearrange("e (k p) f -> p e k f", p=P)).then_inc(mw_in, 16)
            sp.dma_start(w2m, mW2.rearrange("e (f p) d -> p e f d", p=P)).then_inc(mw_in, 16)
            sp.wait_ge(a_scat, 16 * NT)
            sp.dma_start(a_edge, adst_edge[0:EF, :].rearrange("(p t) h -> p t h", p=P)).then_inc(a_in, 16)
            y_v = y_tab.rearrange("(b q p) n -> b p q n", q=QB, p=MQ)

            def store_records(i, s):
                sp.wait_ge(sc_done, 2 * i + s + 1)
                sp.dma_start(rec_v[:, bass.ds((2 * i + s) * CH * RW, CH * RW)],
                             rec_out[:, s, :, :].rearrange("p t c -> p (t c)")).then_inc(rec_st[s], 16)

            sp.wait_ge(blank, 16 * (NCH - 2))
            with sp.Fori(0, NCH // 2) as i:
                for s in range(2):
                    with sp.If(chunks > 2 * i + s):
                        store_records(i, s)
            sp.wait_ge(dn_mm, NMB * NE * QB)
            sp.dma_start(x_all, x2_tab.rearrange("(t p) d -> p t d", p=P)).then_inc(fx_in, 16)

            def load_y(t, n, s):
                sp.dma_start(y_in[s][:, 0:n].rearrange("p t e d -> p t (e d)"),
                             y_tab[bass.ds(t * P, n * P), :].rearrange("(t p) n -> p t n", p=P)).then_inc(fy_in[s], 16)

            sp.wait_ge(y_st, 16 * NMB)
            load_y(0, YT, 0)
            sp.wait_ge(c_scat, 16)
            sp.dma_start(node_c, carry_tab[0:NP, :].rearrange("(t p) c -> p t c", p=P)).then_inc(c_in, 16)

            for s in range(1, YS):
                load_y(s * YT, YT, s)
            with sp.Fori(1, YL) as i:
                for s in range(YS):
                    sp.wait_ge(fo_rdy, YS * i + s - YS + 1)
                    load_y((YS * i + s) * YT, YT, s)
            sp.wait_ge(fo_rdy, YS * (YL - 1) + 1)
            load_y(YL * YS * YT, 1, 0)
            sp.wait_ge(fo_out, 16 * (YL * YS + 1))

        @block.gpsimd
        def _(pool):
            pool.memset(ident[:, :], 0.0).then_inc(pool_c, 1)
            pool.memset(lower[:, :], 1.0).then_inc(pool_c, 1)
            pool.iota(iota_i, [[1, P]], base=0, channel_multiplier=0).then_inc(pool_c, 1)
            pool.iota(part_i[:, :], [[0, 1]], base=0, channel_multiplier=1).then_inc(pool_c, 1)
            pool.wait_ge(pool_c, 4)
            pool.affine_select(out=ident[:, :], in_=ident[:, :], compare_op=ALU.not_equal, fill=1.0,
                               base=0, pattern=[[-1, P]], channel_multiplier=1).then_inc(pool_c, 1)
            pool.affine_select(out=lower[:, :], in_=lower[:, :], compare_op=ALU.is_gt, fill=0.0,
                               base=0, pattern=[[1, P]], channel_multiplier=-1).then_inc(pool_c, 1)

            pool.memset(aggT, 0.0).then_inc(clear, 1)
            pool.memset(tab[:, :, :], 1.0).then_inc(clear, 1)
            with pool.Fori(0, NG) as g:
                pool.wait_ge(h_ev, g + 1)
                pool.tensor_copy(hT[:, bass.ds(g * GN, GN)], h_now).then_inc(hT_cp, 1)

            def gather_pair(p, h, first):
                for s in range(2):
                    if not first:
                        pool.wait_ge(mm_done, 2 * p + s - 1)
                        if s == 1:
                            apart(pool, 4)
                    if s == 0:
                        pool.tensor_copy(g_idx[:, h, :], srcT[:, bass.ds(2 * p, 2), :].rearrange("p a j -> p (a j)")
                                         ).then_inc(idx_cp, 1)
                        pool.wait_ge(idx_cp, p + 1)
                        apart(pool)
                    for j in range(ET):
                        pool.indirect_dma_start(out=g_ring[:, s, j, :], out_offset=None, in_=hp_tab,
                                                in_offset=bass.IndirectOffsetOnAxis(
                                                    ap=g_idx[:, h, s * ET + j:s * ET + j + 1], axis=0)
                                                ).then_inc(gath[s], 16)

            pool.wait_ge(consts, 1)
            pool.wait_ge(cols_ev, 3)
            pool.wait_ge(ge_ev, 2)
            pool.wait_ge(hp_out, 16 * NG)
            gather_pair(0, 0, True)
            with pool.Fori(0, (GG // 2 - 2) // 2) as i:
                for k in (1, 2):
                    gather_pair(2 * i + k, k % 2, False)
            gather_pair(GG // 2 - 1, 1, False)

            with pool.If(pool.value_load(far[0:1, 0:1], min_val=0, max_val=1) > 0):
                pool.wait_ge(mm_done, GG)
                with pool.Fori(0, GG) as g:
                    pool.tensor_copy(g_idx[:, 0, 0:ET], srcT[:, bass.ds(g, 1), :].rearrange("p a j -> p (a j)")).then_inc(far_idx, 1)
                    pool.wait_ge(far_idx, g + 1)
                    apart(pool)
                    for j in range(ET):
                        pool.indirect_dma_start(out=g_ring[:, 0, j, :], out_offset=None, in_=hp_tab,
                                                in_offset=bass.IndirectOffsetOnAxis(ap=g_idx[:, 0, j:j + 1], axis=0)
                                                ).then_inc(far_gath, 16)
                    pool.wait_ge(far_mm, (g + 1) * NT)
                    apart(pool, 4)

            def copy_h(g):
                after(pool, o_mm, g)
                pool.tensor_copy(h_now2, hT[:, bass.ds(g * GN, GN)]).then_inc(h_cp, 1)

            def scatter_logits(g):
                pool.wait_ge(tab_rdy, g + 1)
                for t in range(g * GT, (g + 1) * GT):
                    pool.indirect_dma_start(out=adst_edge, out_offset=bass.IndirectOffsetOnAxis(ap=st_idx[:, t:t + 1], axis=0),
                                            in_=adst[:, t, :], in_offset=None).then_inc(a_scat, 16)

            pool.wait_ge(agg_done, 1)
            pool.wait_ge(sorted_s, 1)
            pool.wait_ge(zero_out, 48)
            for g in range(NG):
                copy_h(g)
                if g >= 3:
                    scatter_logits(g - 3)
            for g in range(NG - 3, NG):
                scatter_logits(g)

            def gather_chunk(c, s):
                pool.tensor_copy(f_idx[:, s, :], s_src[:, bass.ds(c * CH, CH)]).then_inc(fidx_cp, 1)
                pool.wait_ge(fidx_cp, c + 1)
                apart(pool)
                for j in range(CH):
                    pool.indirect_dma_start(out=rec_in[:, s, j, :], out_offset=None, in_=src_tab,
                                            in_offset=bass.IndirectOffsetOnAxis(ap=f_idx[:, s, j:j + 1], axis=0)
                                            ).then_inc(fgath[s], 16)

            pool.wait_ge(tab_out, 32 * NG)
            pool.indirect_dma_start(out=a_first[:, :], out_offset=None, in_=adst_tab,
                                    in_offset=bass.IndirectOffsetOnAxis(ap=first_idx[:, :], axis=0)).then_inc(af_in, 16)
            for c in range(2):
                gather_chunk(c, c)
            chunks = pool.value_load(row_i[0:1, 0:1], min_val=2, max_val=NCH)
            with pool.Fori(1, NCH // 2) as i:
                for s in range(2):
                    with pool.If(chunks > 2 * i + s):
                        pool.wait_ge(in_free, 2 * i + s - 1)
                        gather_chunk(2 * i + s, s)

            pool.wait_ge(rec_st[0], 16 * (NCH // 2 + 1))
            pool.wait_ge(rec_st[1], 16 * (NCH // 2 + 1))
            for t in range(NT):
                pool.indirect_dma_start(out=node_r[:, t, :], out_offset=None, in_=rec_tab,
                                        in_offset=bass.IndirectOffsetOnAxis(ap=e_idx[:, t:t + 1], axis=0)
                                        ).then_inc(r_in[0 if t < YT * YS else 1], 16)
                if t == NT // 4:
                    pool.wait_ge(c_rdy, 1)
                    pool.indirect_dma_start(out=carry_tab, out_offset=bass.IndirectOffsetOnAxis(ap=carry_idx[:, :], axis=0),
                                            in_=carried[:, 0:CR], in_offset=None).then_inc(c_scat, 16)

        @block.scalar
        def _(act):
            for n, cols in enumerate((srcT, relT, wT)):
                act.wait_ge(ge_tp, n + 1)
                for h in range(2):
                    op = nc.scalar.activation(cols[:, :, 4 * h:4 * h + 4].rearrange("p g j -> p j g"),
                                              ps[:, 2 * n + h, 0:4 * GG].rearrange("p (j g) -> p j g", g=GG), ACT.Copy)
                op.then_inc(cols_ev, 1)
            act.wait_ge(consts, 1)
            act.wait_ge(par_in, 16 * N_PAR)
            act.wait_ge(ln_mv, 1)
            first, rest = slice(0, X_FIRST * GT), slice(X_FIRST * GT, NT)
            nc.scalar.activation(sd_x[:, first], mv_x[:, first, 1], ACT.Sqrt, bias=eps[:, :]).then_inc(ln_sd, 1)

            def keep_rows(g):
                act.wait_ge(tp_done, g + 1)
                after(act, h_mm, g)
                nc.scalar.activation(xnT[:, 0, :].rearrange("p (t n) -> p t n", n=P),
                                     flat[:, 0:GN].rearrange("p (t n) -> p t n", n=P),
                                     ACT.Copy).then_inc(tp_ev, 1)

            def relu(g):
                act.wait_ge(h_mm, g + 1)
                after(act, hT_cp, g)
                after(act, hb_mm, g)
                nc.scalar.activation(h_now.rearrange("p (b n) -> p b n", b=2), ps[:, 4:6, 0:HN],
                                     ACT.Relu, bias=bp_sb[:, :]).then_inc(h_ev, 1)

            def squares(g):
                act.wait_ge(hb_mm, g + 1)
                after(act, hp_out, 16 * g)
                nc.scalar.activation(hp_sb[:, :, :].rearrange("p t f -> p (t f)"), flat[:, 6 * 512:6 * 512 + GN],
                                     ACT.Square).then_inc(hb_ev, 1)

            keep_rows(0)
            relu(0)
            keep_rows(1)
            squares(0)
            relu(1)
            keep_rows(2)
            squares(1)
            act.wait_ge(ln_mv, 2)
            nc.scalar.activation(sd_x[:, rest], mv_x[:, rest, 1], ACT.Sqrt, bias=eps[:, :]).then_inc(ln_sd, 1)
            with act.Fori(2, NG - 1) as g:
                relu(g)
                keep_rows(g + 1)
                squares(g)
            relu(NG - 1)
            squares(NG - 1)

            def roots(g):
                after(act, o_mm, g)
                nc.scalar.activation(hp_sb[:, :, :].rearrange("p t f -> p (t f)"), aggT[:, bass.ds(g * GN, GN)],
                                     ACT.Sqrt).then_inc(sq_done, 1)

            def normalize(g):
                act.wait_ge(ln_mv, 3 + g)
                nc.scalar.activation(sd[:, :], mv[:, :, 1], ACT.Sqrt, bias=eps[:, :]).then_inc(ln_sd, 1)
                act.wait_ge(ln_rs, g + 1)
                after(act, t2_done, g)
                for t in range(GT):
                    op = nc.scalar.activation(xn[:, t, :], x_all[:, bass.ds(g * GT + t, 1), :].rearrange("p a d -> p (a d)"),
                                              ACT.Identity, bias=nm[:, t:t + 1], scale=rs[:, t:t + 1])
                op.then_inc(ln_xn, 1)

            def keep_turned(g):
                act.wait_ge(t2_done, g + 1)
                for k in range(KD):
                    op = nc.scalar.activation(xn2T[:, k, bass.ds(g * GN, GN)].rearrange("p (t n) -> p t n", n=P),
                                              flat[:, 2048 + 1024 * k:2048 + 1024 * k + GN].rearrange("p (t n) -> p t n", n=P),
                                              ACT.Copy)
                op.then_inc(t2_ev, 1)

            act.wait_ge(agg_done, 1)
            roots(0)
            roots(1)
            normalize(0)
            with act.Fori(1, NG - 1) as g:
                roots(g + 1)
                keep_turned(g - 1)
                normalize(g)
            keep_turned(NG - 2)
            normalize(NG - 1)
            keep_turned(NG - 1)

            def exps(c):
                act.wait_ge(q_rdy, c + 1)
                nc.scalar.activation(dq, dq, ACT.Exp).then_inc(ex_done, 1)

            def hidden(b, e):
                for f in range(FB):
                    act.wait_ge(up_mm, (b * NE + e) * FB + f + 1)
                    nc.scalar.activation(hid[:, e % 2, f, :], ps[:, f, 0:MB], ACT.Gelu,
                                         bias=b1m[:, e * FB + f:e * FB + f + 1]).then_inc(gelu_done, 1)

            def experts(b, chunk_at, end):
                for e in range(NE):
                    if e in chunk_at:
                        with act.If(chunks > chunk_at[e]):
                            exps(chunk_at[e])
                    if e < NE - 1:
                        hidden(b, e + 1)
                    elif not end:
                        hidden(b + 1, 0)
                    if e == 0:
                        after(act, y_st, 16 * b)
                    act.wait_ge(dn_mm, ((b * NE) + e + 1) * QB)
                    for h in range(2):
                        nc.scalar.activation(y_sb[:, 2 * h:2 * h + 2, e, :],
                                             ps[0:MQ, 4 + 2 * (e % 2) + h, :].rearrange("p (q d) -> p q d", q=2),
                                             ACT.Copy).then_inc(y_ev, 1)
                act.wait_ge(y_ev, (b + 1) * 2 * NE)
                act.dma_start(y_tab.rearrange("(b q p) n -> b p q n", q=QB, p=MQ)[bass.ds(b, 1)].rearrange("a p q n -> p (a q) n"),
                              y_sb.rearrange("p q e d -> p q (e d)")).then_inc(y_st, 16)

            chunks = act.value_load(row_i[0:1, 0:1], min_val=2, max_val=NCH)
            hidden(0, 0)

            def two_blocks(i):
                experts(2 * i, {2: 3 * i}, False)
                experts(2 * i + 1, {1: 3 * i + 1, 3: 3 * i + 2}, False)

            two_blocks(0)
            with act.Fori(1, AHEAD) as i:
                two_blocks(i)
            with act.Fori(2 * AHEAD, NMB - 1) as b:
                experts(b, {0: 2 * b - AHEAD, 2: 2 * b - AHEAD + 1}, False)
            experts(NMB - 1, {0: 2 * (NMB - 1) - AHEAD, 2: 2 * (NMB - 1) - AHEAD + 1}, True)
            with act.Fori(2 * NMB - AHEAD, NCH) as c:
                with act.If(chunks > c):
                    exps(c)
            act.wait_ge(row_q, 1)
            nc.scalar.activation(rowt[0:20, 5:7, :], rowt[0:20, 5:7, :], ACT.Exp).then_inc(row_ex, 1)
            def store_out(n, tiles, rows):
                act.wait_ge(fo_rdy, n + 1)
                act.dma_start(out[bass.ds(n * YT * P, tiles * rows), :].rearrange("(t p) d -> p t d", p=rows),
                              x_all[0:rows, bass.ds(n * YT, tiles), :]).then_inc(fo_out, 16)

            for n, ts in enumerate(NODE_PARTS):
                act.wait_ge(nd_q, 3 * n + 1)
                nc.scalar.activation(n_tmp[:, 4:7, ts], n_tmp[:, 4:7, ts], ACT.Exp).then_inc(nd_act, 1)
                act.wait_ge(nd_q, 3 * n + 2)
                nc.scalar.activation(n_tmp[:, 7, ts, 3], n_tmp[:, 7, ts, 1], ACT.Sqrt, bias=eps[:, :]).then_inc(nd_act, 1)
                act.wait_ge(nd_q, 3 * n + 3)
                nc.scalar.activation(n_tmp[:, 2, ts], n_tmp[:, 2, ts], ACT.Exp).then_inc(nd_act, 1)
                if n == 0:
                    for k in range(YS):
                        store_out(k, YT, P)
            with act.Fori(YS, YL * YS) as n:
                store_out(n, YT, P)
            store_out(YL * YS, 1, N - (NT - 1) * P)

        @block.tensor
        def _(pe):
            pe.wait_ge(pool_c, 6)
            pe.wait_ge(consts, 1)
            pe.wait_ge(ge_in, 48)
            pe.wait_ge(rel_rdy, 1)
            for n, rows in enumerate((g_srcf, g_dstf, g_w)):
                for j in range(ET):
                    at = ps[:, 2 * n + j // 4, (j % 4) * GG:(j % 4 + 1) * GG]
                    mm = nc.tensor.transpose(at, rows[0:GG, j * P:(j + 1) * P], ident[0:GG, 0:GG])
                mm.then_inc(ge_tp, 1)
            for i in range(2):
                mm = nc.tensor.transpose(ps[0:1, 6, i * GG:(i + 1) * GG], spread[0:GG, i:i + 1], ident[0:GG, 0:GG])
            mm.then_inc(ge_tp, 1)
            pe.wait_ge(ge_ev, 1)
            nc.tensor.matmul(ps[:, 7, 0:GG], ones[0:1, :], base_f[:, :], start=True, stop=True).then_inc(ge_tp, 1)
            pe.wait_ge(par_in, 16 * N_PAR)
            pe.wait_ge(ge_ev, 2)
            pe.wait_ge(cols_ev, 3)

            def turn_rows(g, s):
                pe.wait_ge(ln_xn, g + 1)
                after(pe, tp_ev, 2 * g)
                for t in range(GT):
                    for k in range(KD):
                        mm = nc.tensor.transpose(ps[:, 2 * k + t // 4, (t % 4) * P:(t % 4 + 1) * P],
                                                 xn_s[s][:, t, k * P:(k + 1) * P], ident[:, :])
                mm.then_inc(tp_done, 1)

            def project(g):
                pe.wait_ge(tp_ev, 2 * g + 2)
                after(pe, h_ev, g)
                for h in range(2):
                    for k in range(KD):
                        mm = nc.tensor.matmul(ps[:, 4 + h, 0:HN], wp_sb[:, k, :], xnT[:, k, h * HN:(h + 1) * HN],
                                              start=(k == 0), stop=(k == KD - 1))
                mm.then_inc(h_mm, 1)

            def turn_back(g):
                pe.wait_ge(h_ev, g + 1)
                after(pe, hb_ev, g)
                for t in range(GT):
                    mm = nc.tensor.transpose(ps[:, 6 + t // 4, (t % 4) * P:(t % 4 + 1) * P],
                                             h_now[:, t * P:(t + 1) * P], ident[:, :])
                mm.then_inc(hb_mm, 1)

            turn_rows(0, 0)
            project(0)
            turn_rows(1, 1)
            turn_back(0)
            with pe.Fori(0, NG // 2 - 1) as i:
                for s in range(2):
                    project(2 * i + 1 + s)
                    turn_rows(2 * i + 2 + s, s)
                    turn_back(2 * i + 1 + s)
            project(NG - 2)
            turn_rows(NG - 1, 0)
            turn_back(NG - 2)
            project(NG - 1)
            turn_back(NG - 1)
            pe.wait_ge(hb_ev, NG)

            def aggregate(g, s, n):
                pe.wait_ge(gath[s], 16 * ET * (n + 1))
                pe.wait_ge(oh_rdy, g + 1)
                for j in range(ET):
                    mm = nc.tensor.matmul(ps[:, s, 0:P], g_ring[:, s, j, :], oh_ring[:, s, j, :],
                                          start=(j == 0), stop=(j == ET - 1))
                mm.then_inc(mm_done, 1)

            def turn_keys(n, src):
                pe.wait_ge(key_rdy, n + 1)
                for b in range(FC // P):
                    mm = nc.tensor.transpose(ps[:, 2 + b // 4, (b % 4) * P:(b % 4 + 1) * P],
                                             src[:, b * P:(b + 1) * P], ident[:, :])
                mm.then_inc(key_tp, 1)

            def histogram(c):
                pe.wait_ge(hist_rdy, c + 1)
                for t in range(HIST_CH):
                    mm = nc.tensor.matmul(ps[:, 4, 0:64], oh_lo[:, c % 2, t, :], oh_hi[:, c % 2, t, :],
                                          start=(c == 0 and t == 0), stop=(c == FC // HIST_CH - 1 and t == HIST_CH - 1))
                mm.then_inc(hist_mm, 1)

            turns = 0
            for g, step in enumerate(STEPS):
                for kind, a, b in step:
                    if kind == "turn":
                        turn_keys(turns, keys[b])
                        turns += 1
                    elif kind == "hist":
                        histogram(a)
                    elif kind == "cum":
                        pe.wait_ge(cum_rdy, 1)
                        nc.tensor.matmul(ps[:, 4, 64:128], lower[:, :], cum[:, 0, :], start=True, stop=True)
                        nc.tensor.matmul(ps[:, 4, 128:192], ones[:, :], cum[:, 0, :], start=True, stop=True).then_inc(cum_mm, 1)
                    elif kind == "length":
                        pe.wait_ge(counted, 1)
                        nc.tensor.matmul(ps[:, 5, 0:1], ones[:, :], row_len[:, 0:1], start=True, stop=True).then_inc(len_mm, 1)
                if g >= 2:
                    pe.wait_ge(add_done, g - 1)
                aggregate(g, g % 2, g // 2)
            with pe.Fori(len(STEPS) // 2, GG // 2) as i:
                for s in range(2):
                    pe.wait_ge(add_done, 2 * i + s - 1)
                    aggregate(2 * i + s, s, i)

            with pe.If(pe.value_load(far[0:1, 0:1], min_val=0, max_val=1) > 0):
                with pe.Fori(0, GG) as g:
                    with pe.Fori(0, NT) as c:
                        pe.wait_ge(far_gath, 16 * ET * (g + 1))
                        pe.wait_ge(far_oh, g * NT + c + 1)
                        for j in range(ET):
                            mm = nc.tensor.matmul(ps[:, 0, 0:P], g_ring[:, 0, j, :], oh_ring[:, 0, j, :],
                                                  start=(j == 0), stop=(j == ET - 1))
                        mm.then_inc(far_mm, 1)

            def outputs(g, tiles):
                if tiles[0] == 0:
                    pe.wait_ge(sq_done, g + 1)
                    pe.wait_ge(h_cp, g + 1)
                    after(pe, x2_rdy, g)
                for t in tiles:
                    at = ps[:, t // 2, (t % 2) * D:(t % 2 + 1) * D]
                    nc.tensor.matmul(at, h_now2[:, t * P:(t + 1) * P], w1_sb[:, :], start=True, stop=False)
                    mm = nc.tensor.matmul(at, hp_sb[:, t, :], w2_sb[:, :], start=False, stop=True)
                if tiles[-1] == GT - 1:
                    mm.then_inc(o_mm, 1)

            def turn(g):
                pe.wait_ge(ln_xn, NG + 1 + g)
                after(pe, tab_rdy, g)
                for t in range(GT):
                    for k in range(KD):
                        mm = nc.tensor.transpose(ps[:, 4 + 2 * k + t // 4, (t % 4) * P:(t % 4 + 1) * P],
                                                 xn[:, t, k * P:(k + 1) * P], ident[:, :])
                mm.then_inc(t2_done, 1)
                pe.wait_ge(t2_ev, g + 1)
                for h in range(2):
                    for k in range(KD):
                        mm = nc.tensor.matmul(ps[0:HK, 4 + h, 0:HN], wg_sb[:, k, :],
                                              xn2T[:, k, bass.ds(g * GN + h * HN, HN)],
                                              start=(k == 0), stop=(k == KD - 1))
                mm.then_inc(g_mm, 1)

            def features(g):
                for t in range(GT):
                    mm = nc.tensor.transpose(ps[:, 7, 384 + t * HK:384 + (t + 1) * HK], featT[:, t * P:(t + 1) * P],
                                             ident[0:HK, 0:HK])
                mm.then_inc(feat_tp, 1)

            outputs(0, range(GT))
            outputs(1, range(GT))
            turn(0)
            with pe.Fori(2, NG) as g:
                outputs(g, range(3))
                pe.wait_ge(feat_ev, g - 1)
                outputs(g, range(3, 5))
                features(g - 2)
                outputs(g, range(5, GT))
                turn(g - 1)
            pe.wait_ge(feat_ev, NG - 1)
            features(NG - 2)
            turn(NG - 1)
            pe.wait_ge(feat_ev, NG)
            features(NG - 1)

            pe.wait_ge(mw_in, 32)
            pe.wait_ge(tab_rdy, NG)
            pe.wait_ge(b2_rdy, 1)

            def up(b, e, first):
                for f in range(FB):
                    if not first:
                        pe.wait_ge(gelu_done, (b * NE + e) * FB + f + 1 - FB)
                    for k in range(KD):
                        mm = nc.tensor.matmul(ps[:, f, 0:MB], w1m[:, e, k, f * P:(f + 1) * P],
                                              xn2T[:, k, bass.ds(b * MB, MB)], start=(k == 0), stop=(k == KD - 1))
                    mm.then_inc(up_mm, 1)

            def down(b, e, first):
                pe.wait_ge(gelu_done, (b * NE + e + 1) * FB)
                if not first:
                    pe.wait_ge(y_ev, (b * NE + e - 1) * 2)
                for q in range(QB):
                    at = ps[0:MQ, 4 + 2 * (e % 2) + q // 2, (q % 2) * D:(q % 2 + 1) * D]
                    for f in range(FB):
                        nc.tensor.matmul(at, hid[:, e % 2, f, q * MQ:(q + 1) * MQ], w2m[:, e, f, :],
                                         start=(f == 0), stop=False)
                    nc.tensor.matmul(at, ones_bf[:, :], b2_parts[:, e, :], start=False, stop=True).then_inc(dn_mm, 1)

            def experts(b, end):
                for e in range(NE):
                    if e < NE - 1:
                        up(b, e + 1, False)
                    elif not end:
                        up(b + 1, 0, False)
                    down(b, e, isinstance(b, int) and b == 0 and e < 2)

            up(0, 0, True)
            experts(0, False)
            with pe.Fori(1, NMB - 1) as b:
                experts(b, False)
            experts(NMB - 1, True)

            pe.wait_ge(y_ev, 2 * NMB * NE)
            pe.wait_ge(last_rdy, 1)
            for n in range(4):
                mm = nc.tensor.transpose(ps[0:20, 4, n * P:(n + 1) * P], last[:, n, :], ident[:, :])
            mm.then_inc(last_tp, 1)
            pe.wait_ge(back_rdy, 1)
            for n in range(3):
                mm = nc.tensor.transpose(ps[:, 5, n * 20:(n + 1) * 20], rowt[0:20, 9 + n, :], ident[0:20, 0:20])
            mm.then_inc(back_tp, 1)

        @block.vector
        def _(dve):
            V = nc.vector
            chain = [0]

            def step(*ops):
                for ins in ops:
                    ins.then_inc(dv, 1)
                    chain[0] += 1
                dve.wait_ge(dv, chain[0])

            class Loop:

                def __init__(self, sem_, at, i):
                    self.sem, self.at, self.i, self.n = sem_, at, i, 0

                def step(self, per, *ops):
                    for ins in ops:
                        ins.then_inc(self.sem, 1)
                        self.n += 1
                    dve.wait_ge(self.sem, self.i * per + (self.at + self.n))

            def bc(ap, shape):
                return ap.broadcast_to(shape)

            ops = [V.memset(ones[:, :], 1.0), V.memset(eps[:, :], LN_EPS), V.memset(ones_bf[:, :], 1.0), V.memset(zeros[:, :], 0.0),
                   V.memset(no_edge[:, 0:20], -BIG), V.memset(no_edge[:, 20:40], 0.0),
                   V.memset(cum[:, :, :], 0.0)]
            dve.wait_ge(pool_c, 6)
            ops += [V.tensor_copy(iota_row[:, :], iota_i), V.tensor_copy(iota_bf[:, :], iota_i)]
            step(*ops)
            for i in range(8):
                dve_op = V.tensor_scalar(sgn_i[:, i:i + 1], part_i[:, :], i, 1, ALU.logical_shift_right, ALU.bitwise_and)
                dve_op.then_inc(dv, 1)
                chain[0] += 1
            dve.wait_ge(dv, chain[0])
            step(V.tensor_copy(sgn[:, :], sgn_i[:, :]))
            step(V.tensor_scalar(sgn[:, :], sgn[:, :], -2.0, 1.0, ALU.mult, ALU.add))
            V.memset(spread[:, :], 0.0).then_inc(consts, 1)
            V.memset(zeros[:, 0:1], 0.0).then_inc(zero_rdy, 1)

            dve.wait_ge(ge_in, 48)
            step(V.tensor_copy(g_srcf[0:GG, :], g_src[0:GG, :]), V.tensor_copy(g_dstf[0:GG, :], g_dst[0:GG, :]))
            step(V.tensor_reduce(spread[0:GG, 0:1], g_dstf[0:GG, :], AX.X, ALU.min))
            step(V.tensor_scalar(g_dstf[0:GG, :], g_dstf[0:GG, :], spread[0:GG, 0:1], None, ALU.subtract))
            V.tensor_reduce(spread[0:GG, 1:2], g_dstf[0:GG, :], AX.X, ALU.max).then_inc(rel_rdy, 1)

            def group_stats(g):
                step(*[V.bn_stats(st6[:, t, :], x_all[:, g * GT + t, :]) for t in range(GT)])
                step(*[V.bn_aggr(mv_x[:, g * GT + t, :], st6[:, t, :]) for t in range(GT)])

            dve.wait_ge(x_ld[0], 16 * X_FIRST)
            for g in range(X_FIRST):
                group_stats(g)
            V.memset(scrap[:, 3:4], 0.0).then_inc(ln_mv, 1)
            dve.wait_ge(ge_tp, 4)
            step(V.tensor_copy(base_row[:, :, :], ps[0:1, 6, 0:2 * GG].rearrange("p (a g) -> p a g", a=2)),
                 V.tensor_reduce(scrap[0:1, 2:3], ps[0:1, 6, GG:2 * GG], AX.X, ALU.max),
                 V.tensor_copy(base_f[:, :], ps[0:1, 6, 0:GG]))
            V.tensor_scalar(far[:, :], scrap[0:1, 2:3], float(P) - 0.5, None, ALU.is_ge).then_inc(ge_ev, 1)
            dve.wait_ge(ge_tp, 5)
            V.tensor_copy(base_all[:, :], ps[:, 7, 0:GG]).then_inc(ge_ev, 1)
            dve.wait_ge(ge_ev, 2)
            dve.wait_ge(cols_ev, 3)

            first, rest = slice(0, X_FIRST * GT), slice(X_FIRST * GT, NT)
            dve.wait_ge(ln_sd, 1)
            step(V.reciprocal(rs_x[:, first], sd_x[:, first]))

            def normalize(g, s):
                after(dve, tp_done, g - 1)
                for t in range(GT):
                    op = V.tensor_scalar(xn_s[s][:, t, :], x_all[:, bass.ds(g * GT + t, 1), :].rearrange("p a d -> p (a d)"),
                                         mv_x[:, bass.ds(g * GT + t, 1), 0:1].rearrange("p a s -> p (a s)"),
                                         rs_x[:, bass.ds(g * GT + t, 1)], ALU.subtract, ALU.mult)
                op.then_inc(ln_xn, 1)

            def keep_rows(g):
                dve.wait_ge(tp_done, g + 1)
                after(dve, h_mm, g)
                V.tensor_copy(xnT[:, 1, :].rearrange("p (t n) -> p t n", n=P),
                              flat[:, 1024:1024 + GN].rearrange("p (t n) -> p t n", n=P)).then_inc(tp_ev, 1)

            normalize(0, 0)
            normalize(1, 1)
            keep_rows(0)
            dve.wait_ge(x_ld[1], 16 * (NG - X_FIRST))
            group_stats(3)
            normalize(2, 0)
            keep_rows(1)
            for g in range(4, NG):
                group_stats(g)
            V.memset(scrap[:, 3:4], 0.0).then_inc(ln_mv, 1)
            keep_rows(2)
            dve.wait_ge(ln_sd, 2)
            step(V.reciprocal(rs_x[:, rest], sd_x[:, rest]))
            for g in range(3, NG):
                normalize(g, g % 2)
                if g > 3:
                    keep_rows(g - 1)
            keep_rows(NG - 1)
            dve.wait_ge(clear, 2)
            dve.wait_ge(h_mm, NG)

            def one_hots(g, s):
                for j in range(ET):
                    at = [cols.rearrange("p g j -> p (g j)")[:, bass.ds(g * ET + j, 1)] for cols in (relT, wT)]
                    op = V.tensor_scalar(oh_ring[:, s, j, :], iota_row[:, :], at[0], at[1], ALU.is_equal, ALU.mult)
                op.then_inc(oh_rdy, 1)

            def add_window(g, s):
                base = dve.value_load(base_row[0:1, 0, bass.ds(g, 1)], min_val=0, max_val=NP - 1)
                dve.wait_ge(mm_done, g + 1)
                dve.wait_ge(add_done, g)
                V.tensor_tensor(aggT[:, bass.ds(base, P)], aggT[:, bass.ds(base, P)], ps[:, s, 0:P],
                                ALU.add).then_inc(add_done, 1)

            cur = [0]

            def make_keys():
                dve.wait_ge(fe_in, 32)
                k_i = [k.bitcast(I32) for k in keys]
                step(V.tensor_scalar(k_i[0], e_src, float(N - 1), None, ALU.min),
                     V.tensor_scalar(k_i[1], e_dst, DST_BITS, KEY_TOP, ALU.logical_shift_left, ALU.bitwise_or))
                step(V.tensor_tensor(k_i[0], k_i[0], k_i[1], ALU.bitwise_or))

            def row_length():
                step(V.tensor_scalar(keys[1], e_dst, float(N), None, ALU.is_lt))
                V.tensor_reduce(row_len[:, 0:1], keys[1], AX.X, ALU.add).then_inc(counted, 1)
                dve.wait_ge(len_mm, 1)
                step(V.tensor_copy(row_len[:, 1:2], ps[:, 5, 0:1]))
                step(V.tensor_scalar(cum[:, 2, 0:NCH], iota_row[:, 0:NCH], float(CH * P), row_len[:, 1:2],
                                     ALU.mult, ALU.is_lt))
                step(V.tensor_reduce(row_len[:, 1:2], cum[:, 2, 0:NCH], AX.X, ALU.add))
                step(V.tensor_scalar(row_len[:, 1:2], row_len[:, 1:2], 2.0, None, ALU.max))
                step(V.tensor_scalar(row_len[:, 2:3], row_len[:, 1:2], float(CH), None, ALU.mult))
                step(V.reciprocal(row_len[:, 3:4], row_len[:, 2:3]),
                     V.tensor_scalar(cum[:, 3, 1:2], row_len[:, 2:3], -1.0, None, ALU.add),
                     V.tensor_scalar(rows_f, iota_row[0:1, :], row_len[0:1, 2:3], None, ALU.mult),
                     V.tensor_copy(row_i[:, 0:1], row_len[:, 1:2]))
                step(V.tensor_copy(row_i[:, 1:2], cum[:, 3, 1:2]))
                V.tensor_copy(row_at, rows_f).then_inc(len_rdy, 1)
                dve.wait_ge(len_rdy, 1)

            def swap_stage(k, j):
                a, b = cur[0], 1 - cur[0]
                d = 1 << j
                if j == k - 1 and k > FLOG - 1 and k - FLOG < 8:
                    i = k - FLOG
                    if i >= 1:
                        step(V.tensor_scalar(keys[a], keys[a], sgn[:, i - 1:i], None, ALU.mult))
                    if k < ELOG:
                        step(V.tensor_scalar(keys[a], keys[a], sgn[:, i:i + 1], None, ALU.mult))
                if j >= FLOG:
                    if j == k - 1:
                        src = turned(a)
                    else:
                        src = keys[a]
                    m = P // (2 * (d >> FLOG))
                    v = src.rearrange("p (c m s i) -> p s c m i", c=FC // P, m=m, s=2)
                    w = keys[b].rearrange("p (c m s i) -> p s c m i", c=FC // P, m=m, s=2)
                    step(V.tensor_tensor(w[:, 0], v[:, 0], v[:, 1], ALU.min),
                         V.tensor_tensor(w[:, 1], v[:, 0], v[:, 1], ALU.max))
                else:
                    src = turned(a) if (j == FLOG - 1 and k > FLOG) else keys[a]
                    if k < FLOG:
                        r, m = FC >> (k + 1), 1 << (k - 1 - j)
                        v = src.rearrange("p (r z m s i) -> p z s r m i", r=r, z=2, m=m, s=2)
                        w = keys[b].rearrange("p (r z m s i) -> p z s r m i", r=r, z=2, m=m, s=2)
                        step(*[V.tensor_tensor(w[:, z, s], v[:, z, 0], v[:, z, 1], (ALU.min, ALU.max)[z ^ s])
                               for z in range(2) for s in range(2)])
                    else:
                        m = FC // (2 * d)
                        v = src.rearrange("p (m s i) -> p s m i", m=m, s=2)
                        w = keys[b].rearrange("p (m s i) -> p s m i", m=m, s=2)
                        step(V.tensor_tensor(w[:, 0], v[:, 0], v[:, 1], ALU.min),
                             V.tensor_tensor(w[:, 1], v[:, 0], v[:, 1], ALU.max))
                cur[0] = b
                if (k, j) == STAGES[-1]:
                    V.memset(scrap[:, 3:4], 0.0).then_inc(key_end, 1)

            n_turn = [0]

            def turned(a):
                V.tensor_copy(spread[0:1, 3:4], zeros[0:1, 1:2]).then_inc(key_rdy, 1)
                n_turn[0] += 1
                dve.wait_ge(key_tp, n_turn[0])
                step(V.tensor_copy(keys[a], flat[:, 2 * 512:2 * 512 + FC]))
                return keys[a]

            def halves():
                step(V.tensor_scalar(half_i, e_dst, P - 1, None, ALU.bitwise_and))
                step(V.tensor_copy(lo_bf, half_i))
                step(V.tensor_scalar(half_i, e_dst, 7, None, ALU.logical_shift_right))
                step(V.tensor_copy(hi_bf, half_i))

            def histogram(c):
                if c >= 2:
                    dve.wait_ge(hist_mm, c - 1)
                cols = slice(c * HIST_CH, (c + 1) * HIST_CH)
                V.tensor_tensor(oh_lo[:, c % 2], bc(iota_bf[:, :].unsqueeze(1), [P, HIST_CH, P]),
                                bc(lo_bf[:, cols].unsqueeze(2), [P, HIST_CH, P]), ALU.is_equal).then_inc(dv, 1)
                chain[0] += 1
                V.tensor_tensor(oh_hi[:, c % 2], bc(iota_bf[:, 0:64].unsqueeze(1), [P, HIST_CH, 64]),
                                bc(hi_bf[:, cols].unsqueeze(2), [P, HIST_CH, 64]), ALU.is_equal).then_inc(hist_rdy, 1)

            def into_rows(at):
                q, rest, off = cum[:, 2, :], cum[:, 3, :], cum[:, 5, :]
                step(V.tensor_scalar(q, at, row_len[:, 3:4], None, ALU.mult))
                step(V.tensor_copy(half_i[:, 0:64], q))
                step(V.tensor_copy(q, half_i[:, 0:64]))
                step(V.tensor_scalar(rest, q, row_len[:, 2:3], None, ALU.mult))
                step(V.tensor_tensor(rest, at, rest, ALU.subtract))
                step(V.tensor_scalar(off, rest, row_len[:, 2:3], None, ALU.is_ge),
                     V.tensor_scalar(rest, rest, 0.0, None, ALU.is_lt))
                step(V.tensor_tensor(q, q, off, ALU.add))
                step(V.tensor_tensor(q, q, rest, ALU.subtract))
                step(V.tensor_scalar(rest, q, row_len[:, 2:3], None, ALU.mult))
                step(V.tensor_tensor(at, at, rest, ALU.subtract), V.tensor_scalar(q, q, float(FC), None, ALU.mult))
                step(V.tensor_tensor(at, at, q, ALU.add))

            def positions():
                dve.wait_ge(hist_mm, FC // HIST_CH)
                V.tensor_copy(cum[:, 0, :], ps[:, 4, 0:64]).then_inc(cum_rdy, 1)
                dve.wait_ge(cum_rdy, 1)
                dve.wait_ge(cum_mm, 1)
                step(V.tensor_copy(cum[:, 2, :], ps[:, 4, 128:192]))
                step(V.tensor_tensor_scan(cum[:, 1, :], ones[:, 0:64], cum[:, 2, :], 0.0, ALU.mult, ALU.add))
                step(V.tensor_tensor(cum[:, 1, :], cum[:, 1, :], cum[:, 2, :], ALU.subtract))
                step(V.tensor_tensor(cum[:, 1, :], cum[:, 1, :], ps[:, 4, 64:128], ALU.add),
                     V.tensor_scalar(has[:, :], cum[:, 0, 0:NT], 0.0, None, ALU.is_gt))
                step(V.tensor_tensor(cum[:, 4, :], cum[:, 1, :], cum[:, 0, :], ALU.add))
                step(V.tensor_scalar(cum[:, 4, :], cum[:, 4, :], -1.0, 0.0, ALU.add, ALU.max))
                into_rows(cum[:, 4, :])
                into_rows(cum[:, 1, :])
                step(V.tensor_copy(e_idx[:, :], cum[:, 4, 0:NT]))
                step(V.tensor_copy(cum[:, 4, 0:1], part_i[:, :]))
                step(V.tensor_scalar(cum[:, 3, :], iota_row[:, 0:64], float(P), float(EF), ALU.mult, ALU.add))
                step(V.tensor_scalar(cum[:, 3, :], cum[:, 3, :], cum[:, 4, 0:1], None, ALU.add))
                step(V.tensor_tensor(cum[:, 1, :], cum[:, 1, :], cum[:, 3, :], ALU.subtract))
                step(V.tensor_tensor(cum[:, 1, 0:NT], cum[:, 1, 0:NT], has[:, :], ALU.mult))
                step(V.tensor_tensor(cum[:, 1, :], cum[:, 1, :], cum[:, 3, :], ALU.add))
                step(V.tensor_copy(st_idx[:, :], cum[:, 1, 0:NT]))

            def marks():
                dve.wait_ge(fetched, 16)
                k_i = keys[1 - cur[0]].bitcast(I32)
                t_i = keys[cur[0]].bitcast(I32)
                row_end = dve.value_load(row_i[0:1, 1:2], min_val=2 * CH - 1, max_val=FC - 1)
                step(V.tensor_scalar(s_src[:, :], k_i, (1 << DST_BITS) - 1, None, ALU.bitwise_and),
                     V.tensor_scalar(t_i, k_i, DST_BITS, (1 << DST_BITS) - 1, ALU.logical_shift_right, ALU.bitwise_and))
                step(V.tensor_copy(s_dst, t_i))
                step(V.tensor_copy(ends[:, 0:1], s_dst[:, 0:1]))
                V.tensor_copy(ends[:, 1:2], s_dst[:, bass.ds(row_end, 1)]).then_inc(ends_rdy, 1)
                dve.wait_ge(ends_rdy, 1)
                step(V.tensor_copy(first_idx[:, :], ends[:, 0:1]), V.memset(was_equal[:, 0:1], 0.0),
                     V.tensor_tensor(was_equal[:, 1:FC], s_dst[:, 1:FC], s_dst[:, 0:FC - 1], ALU.is_equal))
                V.tensor_scalar(pen[:, :], was_equal, -1.0, BIG, ALU.add, ALU.mult).then_inc(sorted_s, 1)

            def add_bias(g):
                if g == 0:
                    dve.wait_ge(bias_in, 32)
                    step(V.tensor_tensor(b12[:, 0, :], b12[:, 0, :], b12[:, 1, :], ALU.add))
                group = x_all[:, g * GT:(g + 1) * GT, :]
                step(V.tensor_tensor(group, group, bc(b12[:, 0:1, :], [P, GT, D]), ALU.add))

            def do(kind, a, b):
                if kind == "keys":
                    make_keys()
                    halves()
                elif kind == "length":
                    row_length()
                elif kind == "bias":
                    add_bias(a)
                elif kind == "stage":
                    swap_stage(a, b)
                elif kind == "hist":
                    histogram(a)
                elif kind == "cum":
                    positions()
                elif kind == "marks":
                    marks()

            for g, todo in enumerate(STEPS):
                one_hots(g, g % 2)
                for kind, a, b in todo:
                    do(kind, a, b)
                if g >= 1:
                    add_window(g - 1, (g - 1) % 2)
            add_window(len(STEPS) - 1, 1)
            done = len(STEPS)
            with dve.Fori(done // 2, GG // 2) as i:
                for s in range(2):
                    one_hots(2 * i + s, s)
                    add_window(2 * i + s, s)

            dve.wait_ge(add_done, GG)
            with dve.If(dve.value_load(far[0:1, 0:1], min_val=0, max_val=1) > 0):
                with dve.Fori(0, GG) as g:
                    rel = relT[:, bass.ds(g, 1), :].rearrange("p a j -> p (a j)")
                    w = wT[:, bass.ds(g, 1), :].rearrange("p a j -> p (a j)")
                    V.scalar_tensor_tensor(out=far_cols[:, 0, :], in0=rel, scalar=float(P) - 0.5, in1=w,
                                           op0=ALU.is_ge, op1=ALU.mult)
                    V.tensor_scalar(far_cols[:, 1, :], rel, base_all[:, bass.ds(g, 1)], None, ALU.add).then_inc(far_add, 1)
                    with dve.Fori(0, NT) as c:
                        at = g * (NT * 3 + 1) + c * 3
                        dve.wait_ge(far_add, at + 1)
                        V.tensor_tensor(oh_ring[:, 0], bc(iota_row[:, :].unsqueeze(1), [P, ET, P]),
                                        bc(far_cols[:, 1, :].unsqueeze(2), [P, ET, P]), ALU.is_equal).then_inc(far_add, 1)
                        dve.wait_ge(far_add, at + 2)
                        V.tensor_tensor(oh_ring[:, 0], oh_ring[:, 0], bc(far_cols[:, 0, :].unsqueeze(2), [P, ET, P]),
                                        ALU.mult).then_inc(far_oh, 1)
                        V.tensor_scalar(far_cols[:, 1, :], far_cols[:, 1, :], -float(P), None, ALU.add).then_inc(far_add, 1)
                        dve.wait_ge(far_mm, g * NT + c + 1)
                        block_c = aggT[:, bass.ds(c * P, P)]
                        V.tensor_tensor(block_c, block_c, ps[:, 0, 0:P], ALU.add).then_inc(far_add, 1)
                    dve.wait_ge(far_add, (g + 1) * (NT * 3 + 1))
                    apart(dve)
            V.memset(scrap[:, 3:4], 0.0).then_inc(agg_done, 1)

            def add_outputs(g, loop):
                dve.wait_ge(o_mm, g + 1)
                dve.wait_ge(ln_xn, NG + g)
                group = x_all[:, bass.ds(g * GT, GT), :].rearrange("p t d -> p (t d)")
                V.tensor_tensor(group, group, flat[:, 0:GT * D], ALU.add).then_inc(x2_rdy, 1)
                dve.wait_ge(x2_rdy, g + 1)
                apart(dve)
                loop.step(per, *[V.bn_stats(st6[:, t, :], x_all[:, bass.ds(g * GT + t, 1), :].rearrange("p a d -> p (a d)"))
                                 for t in range(GT)])
                apart(dve)
                for t in range(GT):
                    op = V.bn_aggr(mv[:, t, :], st6[:, t, :])
                op.then_inc(ln_mv, 1)

            def scales(g, loop):
                dve.wait_ge(ln_sd, 3 + g)
                loop.step(per, V.reciprocal(rs[:, :], sd[:, :]))
                V.scalar_tensor_tensor(out=nm[:, :], in0=mv[:, :, 0], scalar=-1.0, in1=rs[:, :],
                                       op0=ALU.mult, op1=ALU.mult).then_inc(ln_rs, 1)

            def keep_features(g):
                dve.wait_ge(g_mm, g + 1)
                V.tensor_copy(featT.rearrange("p (b n) -> p b n", b=2), ps[0:HK, 4:6, 0:HN]).then_inc(feat_ev, 1)

            def logits(g, loop):
                dve.wait_ge(feat_tp, g + 1)
                h = ps[:, 7, 384:384 + GT * HK].rearrange("p (t c) -> p t c", c=HK)
                V.tensor_copy(tab[:, bass.ds(g * GT, GT), 4:RW].rearrange("p t (h k) -> p t h k", k=5)[:, :, :, 0:NE],
                              h.rearrange("p t (h k) -> p t h k", k=NE))
                loop.step(per, V.tensor_tensor(att_tmp[:, :, :], h, bc(att[:, 0:1, :], [P, GT, HK]), ALU.mult))
                loop.step(per, V.tensor_reduce(tab[:, bass.ds(g * GT, GT), 0:HEADS],
                                               att_tmp[:, :, :].rearrange("p t (h k) -> p t h k", k=NE), AX.X, ALU.add))
                loop.step(per, V.tensor_tensor(att_tmp[:, :, :], h, bc(att[:, 1:2, :], [P, GT, HK]), ALU.mult))
                V.tensor_reduce(adst[:, bass.ds(g * GT, GT), :],
                                att_tmp[:, :, :].rearrange("p t (h k) -> p t h k", k=NE), AX.X, ALU.add).then_inc(tab_rdy, 1)

            loop = Loop(dv, chain[0], 0)
            per = 0
            for g in range(2):
                add_outputs(g, loop)
                scales(g, loop)
            keep_features(0)
            chain[0] += loop.n
            per = GT + 4
            with dve.Fori(2, NG) as g:
                loop = Loop(dv, chain[0] - 2 * per, g)
                logits(g - 2, loop)
                add_outputs(g, loop)
                scales(g, loop)
                keep_features(g - 1)
                assert loop.n == per, loop.n
            chain[0] += (NG - 2) * per
            loop = Loop(dv, chain[0], 0)
            logits(NG - 2, loop)
            keep_features(NG - 1)
            logits(NG - 1, loop)
            chain[0] += loop.n
            dve.wait_ge(tab_rdy, NG)

            dve.wait_ge(x2_out, 16 * NG)
            step(V.tensor_copy(b2_part, b2m[:, :, :]))
            step(V.tensor_scalar(b2_parts, b2_part, ident[0:3, 0:1], None, ALU.mult),
                 V.tensor_tensor(b2_rest, b2m[:, :, :], b2_part, ALU.subtract))
            step(V.tensor_copy(b2_part, b2_rest))
            step(V.scalar_tensor_tensor(out=b2_parts, in0=b2_part, scalar=ident[0:3, 1:2], in1=b2_parts,
                                        op0=ALU.mult, op1=ALU.add),
                 V.tensor_tensor(b2_rest, b2_rest, b2_part, ALU.subtract))
            step(V.tensor_copy(b2_part, b2_rest))
            V.scalar_tensor_tensor(out=b2_parts, in0=b2_part, scalar=ident[0:3, 2:3], in1=b2_parts,
                                   op0=ALU.mult, op1=ALU.add).then_inc(b2_rdy, 1)
            dve.wait_ge(b2_rdy, 1)

            dve.wait_ge(af_in, 16)
            dve.wait_ge(a_in, 16)
            step(V.tensor_copy(a_edge[:, 0, :], a_first[:, :]))
            step(V.tensor_scalar(not_start, pen[:, :], 0.0, None, ALU.is_equal))
            step(*[V.tensor_tensor_scan(a_edge[:, :, h], not_start, a_edge[:, :, h], 0.0, ALU.mult, ALU.add)
                   for h in range(HEADS)])
            step(V.memset(run[:, :], 0.0))

            def scan_chunk(c, s, i, steps):
                cols = bass.ds(c * CH, CH)
                dve.wait_ge(fgath[s], 16 * CH * (i + 1))
                steps(V.tensor_tensor(z1, rec_in[:, s, :, 0:HEADS], a_edge[:, cols, :], ALU.add))
                steps(V.scalar_tensor_tensor(out=z2, in0=z1, scalar=0.2, in1=z1, op0=ALU.mult, op1=ALU.max))
                dve.wait_ge(rec_st[s], 16 * (i + 1))
                steps(*[V.tensor_tensor_scan(rec_out[:, s, :, h], pen[:, cols], z2[:, :, h], run[:, h:h + 1],
                                             ALU.add, ALU.max) for h in range(HEADS)])
                m = rec_out[:, s, :, 0:HEADS]
                steps(V.tensor_tensor(dq[:, 0, 1:CH, :], m[:, 0:CH - 1, :], m[:, 1:CH, :], ALU.subtract),
                      V.tensor_tensor(dq[:, 0, 0, :], run[:, 0:HEADS], m[:, 0, :], ALU.subtract),
                      V.tensor_tensor(dq[:, 1], z2, m, ALU.subtract))
                V.tensor_tensor(dq[:, 0], dq[:, 0], bc(pen[:, cols].unsqueeze(2), [P, CH, HEADS]), ALU.add).then_inc(q_rdy, 1)
                dve.wait_ge(ex_done, c + 1)
                V.tensor_tensor(vals, rec_in[:, s, :, HEADS:RW].rearrange("p t (h k) -> p t h k", k=5),
                                bc(dq[:, 1].unsqueeze(3), [P, CH, HEADS, 5]), ALU.mult).then_inc(in_free, 1)
                dve.wait_ge(in_free, c + 1)
                for h in range(HEADS):
                    for k in range(5):
                        n = HEADS + h * 5 + k
                        op = V.tensor_tensor_scan(rec_out[:, s, :, n], dq[:, 0, :, h], vals[:, :, h, k],
                                                  run[:, n:n + 1], ALU.mult, ALU.add)
                op.then_inc(sc_done, 1)
                dve.wait_ge(sc_done, c + 1)
                steps(V.tensor_copy(run[:, :], rec_out[:, s, CH - 1, :]))

            per = 10
            chunks = dve.value_load(row_i[0:1, 0:1], min_val=2, max_val=NCH)
            with dve.Fori(0, NCH // 2) as i:
                for s in range(2):
                    with dve.If(chunks > 2 * i + s):
                        loop = Loop(chunk_dv, 0, 2 * i + s)
                        scan_chunk(2 * i + s, s, i, lambda *ops: loop.step(per, *ops))
                        apart(dve)
                        assert loop.n == per, loop.n
                    with dve.If(chunks <= 2 * i + s):
                        V.tensor_copy(z1[:, bass.ds(2 * i + s, 1), 0], zeros[:, 0:1]).then_inc(rec_st[s], 16)

            V.tensor_copy(last[:, 0, :].rearrange("p (h k) -> p h k", k=5), bc(run[:, 0:HEADS].unsqueeze(2), [P, HEADS, 5]))
            V.tensor_copy(last[:, 1, :], run[:, HEADS:RW])
            V.tensor_copy(last[:, 2, :], bc(ends[:, 0:1], [P, 20]))
            V.tensor_copy(last[:, 3, :], bc(ends[:, 1:2], [P, 20])).then_inc(last_rdy, 1)
            dve.wait_ge(last_tp, 1)
            step(V.tensor_copy(rowt[0:20, 0:4, :], ps[0:20, 4, :].rearrange("p (s c) -> p s c", c=P)))
            R = rowt[0:20]
            step(V.memset(R[:, 4, 0:1], 0.0),
                 V.tensor_tensor(R[:, 4, 1:P], R[:, 3, 0:P - 1], R[:, 2, 1:P], ALU.is_equal),
                 V.tensor_tensor(R[:, 7, :], R[:, 2, :], R[:, 3, :], ALU.is_equal))
            step(V.tensor_tensor(R[:, 7, :], R[:, 7, :], R[:, 4, :], ALU.mult))
            step(V.tensor_scalar(R[:, 8, :], R[:, 7, :], -1.0, BIG, ALU.add, ALU.mult))
            step(V.tensor_tensor_scan(R[:, 9, :], R[:, 8, :], R[:, 0, :], 0.0, ALU.add, ALU.max))
            step(V.memset(R[:, 5, 0:1], -BIG),
                 V.tensor_tensor(R[:, 5, 1:P], R[:, 9, 0:P - 1], R[:, 9, 1:P], ALU.subtract),
                 V.tensor_tensor(R[:, 6, :], R[:, 0, :], R[:, 9, :], ALU.subtract))
            V.tensor_tensor(R[:, 5, :], R[:, 5, :], R[:, 8, :], ALU.add).then_inc(row_q, 1)
            dve.wait_ge(row_ex, 1)
            step(V.tensor_tensor(R[:, 6, :], R[:, 6, :], R[:, 1, :], ALU.mult))
            step(V.tensor_tensor_scan(R[:, 1, :], R[:, 5, :], R[:, 6, :], 0.0, ALU.mult, ALU.add))
            step(V.memset(R[:, 0, 0:1], -BIG), V.memset(R[:, 10, 0:1], 0.0),
                 V.tensor_tensor(R[:, 0, 1:P], R[:, 9, 0:P - 1], R[:, 4, 1:P], ALU.mult),
                 V.tensor_tensor(R[:, 10, 1:P], R[:, 1, 0:P - 1], R[:, 4, 1:P], ALU.mult),
                 V.tensor_scalar(R[:, 8, :], R[:, 4, :], -1.0, BIG, ALU.add, ALU.mult))
            step(V.tensor_tensor(R[:, 9, :], R[:, 0, :], R[:, 8, :], ALU.add))
            step(V.memset(R[:, 5, :], 0.0), V.memset(R[:, 11, :], 0.0))
            step(V.tensor_scalar(R[:, 6, :], iota_row[0:20, :], float(TRASH), None, ALU.add))
            step(V.tensor_tensor(R[:, 5, 0:P - 1], R[:, 3, 0:P - 1], R[:, 2, 1:P], ALU.is_equal),
                 V.tensor_tensor(R[:, 11, :], R[:, 2, :], R[:, 3, :], ALU.is_equal))
            step(V.tensor_tensor(R[:, 5, :], R[:, 5, :], R[:, 11, :], ALU.mult))
            step(V.tensor_scalar(R[:, 5, :], R[:, 5, :], -1.0, 1.0, ALU.mult, ALU.add))
            step(V.tensor_tensor(R[:, 5, :], R[:, 5, :], R[:, 4, :], ALU.mult))
            step(V.tensor_tensor(R[:, 2, :], R[:, 2, :], R[:, 6, :], ALU.subtract))
            step(V.tensor_tensor(R[:, 2, :], R[:, 2, :], R[:, 5, :], ALU.mult))
            V.tensor_tensor(R[:, 11, :], R[:, 2, :], R[:, 6, :], ALU.add).then_inc(back_rdy, 1)
            dve.wait_ge(back_tp, 1)
            step(V.tensor_copy(carried, ps[:, 5, 0:60]))
            V.tensor_copy(carry_idx[:, :], carried[:, 40:41]).then_inc(c_rdy, 1)

            dve.wait_ge(c_in, 16)

            def node_gates(part):
                ts = NODE_PARTS[part]
                NN = ts.stop - ts.start
                dve.wait_ge(r_in[part], 16 * NN)

                def nt(i):
                    return n_tmp[:, i, ts]

                m_r, m_c, m_s = nt(0), nt(1), nt(2)
                hasb = bc(has[:, ts].unsqueeze(2), [P, NN, HEADS])
                cm = node_c[:, ts, 0:20].rearrange("p t (h k) -> p t h k", k=5)[:, :, :, 0]
                step(V.tensor_tensor(m_r, node_r[:, ts, 0:HEADS], hasb, ALU.mult),
                     V.tensor_scalar(nt(3), hasb, -1.0, BIG, ALU.add, ALU.mult),
                     V.tensor_tensor(m_s, tab[:, ts, 0:HEADS], adst[:, ts, :], ALU.add),
                     V.tensor_copy(m_c, cm))
                step(V.tensor_tensor(m_r, m_r, nt(3), ALU.add),
                     V.scalar_tensor_tensor(out=nt(7), in0=m_s, scalar=0.2, in1=m_s, op0=ALU.mult, op1=ALU.max))
                step(V.tensor_tensor(nt(3), m_r, m_c, ALU.max))
                step(V.tensor_tensor(nt(3), nt(3), nt(7), ALU.max))
                step(V.tensor_tensor(nt(4), m_r, nt(3), ALU.subtract),
                     V.tensor_tensor(nt(5), m_c, nt(3), ALU.subtract))
                V.tensor_tensor(nt(6), nt(7), nt(3), ALU.subtract).then_inc(nd_q, 1)
                dve.wait_ge(nd_act, 3 * part + 1)

                def b5(ap):
                    return bc(ap.unsqueeze(3), [P, NN, HEADS, 5])

                def hk(ap):
                    return ap.rearrange("p t (h k) -> p t h k", k=5)

                r5, c5, t5 = hk(node_r[:, ts, HEADS:RW]), hk(node_c[:, ts, 20:40]), hk(tab[:, ts, HEADS:RW])
                step(V.tensor_tensor(r5, r5, b5(nt(4)), ALU.mult), V.tensor_tensor(c5, c5, b5(nt(5)), ALU.mult),
                     V.tensor_tensor(s_tmp[:, ts], t5, b5(nt(6)), ALU.mult))
                step(V.tensor_tensor(r5, r5, c5, ALU.add))
                step(V.tensor_tensor(s_tmp[:, ts], s_tmp[:, ts], r5, ALU.add))
                step(V.tensor_scalar(nt(0), s_tmp[:, ts, :, 4], 1e-16, None, ALU.add))
                step(V.reciprocal(nt(1), nt(0)))
                agg, dev = n16[:, 0, ts], n16[:, 1, ts]
                agg4 = agg.rearrange("p t (h k) -> p t h k", k=NE)
                step(V.tensor_tensor(agg4, s_tmp[:, ts, :, 0:NE], bc(nt(1).unsqueeze(3), [P, NN, HEADS, NE]), ALU.mult))
                step(V.tensor_tensor(agg, agg, bc(gat_par[:, 0:1, :], [P, NN, HK]), ALU.add))
                mean, var, sd2, rs2 = (nt(7)[:, :, i] for i in (0, 1, 3, 2))
                step(V.tensor_reduce(mean, agg, AX.X, ALU.add))
                step(V.tensor_scalar(mean, mean, 1.0 / HK, None, ALU.mult))
                step(V.tensor_tensor(agg, agg, bc(mean.unsqueeze(2), [P, NN, HK]), ALU.subtract))
                step(V.tensor_tensor(dev, agg, agg, ALU.mult))
                step(V.tensor_reduce(var, dev, AX.X, ALU.add))
                V.tensor_scalar(var, var, 1.0 / HK, None, ALU.mult).then_inc(nd_q, 1)
                dve.wait_ge(nd_act, 3 * part + 2)
                step(V.reciprocal(rs2, sd2))
                step(V.tensor_tensor(agg, agg, bc(rs2.unsqueeze(2), [P, NN, HK]), ALU.mult))
                step(V.tensor_tensor(agg, agg, bc(gat_par[:, 1:2, :], [P, NN, HK]), ALU.mult))
                step(V.tensor_tensor(agg, agg, bc(gat_par[:, 2:3, :], [P, NN, HK]), ALU.add))
                score, rank, top = nt(0), nt(1), nt(7)[:, :, 0]
                step(V.tensor_reduce(score, agg.rearrange("p t (h k) -> p t k h", k=NE), AX.X, ALU.add))
                step(V.tensor_scalar(score, score, 1.0 / HEADS, None, ALU.mult), V.memset(rank, 0.0))
                beats = nt(3)[:, :, 0]
                for j in range(NE):
                    for i in range(j + 1, NE):
                        step(V.tensor_tensor(beats, score[:, :, j], score[:, :, i], ALU.is_ge))
                        step(V.tensor_tensor(rank[:, :, i], rank[:, :, i], beats, ALU.add),
                             V.scalar_tensor_tensor(out=rank[:, :, j], in0=rank[:, :, j], scalar=1.0, in1=beats,
                                                    op0=ALU.add, op1=ALU.subtract))
                step(V.tensor_reduce(top, score, AX.X, ALU.max))
                V.tensor_tensor(nt(2), score, bc(top.unsqueeze(2), [P, NN, NE]), ALU.subtract).then_inc(nd_q, 1)
                dve.wait_ge(nd_act, 3 * part + 3)
                step(V.tensor_scalar(rank, rank, 1.5, None, ALU.is_lt))
                step(V.tensor_tensor(nt(2), nt(2), rank, ALU.mult))
                step(V.tensor_reduce(top, nt(2), AX.X, ALU.add))
                step(V.reciprocal(nt(7)[:, :, 2], top))
                step(V.tensor_tensor(gates[:, ts, :], nt(2), bc(nt(7)[:, :, 2].unsqueeze(2), [P, NN, NE]), ALU.mult))

            def combine(t, n, s, i, steps):
                dve.wait_ge(fy_in[s], 16 * (i + 1))
                for e in range(NE):
                    ops = []
                    for k in range(n):
                        acc = x_all[:, bass.ds(t + k, 1), :].rearrange("p a d -> p (a d)")
                        gate = gates[:, bass.ds(t + k, 1), e:e + 1].rearrange("p a e -> p (a e)")
                        ops.append(V.scalar_tensor_tensor(out=acc, in0=y_in[s][:, k, e, :], scalar=gate, in1=acc,
                                                          op0=ALU.mult, op1=ALU.add))
                    if e < NE - 1:
                        steps(*ops)
                ops[-1].then_inc(fo_rdy, 1)

            dve.wait_ge(fx_in, 16)
            per = YS * (NE - 1) * YT
            node_gates(0)
            for s in range(YS):
                combine(s * YT, YT, s, 0, step)
            node_gates(1)
            with dve.Fori(1, YL) as i:
                loop = Loop(dv, chain[0] - per, i)
                for s in range(YS):
                    combine((YS * i + s) * YT, YT, s, i, lambda *ops: loop.step(per, *ops))
                assert loop.n == per
            chain[0] += (YL - 1) * per
            combine(YL * YS * YT, 1, 0, YL, step)


def plan_steps():
    work = [("keys", 0, 0), ("length", 0, 0)]
    cur = 0
    for k, j in STAGES:
        if (j >= FLOG and j == k - 1) or (j == FLOG - 1 and k > FLOG):
            work.append(("turn", 0, cur))
        work.append(("stage", k, j))
        cur = 1 - cur
    work += [("hist", c, 0) for c in range(FC // HIST_CH)]
    work += [("bias", g, 0) for g in range(NG)]
    work += [("cum", 0, 0), ("marks", 0, 0)]
    steps, room = [[]], BUDGET
    for kind, a, b in work:
        took = {"keys": 8.0, "length": 4.0, "bias": 2.5, "turn": 4.0, "stage": 1.4, "hist": 3.4, "cum": 5.0, "marks": 8.0}[kind]
        if took > room and steps[-1]:
            steps.append([])
            room = BUDGET
        steps[-1].append((kind, a, b))
        room -= took
    if len(steps) % 2:
        steps.append([])
    assert len(steps) < GG
    return steps


STEPS = plan_steps()


DEBUG = ()


def kernel(x, src, dst, edge_weight, L0_gnn_Wp, L0_gnn_bp, L0_gnn_W1, L0_gnn_b1, L0_gnn_W2, L0_gnn_b2, L0_ffn_W_gat,
           L0_ffn_att_src, L0_ffn_att_dst, L0_ffn_b_gat, L0_ffn_ln_gamma, L0_ffn_ln_beta, L0_ffn_W1, L0_ffn_b1,
           L0_ffn_W2, L0_ffn_b2, L0_ffn_edge_index):
    import numpy as np
    import concourse.bacc as bacc
    from concourse.bass_utils import run_bass_kernel_spmd as run

    nc = bacc.Bacc("TRN2", target_bir_lowering=False, num_devices=1)
    tail = GG * EGN - EG
    pad_e = lambda a: np.pad(np.asarray(a), (0, tail), mode="edge").reshape(GG, EGN)
    edges = np.asarray(L0_ffn_edge_index)
    arrays = {
        "x": np.pad(np.asarray(x), ((0, NP - N), (0, 0))),
        "gsrc": pad_e(src), "gdst": pad_e(dst),
        "gw": np.pad(np.asarray(edge_weight), (0, tail)).reshape(GG, EGN),
        "WpT": np.asarray(L0_gnn_Wp).T, "bp": L0_gnn_bp, "W1T": np.asarray(L0_gnn_W1).T, "b1": L0_gnn_b1,
        "W2T": np.asarray(L0_gnn_W2).T, "b2": L0_gnn_b2, "Wgat": L0_ffn_W_gat, "att_src": L0_ffn_att_src,
        "att_dst": L0_ffn_att_dst, "b_gat": L0_ffn_b_gat, "ln_gamma": L0_ffn_ln_gamma, "ln_beta": L0_ffn_ln_beta,
        "mW1": L0_ffn_W1, "mb1": np.asarray(L0_ffn_b1).reshape(NE * FB, P).T, "mW2": L0_ffn_W2,
        "mb2": np.asarray(L0_ffn_b2).reshape(NE * D),
        "fsrc": edges[0].reshape(P, FC), "fdst": edges[1].reshape(P, FC),
    }
    arrays = {k: np.ascontiguousarray(v) for k, v in arrays.items()}
    args = [nc.dram_tensor(k, v.shape, mybir.dt.from_np(v.dtype), kind="ExternalInput").ap() for k, v in arrays.items()]
    out = nc.dram_tensor("out", (N, D), F32, kind="ExternalOutput").ap()
    gnn_ffn(nc, *args, out, DEBUG)
    r = run(nc, [arrays], core_ids=[0])
    return r.results[0]["out"]
```
